# Optimizing a Trainium2 kernel written in Bass

```python
import numpy as np
import jax
import jax.numpy as jnp

def _softmax(x, axis=-1):
    return jax.nn.softmax(x, axis=axis)

def _gelu(x):
    return jax.nn.gelu(x, approximate=True)

def _silu(x):
    return jax.nn.silu(x)

def _sigmoid(x):
    return jax.nn.sigmoid(x)

def _layernorm(x, axis=-1, eps=1e-05):
    m = jnp.mean(x, axis=axis, keepdims=True)
    v = jnp.var(x, axis=axis, keepdims=True)
    return (x - m) / jnp.sqrt(v + eps)

def _scatter_add(tgt, idx, src, axis=0):
    return tgt.at[idx].add(src)

def _segment_sum(src, seg, n):
    return jax.ops.segment_sum(src, seg, n)
kernel_name = 'mk_metaformer_d2_conv_nchw1024_r4_6d2b71'

def setup_inputs(seed: int=0):
    np.random.seed(seed)
    _w = jnp.asarray

    def _rec_inputs():
        import jax
        import jax.numpy as jnp
        _gk = jax.random.key(seed)
        x = -7.109e-05 + 0.9999 * jax.random.normal(jax.random.fold_in(_gk, 1), (16, 256, 16, 16), jnp.float32)
        return x
    x = _rec_inputs()

    def _L0_conv_setup():
        import jax, jax.numpy as jnp
        import numpy as np
        GROUPS = 32
        EPS = 1e-05
        key = jax.random.key(seed)
        k1, k2, k3 = jax.random.split(key, 3)
        b, c, h, w = (16, 256, 16, 16)
        cg = c // GROUPS
        return {'x': jax.random.normal(k1, (b, c, h, w), dtype=jnp.float32), 'conv_w': jax.random.normal(k2, (cg, cg), dtype=jnp.float32) * (1.0 / np.sqrt(cg)), 'conv_b': jax.random.normal(k3, (cg,), dtype=jnp.float32) * 0.01, 'gn_w': jnp.ones((cg,), dtype=jnp.float32), 'gn_b': jnp.zeros((cg,), dtype=jnp.float32)}
    _L0_conv_all = _L0_conv_setup()
    _L0_conv_in = {k: v for k, v in _L0_conv_all.items() if k in ('conv_w', 'conv_b', 'gn_w', 'gn_b')}
    del _L0_conv_all

    def _L0_ffn_setup():
        import jax, jax.numpy as jnp
        import numpy as np
        B, T, D = (2, 512, 256)
        E, H, K = (8, 512, 2)
        key = jax.random.key(seed)
        ks = jax.random.split(key, 5)
        s = 0.02
        return {'x': jax.random.normal(ks[0], (B, T, D), dtype=jnp.float32), 'gate_w': jax.random.normal(ks[1], (E, D), dtype=jnp.float32) * s, 'w1': jax.random.normal(ks[2], (E, H, D), dtype=jnp.float32) * s, 'w2': jax.random.normal(ks[3], (E, D, H), dtype=jnp.float32) * s, 'w3': jax.random.normal(ks[4], (E, H, D), dtype=jnp.float32) * s}
    _L0_ffn_all = _L0_ffn_setup()
    _L0_ffn_in = {k: v for k, v in _L0_ffn_all.items() if k in ('gate_w', 'w1', 'w2', 'w3')}
    del _L0_ffn_all

    def _L1_conv_setup():
        import jax, jax.numpy as jnp
        import numpy as np
        IN_C = 256
        OUT_C = 256
        N, H, W = (32, 28, 28)
        key = jax.random.key(seed)
        k1, k2, k3 = jax.random.split(key, 3)
        x = jax.random.normal(k1, (N, IN_C, H, W), dtype=jnp.float32)
        weight = jax.random.normal(k2, (OUT_C, IN_C), dtype=jnp.float32)
        bound = 1.0 / np.sqrt(IN_C)
        bias = jax.random.uniform(k3, (OUT_C, 1), dtype=jnp.float32, minval=-bound, maxval=bound)
        return {'x': x, 'weight': weight, 'bias': bias}
    _L1_conv_all = _L1_conv_setup()
    _L1_conv_in = {k: v for k, v in _L1_conv_all.items() if k in ('weight', 'bias')}
    del _L1_conv_all

    def _L1_ffn_setup():
        import jax, jax.numpy as jnp
        import numpy as np
        B, S, D, F, E, K = (4, 512, 256, 1024, 8, 2)
        key = jax.random.key(seed)
        ks = jax.random.split(key, 6)
        sc = 0.02
        return {'x': jax.random.normal(ks[0], (B, S, D), jnp.float32), 'gate_w': jax.random.normal(ks[1], (D, E), jnp.float32) * sc, 'gate_b': jnp.zeros((E,), jnp.float32), 'w1': jax.random.normal(ks[2], (E, D, F), jnp.float32) * sc, 'b1': jnp.zeros((E, F), jnp.float32), 'w2': jax.random.normal(ks[3], (E, F, D), jnp.float32) * sc, 'b2': jnp.zeros((E, D), jnp.float32)}
    _L1_ffn_all = _L1_ffn_setup()
    _L1_ffn_in = {k: v for k, v in _L1_ffn_all.items() if k in ('gate_w', 'gate_b', 'w1', 'b1', 'w2', 'b2')}
    del _L1_ffn_all
    return {'x': x, 'L0_conv_conv_w': _L0_conv_in['conv_w'], 'L0_conv_conv_b': _L0_conv_in['conv_b'], 'L0_conv_gn_w': _L0_conv_in['gn_w'], 'L0_conv_gn_b': _L0_conv_in['gn_b'], 'L0_ffn_gate_w': _L0_ffn_in['gate_w'], 'L0_ffn_w1': _L0_ffn_in['w1'], 'L0_ffn_w2': _L0_ffn_in['w2'], 'L0_ffn_w3': _L0_ffn_in['w3'], 'L1_conv_weight': _L1_conv_in['weight'], 'L1_conv_bias': _L1_conv_in['bias'], 'L1_ffn_gate_w': _L1_ffn_in['gate_w'], 'L1_ffn_gate_b': _L1_ffn_in['gate_b'], 'L1_ffn_w1': _L1_ffn_in['w1'], 'L1_ffn_b1': _L1_ffn_in['b1'], 'L1_ffn_w2': _L1_ffn_in['w2'], 'L1_ffn_b2': _L1_ffn_in['b2']}

def reference(x, L0_conv_conv_w, L0_conv_conv_b, L0_conv_gn_w, L0_conv_gn_b, L0_ffn_gate_w, L0_ffn_w1, L0_ffn_w2, L0_ffn_w3, L1_conv_weight, L1_conv_bias, L1_ffn_gate_w, L1_ffn_gate_b, L1_ffn_w1, L1_ffn_b1, L1_ffn_w2, L1_ffn_b2):
    import jax
    import jax.numpy as jnp

    def _L0_conv_ref(x, conv_w, conv_b, gn_w, gn_b):
        import jax, jax.numpy as jnp
        import numpy as np
        GROUPS = 32
        EPS = 1e-05
        b, c, h, w = x.shape
        cg = c // GROUPS
        g = x.reshape(b * GROUPS, cg, h, w)

        def conv1x1(t):
            return jnp.einsum('oi,bil->bol', conv_w, t) + conv_b[None, :, None]

        def gnorm(t):
            mu = t.mean(axis=(2, 3), keepdims=True)
            var = t.var(axis=(2, 3), keepdims=True)
            return (t - mu) * jax.lax.rsqrt(var + EPS) * gn_w[None, :, None, None] + gn_b[None, :, None, None]

        def branch(ph, pw):
            hw = conv1x1(jnp.concatenate([ph, pw], axis=2))
            ah, aw = (hw[:, :, :h], hw[:, :, h:])
            gated = g * jax.nn.sigmoid(ah)[..., None] * jax.nn.sigmoid(aw)[:, :, None, :]
            return gnorm(gated)
        x1 = branch(g.mean(axis=3), g.mean(axis=2))
        y1 = branch(g.max(axis=3), g.max(axis=2))
        x11 = x1.reshape(b * GROUPS, cg, h * w)
        y11 = y1.reshape(b * GROUPS, cg, h * w)
        x12 = jax.nn.softmax(x1.mean(axis=(2, 3)), axis=-1)
        y12 = jax.nn.softmax(y1.max(axis=(2, 3)), axis=-1)
        weights = jnp.einsum('bc,bcl->bl', x12, y11) + jnp.einsum('bc,bcl->bl', y12, x11)
        out = g * jax.nn.sigmoid(weights).reshape(b * GROUPS, 1, h, w)
        return out.reshape(b, c, h, w)

    def _L0_ffn_ref(x, gate_w, w1, w2, w3):
        import jax, jax.numpy as jnp
        import numpy as np
        B, T, D = (2, 512, 256)
        E, H, K = (8, 512, 2)
        Bb, Tt, Dd = x.shape
        xf = x.reshape(-1, Dd)
        logits = xf @ gate_w.T
        probs = jax.nn.softmax(logits, axis=-1)
        vals, idx = jax.lax.top_k(probs, K)
        w = vals / (vals.sum(-1, keepdims=True) + 1e-08)
        onehot = jax.nn.one_hot(idx, E, dtype=xf.dtype)
        comb = jnp.einsum('nk,nke->ne', w, onehot)
        h = jnp.einsum('nd,ehd->neh', xf, w1)
        g = jnp.einsum('nd,ehd->neh', xf, w3)
        eo = jnp.einsum('neh,edh->ned', jax.nn.silu(h) * g, w2)
        out = jnp.einsum('ned,ne->nd', eo, comb)
        return out.reshape(Bb, Tt, Dd)

    def _L1_conv_ref(x, weight, bias):
        import jax, jax.numpy as jnp
        import numpy as np
        IN_C = 256
        OUT_C = 256
        N, H, W = (32, 28, 28)
        out = jnp.einsum('oi,nihw->nohw', weight, x)
        out = out + bias[:, 0][None, :, None, None]
        return out

    def _L1_ffn_ref(x, gate_w, gate_b, w1, b1, w2, b2):
        import jax, jax.numpy as jnp
        import numpy as np
        B, S, D, F, E, K = (4, 512, 256, 1024, 8, 2)
        b, s, d = x.shape
        e = gate_w.shape[1]
        xf = x.reshape(-1, d)
        t = xf.shape[0]
        router = jax.nn.softmax(xf @ gate_w + gate_b, axis=-1)
        k_scores, k_idx = jax.lax.top_k(router, K)
        comb = jnp.zeros((t, e), x.dtype).at[jnp.arange(t)[:, None], k_idx].add(k_scores)
        out = jnp.zeros_like(xf)
        for i in range(e):
            h = jax.nn.silu(xf @ w1[i] + b1[i])
            y = h @ w2[i] + b2[i]
            out = out + y * comb[:, i:i + 1]
        return out.reshape(b, s, d)

    def _gn(v, G=32, eps=1e-05):
        B_, C_, H_, W_ = v.shape
        g = v.reshape(B_, G, C_ // G, H_, W_)
        m = jnp.mean(g, axis=(2, 3, 4), keepdims=True)
        s = jnp.var(g, axis=(2, 3, 4), keepdims=True)
        return ((g - m) / jnp.sqrt(s + eps)).reshape(v.shape)

    def _ln_c(v, eps=1e-06):
        m = jnp.mean(v, axis=1, keepdims=True)
        s = jnp.var(v, axis=1, keepdims=True)
        return (v - m) / jnp.sqrt(s + eps)

    def _ln_t(v, eps=1e-05):
        m = jnp.mean(v, axis=-1, keepdims=True)
        s = jnp.var(v, axis=-1, keepdims=True)
        return (v - m) / jnp.sqrt(s + eps)

    def _to_tokens(v):
        B_, C_, H_, W_ = v.shape
        return v.reshape(B_, C_, H_ * W_).transpose(0, 2, 1)

    def _from_tokens(t, like):
        B_, C_, H_, W_ = like.shape
        return t.transpose(0, 2, 1).reshape(B_, C_, H_, W_)
    x = x + _L0_conv_ref(_ln_c(x), L0_conv_conv_w, L0_conv_conv_b, L0_conv_gn_w, L0_conv_gn_b)
    t = _to_tokens(x)
    t = t + _L0_ffn_ref(_ln_t(t), L0_ffn_gate_w, L0_ffn_w1, L0_ffn_w2, L0_ffn_w3)
    x = _from_tokens(t, x)
    x = x + _L1_conv_ref(_ln_c(x), L1_conv_weight, L1_conv_bias)
    t = _to_tokens(x)
    t = t + _L1_ffn_ref(_ln_t(t), L1_ffn_gate_w, L1_ffn_gate_b, L1_ffn_w1, L1_ffn_b1, L1_ffn_w2, L1_ffn_b2)
    x = _from_tokens(t, x)
    return x

_drawn_inputs = setup_inputs


def setup_inputs(seed=0):
    import zlib

    import numpy as np

    out = dict(_drawn_inputs(seed))
    spreads = {'L0_conv_gn_w': (1.0, 0.2),
     'L0_conv_gn_b': (0.0, 0.587),
     'L1_ffn_gate_b': (0.0, 0.8),
     'L1_ffn_b1': (0.0, 0.8),
     'L1_ffn_b2': (0.0, 0.8)}
    factors = {'L0_conv_conv_b': 8.0,
     'L0_ffn_gate_w': 5.867,
     'L0_ffn_w1': 5.131,
     'L0_ffn_w2': 5.09,
     'L0_ffn_w3': 5.096,
     'L1_conv_bias': 8.0,
     'L1_ffn_gate_w': 8.0,
     'L1_ffn_w1': 8.0,
     'L1_ffn_w2': 8.0}
    for name, (base, spread) in spreads.items():
        noise = np.random.default_rng([zlib.crc32(name.encode()), seed]).standard_normal(out[name].shape)
        drawn = base * np.exp(spread * noise) if base else spread * noise
        out[name] = jnp.asarray(drawn.astype(out[name].dtype))
    for name, factor in factors.items():
        out[name] = (out[name] * factor).astype(out[name].dtype)
    return out
```

```python
from contextlib import ExitStack

import concourse.bass as bass
from concourse import mybir

ALU = mybir.AluOpType
ACT = mybir.ActivationFunctionType
AX = mybir.AxisListType
F32 = mybir.dt.float32
F16 = mybir.dt.float16
I32 = mybir.dt.int32
U32 = mybir.dt.uint32

P = 128
NB, C, HW = 16, 256, 16
L = HW * HW
KC = C // P
HB = NB // 2
UT = L // P
NT = NB * UT
CG = 8
NG = P // CG
E = 8
FH = (512, 1024)
TILE = 256
TILES = (2 * NB * L + E * TILE) // TILE
XSCALE = 1024.0
BIG = 2.0 ** 14


def bass_metaformer(nc, x, conv_w, conv_b, gn_w, gn_b, gate0, w1, w2, w3, weight, bias,
                    gate1, gate1_b, v1, b1, v2, b2, out):
    ctx = ExitStack()
    with ctx:
        def sb(name, shape, dt=F32):
            return ctx.enter_context(nc.sbuf_tensor(name, shape, dt))

        def sem(name):
            return ctx.enter_context(nc.semaphore(name))

        def sem2(name):
            return [sem(f"{name}_{j}") for j in range(2)]

        sorted_x = nc.dram_tensor("sorted_x", ((TILES + 1) * TILE, 2 * C), F16, kind="Internal").ap()
        sorted_y = nc.dram_tensor("sorted_y", (TILES * TILE, C), F32, kind="Internal").ap()

        bank = [ctx.enter_context(nc.psum_tensor(f"bank{n}", [P, 512], F32)) for n in range(8)]
        turn = bank[0:2]
        zb = bank[2:6]
        yb = bank[6]
        misc = bank[7]

        tok = sb("tok", [P, NT, C])
        region = sb("region", [P, 8192])
        wreg = sb("wreg", [P, 32768])
        line = region[:, 0:2048].rearrange("p (r k b l) -> p r k b l", r=2, k=KC, b=NB)
        sig = region[:, 2048:4096].rearrange("p (r k b l) -> p r k b l", r=2, k=KC, b=NB)
        rows = region[:, :].bitcast(F16).rearrange("p (t c) -> p t c", t=NT)
        gate_act = region[:, 0:2048].rearrange("p (h n) -> p h n", h=4)
        hid_hi = region[:, 2048:3072].bitcast(F16).rearrange("p (c n) -> p c n", n=TILE)
        hid_lo = region[:, 3072:4096].bitcast(F16).rearrange("p (c n) -> p c n", n=TILE)
        hid = region[:, 5632:6656].rearrange("p (h n) -> p h n", h=2)
        b2_all = region[:, 5632:7680].rearrange("p (e c) -> p e c", e=E)
        x_rows = region[:, 4096:4608].bitcast(F16).rearrange("p (g c) -> p g c", g=2)
        x_cols = region[:, 4608:5120].bitcast(F16).rearrange("p (k s n) -> p k s n", k=KC, s=2)
        y_rows = region[:, 5120:5632].rearrange("p (g c) -> p g c", g=2)
        stage1 = region[:, :].rearrange("p (j m n) -> p j m n", j=2, m=2)
        g = wreg[:, 0:8192].rearrange("p (k n) -> p k n", k=KC)
        gated = wreg[:, 8192:24576].rearrange("p (r k n) -> p r k n", r=2, k=KC)
        w1_s = wreg[:, 0:8192].bitcast(F16).rearrange("p (e k s n) -> p e k s n", e=E, k=KC, s=2)
        w3_s = wreg[:, 8192:16384].bitcast(F16).rearrange("p (e k s n) -> p e k s n", e=E, k=KC, s=2)
        w2_s = wreg[:, 16384:24576].bitcast(F16).rearrange("p (e c s n) -> p e c s n", e=E, c=4, s=2)
        stage0 = wreg[:, 24576:30720].rearrange("p (j m n) -> p j m n", j=2, m=3)
        v1_s = wreg[:, 0:16384].bitcast(F16).rearrange("p (e k s n) -> p e k s n", e=E, k=KC, s=2)
        v2_s = wreg[:, 16384:32768].bitcast(F16).rearrange("p (e c s n) -> p e c s n", e=E, c=8, s=2)

        x_in = region[:, 4096:5120].rearrange("p (j k n) -> p j k n", j=2, k=KC)
        mix = region[:, 5120:6144].rearrange("p (j r k n) -> p j r k n", j=2, r=2, k=KC)
        sig_mix = region[:, 6144:7168].rearrange("p (j k n) -> p j k n", j=2, k=KC)
        own = iter((region[:, a:b] for a, b in [(7168 + 64 * n, 7232 + 64 * n) for n in range(7)]))
        four = lambda v: v.rearrange("p (r k b) -> p r k b", r=2, k=KC)
        coef, a_gn, b_gn, soft, shift, ends = (four(next(own)) for _ in range(6))
        soft_in = next(own)
        soft_t = region[0:64, 7616:7872].rearrange("p (a n) -> p a n", a=2)
        soft_s = region[0:64, 7872:7904].rearrange("p (a n) -> p a n", a=2)
        in_group = region[:, 7904:8032]
        conv_bd = region[:, 8032:8160]
        xn = sb("xn", [P, 2, UT, C])
        xt = sb("xt", [P, 2, KC, L])
        ident = sb("ident", [P, P])
        ident16 = sb("ident16", [P, P], F16)
        ones16 = sb("ones16", [P, P], F16)
        before16 = sb("before16", [P, P], F16)
        small = sb("small", [P, CG + 3])
        st = sb("st", [P, NT, 6])
        st_gn = xt[:, 0].rearrange("p k n -> p (k n)")[:, 0:384].rearrange("p (n s) -> p n s", s=6)
        conv1_nat = xn[:, 0].rearrange("p a c -> p (a c)").rearrange("p (q i) -> p q i", q=KC)
        gate0_nat = xt[0:E, 1].rearrange("p k n -> p (k n)")[:, 0:C]
        b1_nat = xt[0:64, 1].rearrange("p k n -> p (k n)")[:, C:C + P]
        gath0 = [xn[:, 0], xn[:, 1], xt[:, 0], xt[:, 1]]
        gath1 = [wreg[:, 512 * n:512 * n + 512].rearrange("p (a c) -> p a c", a=2) for n in range(4)]
        quart = [v[:, j, h] for v in (xn, xt) for j in range(2) for h in range(2)]
        lg, ex, hot1, hot2, eq, slot_f, incl, tot = (q.rearrange("p (t e) -> p t e", e=E) for q in quart)
        hots16 = sb("hots16", [P, NT, E], F16)
        conv1_wt = sb("conv1_wt", [P, KC, C])
        bias_row, ones_row = region[0:1, 0:C], region[0:1, C:C + P]
        gate_w = sb("gate_w", [P, 2, KC, E])
        gate_b = sb("gate_b", [P, E])
        rank = sb("rank", [P, E])
        top = sb("top", [P, 4, NT])
        red = sb("red", [P, 2, NT])
        per_e = sb("per_e", [P, 4, E])
        int_e = sb("int_e", [P, 2, E], I32)
        bounds = sb("bounds", [P, E + 1], I32)
        slots = sb("slots", [P, 2, NT], U32)
        b1_t = sb("b1_t", [P, E, 8])
        peak = sb("peak", [P, E, 3])
        peak_all = sb("peak_all", [P, E, 3])
        pw = sb("pw", [P, E, 3])
        inv = sb("inv", [P, E, 3])
        scl = sb("scl", [P, E, 3])
        fac = sb("fac", [P, 3, E])
        mean, var, rstd = (sb(name, [P, NT]) for name in ("mean", "var", "rstd"))
        tmp = sb("tmp", [P, 4, NT])
        wide = xt[:, 1].rearrange("p k n -> p (k n)")
        tmp_gn = wide[:, 0:256].rearrange("p (q n) -> p q n", q=4)
        mean_gn, var_gn, rstd_gn = (wide[:, 256 + 64 * q:320 + 64 * q] for q in range(3))

        step = sem("vector_step")
        consts = sem("consts")
        params = sem("params")

        x_loaded, x_turned, x_copied = sem2("x_loaded"), sem2("x_turned"), sem2("x_copied")
        stats = sem("stats")
        var_ready = [sem(f"var_ready{s}") for s in range(5)]
        sd_ready = [sem(f"sd_ready{s}") for s in range(5)]
        xn_ready, xn_turned, xt_ready, xt_used = sem2("xn_ready"), sem2("xn_turned"), sem2("xt_ready"), sem2("xt_used")
        bd_ready, lines_ready, gates_psum, sig_ready = sem("bd_ready"), sem("lines_ready"), sem("gates_psum"), sem("sig_ready")
        gated_mid, gated_ready, gn_stats = sem("gated_mid"), sem("gated_ready"), sem("gn_stats")
        logit_ready, logit_turned, logit_sub, logit_exp = sem("logit_ready"), sem("logit_turned"), sem("logit_sub"), sem("logit_exp")
        soft_ready, soft_turned, shift_ready, shift_psum = sem("soft_ready"), sem("soft_turned"), sem("shift_ready"), sem("shift_psum")
        coef_ready = sem("coef_ready")
        mix_ready, mix_psum, mix_sig, mix_out = sem2("mix_ready"), sem2("mix_psum"), sem2("mix_sig"), sem2("mix_out")
        mix_turned, mix_added = sem2("mix_turned"), sem2("mix_added")
        fin_turned, fin_copied, fin_stored = sem2("fin_turned"), sem2("fin_copied"), sem2("fin_stored")


        zeros = wreg[:, 30720:32768]
        ZX = (TILES + 1) * TILE * 2 * C // P
        ZY = TILES * TILE * C // P
        ZERO_DMAS = -(-ZX // 4096) + -(-ZY // 2048)
        zeroed, zero_stored = sem("zeroed"), sem("zero_stored")
        nat_loaded, nat_turned, nat_copied, bias_loaded = sem("nat_loaded"), sem("nat_turned"), sem("nat_copied"), sem("bias_loaded")
        gates_loaded, ones_set = sem("gates_loaded"), sem("ones_set")
        two = lambda name: [sem(f"{name}{f}") for f in range(2)]
        rows_hi, rows_ready = sem2("rows_hi"), sem2("rows_ready")
        router_psum, exp_in, exp_out = two("router_psum"), two("exp_in"), two("exp_out")
        hots_ready, counts_psum, slots_ready, scattered = two("hots_ready"), two("counts_psum"), two("slots_ready"), two("scattered")
        y_used = [sem(f"y_used_{n}") for n in range(4)]
        y_gathered = [sem(f"y_gathered_{n}") for n in range(4)]
        y_half = two("y_half")
        peak_ready, peak_spread = two("peak_ready"), two("peak_spread")
        stage_loaded = [sem2(f"stage_loaded{f}") for f in range(2)]
        w_scale, w_turned, w_hi, w_lo = two("w_scale"), sem("w_turned"), two("w_hi"), two("w_lo")
        pw_step = two("pw_step")
        fac_ready = two("fac_ready")
        xr_loaded, xr_turned, xc_ready = two("xr_loaded"), two("xr_turned"), two("xc_ready")
        z_ready, silu_done, hid_ready, hi_ready, lo_ready = two("z_ready"), two("silu_done"), sem("hid_ready"), two("hi_ready"), two("lo_ready")
        y_ready, y_copied, y_stored = two("y_ready"), two("y_copied"), two("y_stored")
        conv_psum, conv_added = sem2("conv_psum"), sem2("conv_added")
        late_loaded, b1_turned, b1_ready = sem("late_loaded"), sem("b1_turned"), sem("b1_ready")

        block = ctx.enter_context(nc.Block())

        @block.sync
        def _(sp):
            sp.dma_start(conv1_nat, weight.rearrange("(q p) i -> p q i", p=P)).then_inc(nat_loaded, 16)
            sp.dma_start(gate0_nat, gate0).then_inc(nat_loaded, 16)
            sp.dma_start(b1_nat, b1.rearrange("e (c n) -> (e c) n", n=P)).then_inc(nat_loaded, 16)
            sp.dma_start(gate_w[:, 1], gate1.rearrange("(k p) e -> p k e", p=P)).then_inc(gates_loaded, 16)
            sp.dma_start(gate_b[:], gate1_b.partition_broadcast(P)).then_inc(gates_loaded, 16)
            w_t = conv_w.rearrange("o i -> i o")
            for n in range(NG):
                at = slice(n * CG, (n + 1) * CG)
                sp.dma_start(small[at, 0:CG], w_t, allow_slow_non_contiguous=True).then_inc(params, 16)
                for c, v in enumerate((conv_b, gn_w, gn_b)):
                    sp.dma_start(small[at, CG + c:CG + c + 1], v.rearrange("(c a) -> c a", a=1)).then_inc(params, 16)
            with sp.Fori(0, HB) as i:
                for j in range(2):
                    sp.wait_ge(x_turned[j], i)
                    sp.dma_start(x_in[:, j], x[bass.ds(2 * i + j, 1)].rearrange("a (k p) l -> p (a k) l", p=P)
                                 ).then_inc(x_loaded[j], 16)
            sp.wait_ge(zeroed, 1)
            zx = sorted_x.rearrange("(p a) c -> p (a c)", p=P)
            for a in range(0, ZX, 4096):
                n = min(4096, ZX - a)
                sp.dma_start(zx[:, a:a + n], zeros.bitcast(F16)[:, 0:n]).then_inc(zero_stored, 16)
            zy = sorted_y.rearrange("(p a) c -> p (a c)", p=P)
            for a in range(0, ZY, 2048):
                n = min(2048, ZY - a)
                sp.dma_start(zy[:, a:a + n], zeros[:, 0:n]).then_inc(zero_stored, 16)

            def load_stage0(e, j):
                for m, w in enumerate((w1, w3)):
                    sp.dma_start(stage0[:, j, m].rearrange("p (c d) -> p c d", c=4),
                                 w[bass.ds(e, 1)].rearrange("a (c p) d -> p (a c) d", p=P)).then_inc(stage_loaded[0][j], 16)
                sp.dma_start(stage0[:, j, 2].rearrange("p (c h) -> p c h", c=KC),
                             w2[bass.ds(e, 1)].rearrange("a (c p) h -> p (a c) h", p=P)).then_inc(stage_loaded[0][j], 16)

            def load_stage1(e, j):
                sp.dma_start(stage1[:, j, 0].rearrange("p (c h) -> p c h", c=KC),
                             v1[bass.ds(e, 1)].rearrange("a (c p) h -> p (a c) h", p=P)).then_inc(stage_loaded[1][j], 16)
                sp.dma_start(stage1[:, j, 1].rearrange("p (c d) -> p c d", c=8),
                             v2[bass.ds(e, 1)].rearrange("a (c p) d -> p (a c) d", p=P)).then_inc(stage_loaded[1][j], 16)

            def load_rows(tile):
                return sp.dma_start(x_rows, sorted_x[bass.ds(tile * TILE, TILE)].rearrange("(g p) c -> p g c", p=P))

            for f, load in enumerate((load_stage0, load_stage1)):
                if f == 1:
                    sp.wait_ge(y_stored[0], 16 * total)
                for j in range(2):
                    load(j, j)
                with sp.Fori(1, E // 2) as i:
                    for j in range(2):
                        sp.wait_ge(w_lo[f], 2 * i + j - 1)
                        load(2 * i + j, j)
                if f == 1:
                    sp.wait_ge(w_lo[1], E)
                    sp.dma_start(bias_row, bias.rearrange("c a -> a c"), allow_slow_non_contiguous=True).then_inc(bias_loaded, 16)
                sp.wait_ge(scattered[f], 16 * 2 * NT)
                total = sp.value_load(bounds[0:1, E:E + 1], min_val=E, max_val=TILES)
                if f == 1:
                    sp.dma_start(b2_all, b2.partition_broadcast(P)).then_inc(late_loaded, 16)
                load_rows(0).then_inc(xr_loaded[f], 16)
                with sp.Fori(0, total) as n:
                    sp.wait_ge(xr_turned[f], n + 1)
                    load_rows(n + 1).then_inc(xr_loaded[f], 16)
                    sp.wait_ge(y_copied[f], n + 1)
                    sp.dma_start(sorted_y[bass.ds(n * TILE, TILE)].rearrange("(g p) c -> p g c", p=P), y_rows
                                 ).then_inc(y_stored[f], 16)

        @block.gpsimd
        def _(pool):
            ones = zeros[:, 0:P]
            nc.gpsimd.memset(ones, 1.0).then_inc(consts, 1)
            nc.gpsimd.memset(ident[:], 0.0).then_inc(consts, 1)
            nc.gpsimd.memset(ones16[:], 1.0).then_inc(consts, 1)
            nc.gpsimd.iota(int_e[:, 0, :], [[-1, E]], base=E, channel_multiplier=0).then_inc(consts, 1)
            pool.wait_ge(consts, 4)
            nc.gpsimd.affine_select(out=ident[:], in_=ident[:], compare_op=ALU.not_equal, fill=1.0, base=0,
                                    pattern=[[-1, P]], channel_multiplier=1).then_inc(consts, 1)
            nc.gpsimd.affine_select(out=before16[:], in_=ones16[:], compare_op=ALU.is_gt, fill=0.0, base=0,
                                    pattern=[[1, P]], channel_multiplier=-1).then_inc(consts, 1)
            grp = in_group.rearrange("p (g c) -> p g c", c=CG)
            nc.gpsimd.affine_select(out=grp, in_=ones.rearrange("p (g c) -> p g c", c=CG),
                                    compare_op=ALU.is_ge, fill=0.0, base=0,
                                    pattern=[[-CG, NG], [0, CG]], channel_multiplier=1).then_inc(consts, 1)
            nc.gpsimd.tensor_copy(rank[:], int_e[:, 0, :]).then_inc(consts, 1)
            pool.wait_ge(consts, 8)
            nc.gpsimd.tensor_copy(ident16[:], ident[:]).then_inc(consts, 1)
            nc.gpsimd.affine_select(out=grp, in_=grp, compare_op=ALU.is_ge, fill=0.0, base=CG - 1,
                                    pattern=[[CG, NG], [0, CG]], channel_multiplier=-1).then_inc(consts, 1)
            nc.gpsimd.memset(zeros, 0.0).then_inc(zeroed, 1)

            def scatter(f, t, k):
                nc.gpsimd.indirect_dma_start(sorted_x, bass.IndirectOffsetOnAxis(ap=slots[:, k, t:t + 1], axis=0),
                                             rows[:, t, :], None).then_inc(scattered[f], 16)

            def gather(f, t):
                pool.wait_ge(y_used[t % 4], HB * f + t // 4)
                to = (gath0, gath1)[f][t % 4]
                for k in range(2):
                    nc.gpsimd.indirect_dma_start(to[:, k, :], None, sorted_y,
                                                 bass.IndirectOffsetOnAxis(ap=slots[:, k, t:t + 1], axis=0)
                                                 ).then_inc(y_gathered[t % 4], 16)

            for f in range(2):
                pool.wait_ge(slots_ready[f], 1)
                for j in range(2):
                    pool.wait_ge(rows_ready[j], HB * (f + 1))
                if f == 0:
                    pool.wait_ge(zero_stored, 16 * ZERO_DMAS)
                for n in range(E):
                    if f == 0:
                        pool.wait_ge(peak_ready[f], n + 1)
                        nc.gpsimd.partition_all_reduce(peak_all[:, n], peak[:, n], P, bass.bass_isa.ReduceOp.max
                                                       ).then_inc(peak_spread[f], 1)
                    for t in range(4 * n, 4 * n + 4):
                        for k in range(2):
                            scatter(f, t, k)
                total = pool.value_load(bounds[0:1, E:E + 1], min_val=E, max_val=TILES)
                if f == 0:
                    for n in range(E):
                        pool.wait_ge(peak_ready[1], n + 1)
                        nc.gpsimd.partition_all_reduce(peak_all[:, n], peak[:, n], P, bass.bass_isa.ReduceOp.max
                                                       ).then_inc(peak_spread[1], 1)
                with pool.Fori(0, total) as n:
                    pool.wait_ge(xc_ready[f], n + 2)
                    pool.wait_ge(y_stored[f], 16 * (n + 1))
                for t in range(NT):
                    gather(f, t)

        CONSTS = 10

        @block.tensor
        def _(pe):
            def norm_turn(s, i, j):
                pe.wait_ge(xn_ready[j], HB * s + i + 1)
                pe.wait_ge(xt_ready[j], HB * s + i)
                to = turn[j][:].rearrange("p (k n) -> p k n", k=KC)
                for k in range(KC):
                    for h in range(UT):
                        last = pe.transpose(to[:, k, h * P:(h + 1) * P], xn[:, j, h, k * P:(k + 1) * P], ident[:])
                last.then_inc(xn_turned[j], 1)

            pe.wait_ge(consts, CONSTS)
            pe.wait_ge(nat_loaded, 16 * 3)
            for q in range(KC):
                for k in range(KC):
                    pe.transpose(zb[0][:, k * C + q * P:k * C + (q + 1) * P], conv1_nat[:, q, k * P:(k + 1) * P], ident[:])
            for k in range(KC):
                pe.transpose(zb[1][:, k * E:(k + 1) * E], gate0_nat[:, k * P:(k + 1) * P], ident[0:E, 0:E])
            pe.transpose(zb[1][:, 64:128], b1_nat, ident[0:64, 0:64]).then_inc(nat_turned, 1)
            with pe.Fori(0, HB) as i:
                for j in range(2):
                    pe.wait_ge(x_loaded[j], 16 * (i + 1))
                    pe.wait_ge(x_copied[j], i)
                    to = turn[j][:].rearrange("p (h c) -> p h c", h=UT)
                    for h in range(UT):
                        for k in range(KC):
                            last = pe.transpose(to[:, h, k * P:(k + 1) * P], x_in[:, j, k, h * P:(h + 1) * P], ident[:])
                    last.then_inc(x_turned[j], 1)
            with pe.Fori(0, HB) as i:
                for j in range(2):
                    norm_turn(0, i, j)
            pe.wait_ge(bd_ready, 1)
            for r in range(2):
                for k in range(KC):
                    pe.wait_ge(lines_ready, 2 * (r * KC + k) + 2)
                    pe.matmul(zb[2 * r + k][:], conv_bd[:], line[:, r, k].rearrange("p b l -> p (b l)"),
                              start=True, stop=True).then_inc(gates_psum, 1)
            pe.wait_ge(logit_ready, 1)
            pe.transpose(misc[0:64, 0:P], soft_in[:], ident[:]).then_inc(logit_turned, 1)
            pe.wait_ge(soft_ready, 1)
            pe.transpose(misc[:, P:P + 64], soft_t[:, 0, :], ident[0:64, 0:64]).then_inc(soft_turned, 1)
            pe.wait_ge(shift_ready, 1)
            pe.matmul(misc[:, 256:256 + KC * NB], in_group[:], shift[:, 0].rearrange("p k b -> p (k b)"),
                      start=True, stop=True).then_inc(shift_psum, 1)
            with pe.Fori(0, HB) as i:
                for j in range(2):
                    pe.wait_ge(mix_ready[j], i + 1)
                    pe.wait_ge(mix_sig[j], i)
                    for k in range(KC):
                        for r in range(2):
                            last = pe.matmul(zb[j][:, k * L:(k + 1) * L], mix[:, j, r, k],
                                             gated[:, r, k, bass.ds((2 * i + j) * L, L)], start=(r == 0), stop=(r == 1))
                    last.then_inc(mix_psum[j], 1)
                for j in range(2):
                    pe.wait_ge(mix_out[j], i + 1)
                    pe.wait_ge(mix_added[j], i)
                    to = turn[j][:].rearrange("p (h c) -> p h c", h=UT)
                    for h in range(UT):
                        for k in range(KC):
                            last = pe.transpose(to[:, h, k * P:(k + 1) * P], sig_mix[:, j, k, h * P:(h + 1) * P], ident[:])
                    last.then_inc(mix_turned[j], 1)
            def router(f, i, j):
                pe.wait_ge(xt_ready[j], HB * (2 * f + 1) + i + 1)
                for h in range(UT):
                    for k in range(KC):
                        last = pe.matmul(yb[:, bass.ds((4 * i + 2 * j + h) * E, E)], xt[:, j, k, h * P:(h + 1) * P],
                                         gate_w[:, f, k], start=(k == 0), stop=(k == KC - 1))
                last.then_inc(xt_used[j], 1)

            def routing(f):
                with pe.Fori(0, HB) as i:
                    for j in range(2):
                        norm_turn(2 * f + 1, i, j)
                    for j in range(2):
                        router(f, i, j)
                pe.wait_ge(hots_ready[f], 1)
                flat_hots = hots16[:].rearrange("p t e -> p (t e)")
                pe.matmul(misc[:, 0:NT * E], before16[:], flat_hots, start=True, stop=True)
                pe.matmul(misc[:, NT * E:2 * NT * E], ones16[:], flat_hots, start=True, stop=True).then_inc(counts_psum[f], 1)

            def stage_turns(i, j):
                e = 2 * i + j
                pe.wait_ge(stage_loaded[0][j], 48 * (i + 1))
                pe.wait_ge(w_lo[0], e)
                for m in range(2):
                    for k in range(KC):
                        for c in range(4):
                            last = pe.transpose(zb[2 * m + k][:, c * P:(c + 1) * P],
                                                stage0[:, j, m, c * C + k * P:c * C + (k + 1) * P], ident[:])
                        last.then_inc(w_turned, 1)
                for c in range(4):
                    for k in range(KC):
                        last = pe.transpose(turn[c // 2][:, (c % 2) * C + k * P:(c % 2) * C + (k + 1) * P],
                                            stage0[:, j, 2, k * FH[0] + c * P:k * FH[0] + (c + 1) * P], ident[:])
                    if c % 2:
                        last.then_inc(w_turned, 1)

            x_turn16 = turn[0][:].bitcast(F16).rearrange("p (k s n) -> p k s n", k=KC, s=2)

            def turn_rows(f, tile):
                pe.wait_ge(xr_loaded[f], 16 * (tile + 1))
                for k in range(KC):
                    for s_ in range(2):
                        for r in range(2):
                            last = pe.transpose(x_turn16[:, k, s_, r * P:(r + 1) * P],
                                                x_rows[:, r, s_ * C + k * P:s_ * C + (k + 1) * P], ident16[:])
                last.then_inc(xr_turned[f], 1)

            PARTS = ((0, 0), (0, 1), (1, 0))

            def up(f, e, h):
                ws = ((w1_s, zb[2 * (h % 2)]), (w3_s, zb[2 * (h % 2) + 1])) if f == 0 else ((v1_s, zb[h]),)
                for w, z in ws:
                    for c in (2 * h, 2 * h + 1):
                        to = z[:, (c % 2) * TILE:(c % 2 + 1) * TILE]
                        for k in range(KC):
                            for ws_, xs_ in PARTS:
                                last = pe.matmul(to, w[:, e, k, ws_, c * P:(c + 1) * P], x_cols[:, k, xs_, :],
                                                 start=(k == 0 and ws_ + xs_ == 0), stop=(k == KC - 1 and ws_ == 1))
                last.then_inc(z_ready[f], 1)

            def down(f, e, tile, h, halves):
                w = (w2_s, v2_s)[f]
                pe.wait_ge(lo_ready[f], halves * tile + h + 1)
                for c in (2 * h, 2 * h + 1):
                    for r in range(2):
                        for hs, ws_ in PARTS:
                            lhs = (hid_hi, hid_lo)[hs]
                            first = c == 0 and r == 0 and hs + ws_ == 0
                            end = c == 2 * halves - 1 and hs == 1
                            last = pe.matmul(yb[:, r * C:(r + 1) * C], lhs[:, c, r * P:(r + 1) * P], w[:, e, c, ws_, :],
                                             start=first, stop=end, skip_group_check=True)
                if h == halves - 1:
                    last.then_inc(y_ready[f], 1)

            def experts(f):
                halves = FH[f] // (2 * P)
                pe.wait_ge(w_lo[f], E)
                pe.wait_ge(fac_ready[f], 1)
                turn_rows(f, 0)
                edges = [pe.value_load(bounds[0:1, e:e + 1], min_val=0, max_val=TILES) for e in range(E + 1)]
                for e in range(E):
                    with pe.Fori(edges[e], edges[e + 1]) as n:
                        pe.wait_ge(xc_ready[f], n + 1)
                        for h in range(halves):
                            up(f, e, h)
                        pe.wait_ge(y_copied[f], n)
                        for h in range(halves - 1):
                            down(f, e, n, h, halves)
                        turn_rows(f, n + 1)
                        down(f, e, n, halves - 1, halves)

            routing(0)
            with pe.Fori(0, E // 2) as i:
                for j in range(2):
                    stage_turns(i, j)
            experts(0)
            pe.wait_ge(bias_loaded, 16)
            pe.wait_ge(ones_set, 1)
            with pe.Fori(0, HB) as i:
                for j in range(2):
                    norm_turn(2, i, j)
                for j in range(2):
                    pe.wait_ge(xt_ready[j], HB * 2 + i + 1)
                    pe.wait_ge(conv_added[j], i)
                    for h in range(UT):
                        to = zb[j][:, h * C:(h + 1) * C]
                        for k in range(KC):
                            mm = pe.matmul(to, xt[:, j, k, h * P:(h + 1) * P], conv1_wt[:, k], start=(k == 0), stop=False)
                        if h == UT - 1:
                            mm.then_inc(xt_used[j], 1)
                        last = pe.matmul(to, ones_row, bias_row, start=False, stop=True)
                    last.then_inc(conv_psum[j], 1)
            routing(1)
            experts(1)
            with pe.Fori(0, HB) as i:
                for j in range(2):
                    for h in range(UT):
                        pe.wait_ge(y_used[2 * j + h], HB + i + 1)
                    pe.wait_ge(fin_copied[j], i)
                    to = turn[j][:].rearrange("p (k n) -> p k n", k=KC)
                    for k in range(KC):
                        for h in range(UT):
                            last = pe.transpose(to[:, k, h * P:(h + 1) * P], xn[:, j, h, k * P:(k + 1) * P], ident[:])
                    last.then_inc(fin_turned[j], 1)

        @block.scalar
        def _(act):
            def deviation(s):
                act.wait_ge(var_ready[s], 1)
                r, v = (rstd[:], var[:]) if s < 4 else (rstd_gn, var_gn)
                act.activation(r, v, ACT.Sqrt).then_inc(sd_ready[s], 1)

            act.wait_ge(nat_turned, 1)
            act.activation(conv1_wt[:].rearrange("p k c -> p (k c)"), zb[0][:], ACT.Copy).then_inc(nat_copied, 1)
            act.activation(gate_w[:, 0].rearrange("p k e -> p (k e)"), zb[1][:, 0:KC * E], ACT.Copy).then_inc(nat_copied, 1)
            act.activation(b1_t[:].rearrange("p e c -> p (e c)"), zb[1][:, 64:128], ACT.Copy).then_inc(nat_copied, 1)
            with act.Fori(0, HB) as i:
                for j in range(2):
                    act.wait_ge(x_turned[j], i + 1)
                    act.activation(tok[:, bass.ds(4 * i + 2 * j, UT), :].rearrange("p h c -> p (h c)"),
                                   turn[j][:], ACT.Copy).then_inc(x_copied[j], 1)
            deviation(0)
            with act.Fori(0, HB) as i:
                for j in range(2):
                    act.wait_ge(xn_turned[j], i + 1)
                    act.activation(g[:, :, bass.ds((2 * i + j) * L, L)], turn[j][:].rearrange("p (k n) -> p k n", k=KC),
                                   ACT.Copy).then_inc(xt_ready[j], 1)
            act.wait_ge(params, 16 * 4 * NG)
            for r in range(2):
                for k in range(KC):
                    act.wait_ge(gates_psum, r * KC + k + 1)
                    act.activation(sig[:, r, k].rearrange("p b l -> p (b l)"), zb[2 * r + k][:], ACT.Sigmoid,
                                   bias=small[:, CG:CG + 1], scale=(1.0 / HW if r == 0 else 1.0)).then_inc(sig_ready, 1)
            deviation(4)
            act.wait_ge(logit_sub, 1)
            act.activation(soft_t[:, 1, :], soft_t[:, 0, :], ACT.Exp).then_inc(logit_exp, 1)
            with act.Fori(0, HB) as i:
                for j in range(2):
                    act.wait_ge(mix_psum[j], i + 1)
                    act.wait_ge(mix_turned[j], i)
                    for k in range(KC):
                        last = act.activation(sig_mix[:, j, k], zb[j][:, k * L:(k + 1) * L], ACT.Sigmoid,
                                              bias=shift[:, 1, k, bass.ds(2 * i + j, 1)])
                    last.then_inc(mix_sig[j], 1)
            def to_columns(s, i, j):
                act.wait_ge(xn_turned[j], HB * s + i + 1)
                act.wait_ge(xt_used[j], HB * (s - 1) + i)
                act.activation(xt[:, j].rearrange("p k n -> p (k n)"), turn[j][:], ACT.Copy).then_inc(xt_ready[j], 1)

            def route(f):
                deviation(2 * f + 1)
                with act.Fori(0, HB) as i:
                    for j in range(2):
                        to_columns(2 * f + 1, i, j)
                        act.activation(rows[:, bass.ds(4 * i + 2 * j, UT), 0:C], xn[:, j], ACT.Copy, scale=XSCALE
                                       ).then_inc(rows_hi[j], 1)
                act.wait_ge(exp_in[f], 1)
                act.activation(ex, lg, ACT.Exp).then_inc(exp_out[f], 1)

            def columns16(f, tile):
                act.wait_ge(xr_turned[f], tile + 1)
                act.activation(x_cols.rearrange("p k s n -> p (k s n)"), turn[0][:].bitcast(F16), ACT.Copy
                               ).then_inc(xc_ready[f], 1)

            def experts(f):
                halves = FH[f] // (2 * P)
                columns16(f, 0)
                edges = [act.value_load(bounds[0:1, e:e + 1], min_val=0, max_val=TILES) for e in range(E + 1)]
                act.wait_ge(fac_ready[f], 1)
                for e in range(E):
                    with act.Fori(edges[e], edges[e + 1]) as n:
                        for h in range(halves):
                            act.wait_ge(z_ready[f], halves * n + h + 1)
                            if f == 0:
                                act.activation(gate_act[:, h], zb[2 * h][:], ACT.Silu, scale=fac[:, 0, e:e + 1]
                                               ).then_inc(silu_done[f], 1)
                                act.wait_ge(hid_ready, halves * n + h + 1)
                                act.activation(hid_hi[:, 2 * h:2 * h + 2].rearrange("p c n -> p (c n)"), hid[:, h], ACT.Copy
                                               ).then_inc(hi_ready[f], 1)
                            else:
                                for c in range(2):
                                    last = act.activation(gate_act[:, h, c * TILE:(c + 1) * TILE], zb[h][:, c * TILE:(c + 1) * TILE],
                                                          ACT.Silu, bias=b1_t[:, e, 2 * h + c:2 * h + c + 1], scale=fac[:, 0, e:e + 1])
                                last.then_inc(silu_done[f], 1)
                        columns16(f, n + 1)
                        if f == 0:
                            act.wait_ge(y_ready[f], n + 1)
                            act.wait_ge(y_stored[f], 16 * n)
                            act.activation(y_rows.rearrange("p g c -> p (g c)"), yb[:], ACT.Copy, scale=fac[:, 2, e:e + 1]
                                           ).then_inc(y_copied[f], 1)

            route(0)
            with act.Fori(0, E // 2) as i:
                for j in range(2):
                    e = 2 * i + j
                    act.wait_ge(w_scale[0], e + 1)
                    for q in range(6):
                        act.wait_ge(w_turned, 6 * e + q + 1)
                        m, k = divmod(q, 2)
                        to = ((w1_s, w3_s)[m][:, bass.ds(e, 1), k, 0, :].rearrange("p a n -> p (a n)") if m < 2 else
                              w2_s[:, bass.ds(e, 1), 2 * k:2 * k + 2, 0, :].rearrange("p a c n -> p (a c) n"))
                        src = zb[q][:] if m < 2 else turn[k][:].rearrange("p (c n) -> p c n", c=2)
                        act.activation(to, src, ACT.Copy, scale=scl[:, bass.ds(e, 1), m:m + 1].rearrange("p a b -> p (a b)")
                                       ).then_inc(w_hi[0], 1)
            experts(0)
            with act.Fori(0, E // 2) as i:
                for j in range(2):
                    e = 2 * i + j
                    act.wait_ge(w_scale[1], e + 1)
                    for m, (w, c) in enumerate(((v1_s, KC), (v2_s, 8))):
                        act.activation(w[:, bass.ds(e, 1), :, 0, :].rearrange("p a c n -> p (a c) n"),
                                       stage1[:, j, m].rearrange("p (c n) -> p c n", c=c), ACT.Copy,
                                       scale=scl[:, bass.ds(e, 1), m:m + 1].rearrange("p a b -> p (a b)")).then_inc(w_hi[1], 1)
            deviation(2)
            with act.Fori(0, HB) as i:
                for j in range(2):
                    to_columns(2, i, j)
            route(1)
            experts(1)
            with act.Fori(0, HB) as i:
                for j in range(2):
                    act.wait_ge(fin_turned[j], i + 1)
                    act.wait_ge(fin_stored[j], 16 * i)
                    act.activation(xt[:, j].rearrange("p k n -> p (k n)"), turn[j][:], ACT.Copy).then_inc(fin_copied[j], 1)
                for j in range(2):
                    act.wait_ge(fin_copied[j], i + 1)
                    act.dma_start(out[bass.ds(2 * i + j, 1)].rearrange("a (k p) l -> p (a k) l", p=P), xt[:, j]
                                  ).then_inc(fin_stored[j], 16)
            for j in range(2):
                act.wait_ge(fin_stored[j], 16 * HB)

        @block.vector
        def _(dve):
            done = [0]

            def chain(ins):
                done[0] += 1
                ins.then_inc(step, 1)
                dve.wait_ge(step, done[0])

            def deviations(s, count, eps):
                a, b = (st[:] if s < 4 else st_gn), [(tmp if s < 4 else tmp_gn)[:, q, :] for q in range(4)]
                m, v, r = (mean[:], var[:], rstd[:]) if s < 4 else (mean_gn, var_gn, rstd_gn)
                chain(dve.tensor_tensor(b[0], a[:, :, 1], a[:, :, 4], ALU.add))
                chain(dve.tensor_tensor(b[1], a[:, :, 1], a[:, :, 4], ALU.subtract))
                chain(dve.tensor_tensor(b[2], a[:, :, 2], a[:, :, 5], ALU.add))
                chain(dve.tensor_scalar(m, b[0], 0.5, None, ALU.mult))
                chain(dve.scalar_tensor_tensor(b[3], b[1], 0.25, b[1], ALU.mult, ALU.mult))
                chain(dve.scalar_tensor_tensor(b[0], b[2], 1.0 / count, b[3], ALU.mult, ALU.add))
                dve.tensor_scalar(v, b[0], eps, None, ALU.add).then_inc(var_ready[s], 1)
                dve.wait_ge(sd_ready[s], 1)
                chain(dve.reciprocal(b[1], r))
                chain(dve.tensor_tensor(b[2], b[1], b[1], ALU.mult))
                chain(dve.tensor_tensor(b[3], b[2], v, ALU.mult))
                chain(dve.tensor_scalar(b[0], b[3], -0.5, 1.5, ALU.mult, ALU.add))
                chain(dve.tensor_tensor(r, b[1], b[0], ALU.mult))

            def tile_stats(s, i, j):
                for h in range(UT):
                    t = 4 * i + 2 * j + h
                    dve.bn_stats(st[:, bass.ds(t, 1), :].rearrange("p a b -> p (a b)"),
                                 tok[:, bass.ds(t, 1), :].rearrange("p a b -> p (a b)")).then_inc(stats, 1)

            def norm(s, i, j):
                if s % 2:
                    dve.wait_ge(rows_ready[j], HB * (s // 2) + i)
                dve.wait_ge(xn_turned[j], HB * s + i)
                for h in range(UT):
                    t = 4 * i + 2 * j + h
                    last = dve.tensor_scalar(xn[:, j, h], tok[:, bass.ds(t, 1), :].rearrange("p a b -> p (a b)"),
                                             mean[:, bass.ds(t, 1)], rstd[:, bass.ds(t, 1)], ALU.subtract, ALU.mult)
                last.then_inc(xn_ready[j], 1)

            with dve.Fori(0, HB) as i:
                for j in range(2):
                    dve.wait_ge(x_copied[j], i + 1)
                    tile_stats(0, i, j)
            dve.wait_ge(stats, NT * 1)
            deviations(0, C, 1e-6)
            with dve.Fori(0, HB) as i:
                for j in range(2):
                    norm(0, i, j)
            dve.wait_ge(params, 16 * 4 * NG)
            dve.wait_ge(consts, CONSTS)
            dve.tensor_tensor(conv_bd[:].rearrange("p (g c) -> p g c", c=CG), in_group[:].rearrange("p (g c) -> p g c", c=CG),
                              small[:, 0:CG].unsqueeze(1).to_broadcast([P, NG, CG]), ALU.mult).then_inc(bd_ready, 1)
            for j in range(2):
                dve.wait_ge(xt_ready[j], HB)
            for r, op in enumerate((ALU.add, ALU.max)):
                for k in range(KC):
                    v = g[:, k, :].rearrange("p (b h w) -> p b h w", b=NB, h=HW)
                    dve.tensor_reduce(line[:, r, k, :, 0:HW], v, AX.X, op).then_inc(lines_ready, 1)
                    dve.tensor_reduce(line[:, r, k, :, HW:2 * HW], v.rearrange("p b h w -> p b w h"), AX.X, op).then_inc(lines_ready, 1)
            for r in range(2):
                for k in range(KC):
                    dve.wait_ge(sig_ready, r * KC + k + 1)
                    v = g[:, k, :].rearrange("p (b h w) -> p b h w", b=NB, h=HW)
                    o = gated[:, r, k, :].rearrange("p (b h w) -> p b h w", b=NB, h=HW)
                    rows_g = sig[:, r, k, :, 0:HW].unsqueeze(3).to_broadcast([P, NB, HW, HW])
                    cols_g = sig[:, r, k, :, HW:2 * HW].unsqueeze(2).to_broadcast([P, NB, HW, HW])
                    dve.tensor_tensor(o, v, rows_g, ALU.mult).then_inc(gated_mid, 1)
                    dve.wait_ge(gated_mid, r * KC + k + 1)
                    dve.tensor_tensor(o, o, cols_g, ALU.mult).then_inc(gated_ready, 1)
            dve.wait_ge(nat_copied, 3)
            for r in range(2):
                for k in range(KC):
                    dve.wait_ge(gated_ready, r * KC + k + 1)
                    with dve.Fori(0, NB) as b:
                        dve.bn_stats(st_gn[:, bass.ds((r * KC + k) * NB + b, 1), :].rearrange("p a b -> p (a b)"),
                                     gated[:, r, k, bass.ds(b * L, L)]).then_inc(gn_stats, 1)
            for k in range(KC):
                v = gated[:, 1, k, :].rearrange("p (b n) -> p b n", b=NB)
                dve.tensor_reduce(ends[:, 0, k], v, AX.X, ALU.max)
                chain(dve.tensor_reduce(ends[:, 1, k], v, AX.X, ALU.min))
            dve.wait_ge(gn_stats, 64)
            deviations(4, L, 1e-5)
            flat = lambda v: v.rearrange("p r k b -> p (r k b)")
            chain(dve.tensor_scalar(flat(a_gn[:]), rstd_gn, small[:, CG + 1:CG + 2], None, ALU.mult))
            chain(dve.tensor_tensor(tmp_gn[:, 0, :], mean_gn, flat(a_gn[:]), ALU.mult))
            chain(dve.tensor_scalar(flat(b_gn[:]), tmp_gn[:, 0, :], -1.0, small[:, CG + 2:CG + 3], ALU.mult, ALU.add))
            m0, a1 = tmp_gn[:, 0, 0:32], a_gn[:, 1].rearrange("p k b -> p (k b)")
            chain(dve.tensor_tensor(m0, mean_gn[:, 0:32], a_gn[:, 0].rearrange("p k b -> p (k b)"), ALU.mult))
            chain(dve.tensor_tensor(soft_in[:, 0:32], m0, b_gn[:, 0].rearrange("p k b -> p (k b)"), ALU.add))
            for q in range(2):
                chain(dve.tensor_tensor(tmp_gn[:, 1 + q, 0:32], ends[:, q].rearrange("p k b -> p (k b)"), a1, ALU.mult))
            chain(dve.tensor_tensor(tmp_gn[:, 3, 0:32], tmp_gn[:, 1, 0:32], tmp_gn[:, 2, 0:32], ALU.max))
            dve.tensor_tensor(soft_in[:, 32:64], tmp_gn[:, 3, 0:32], b_gn[:, 1].rearrange("p k b -> p (k b)"),
                              ALU.add).then_inc(logit_ready, 1)
            dve.wait_ge(logit_turned, 1)
            of_group = lambda v: v.rearrange("p (g c) -> p g c", c=CG)
            wide = lambda v: v.unsqueeze(2).to_broadcast([64, NG, CG])
            chain(dve.tensor_reduce(soft_s[:, 0, :], of_group(misc[0:64, 0:P]), AX.X, ALU.max))
            dve.tensor_tensor(of_group(soft_t[:, 0, :]), of_group(misc[0:64, 0:P]), wide(soft_s[:, 0, :]),
                              ALU.subtract).then_inc(logit_sub, 1)
            dve.wait_ge(logit_exp, 1)
            chain(dve.tensor_reduce(soft_s[:, 0, :], of_group(soft_t[:, 1, :]), AX.X, ALU.add))
            chain(dve.reciprocal(soft_s[:, 1, :], soft_s[:, 0, :]))
            dve.tensor_tensor(of_group(soft_t[:, 0, :]), of_group(soft_t[:, 1, :]), wide(soft_s[:, 1, :]),
                              ALU.mult).then_inc(soft_ready, 1)
            dve.wait_ge(soft_turned, 1)
            chain(dve.tensor_copy(flat(soft[:]), misc[:, P:P + 64]))
            for r in range(2):
                chain(dve.tensor_tensor(coef[:, r], soft[:, 1 - r], a_gn[:, r], ALU.mult))
                chain(dve.tensor_tensor(shift[:, r], soft[:, 1 - r], b_gn[:, r], ALU.mult))
            dve.tensor_tensor(shift[:, 0], shift[:, 0], shift[:, 1], ALU.add).then_inc(shift_ready, 1)
            dve.wait_ge(shift_psum, 1)
            chain(dve.tensor_copy(shift[:, 1].rearrange("p k b -> p (k b)"), misc[:, 256:256 + KC * NB]))

            def masks(i, j):
                dve.wait_ge(mix_psum[j], i)
                for r in range(2):
                    for k in range(KC):
                        last = dve.tensor_scalar(mix[:, j, r, k], in_group[:], coef[:, r, k, bass.ds(2 * i + j, 1)],
                                                 None, ALU.mult)
                last.then_inc(mix_ready[j], 1)

            masks(0, 0)
            masks(0, 1)

            def gate_units(i, more):
                for j in range(2):
                    dve.wait_ge(mix_sig[j], i + 1)
                    dve.tensor_tensor(sig_mix[:, j], sig_mix[:, j], g[:, :, bass.ds((2 * i + j) * L, L)],
                                      ALU.mult).then_inc(mix_out[j], 1)
                if more:
                    masks(i + 1, 0)
                    masks(i + 1, 1)
                for j in range(2):
                    dve.wait_ge(mix_turned[j], i + 1)
                    t = tok[:, bass.ds(4 * i + 2 * j, UT), :].rearrange("p h c -> p (h c)")
                    dve.tensor_tensor(t, t, turn[j][:], ALU.add).then_inc(mix_added[j], 1)
                for j in range(2):
                    dve.wait_ge(mix_added[j], i + 1)
                    tile_stats(1, i, j)

            with dve.Fori(0, HB - 1) as i:
                gate_units(i, True)
            gate_units(HB - 1, False)
            dve.wait_ge(stats, NT * 2)

            def route(f):
                s = 2 * f + 1
                deviations(s, C, 1e-5)
                with dve.Fori(0, HB) as i:
                    for j in range(2):
                        norm(s, i, j)
                    for j in range(2):
                        dve.wait_ge(rows_hi[j], HB * f + i + 1)
                        at = rows[:, bass.ds(4 * i + 2 * j, UT), :]
                        dve.scalar_tensor_tensor(at[:, :, C:2 * C], xn[:, j], XSCALE, at[:, :, 0:C], ALU.mult, ALU.subtract
                                                 ).then_inc(rows_ready[j], 1)
                for j in range(2):
                    dve.wait_ge(xt_used[j], HB * s)
                    dve.wait_ge(rows_ready[j], HB * (f + 1))
                over_e = lambda v: v.unsqueeze(2).to_broadcast([P, NT, E])
                over_t = lambda v: v.unsqueeze(1).to_broadcast([P, NT, E])
                logits = yb[:, 0:NT * E].rearrange("p (t e) -> p t e", e=E)
                if f == 0:
                    chain(dve.tensor_copy(lg, logits))
                else:
                    dve.wait_ge(gates_loaded, 16 * 2)
                    chain(dve.tensor_tensor(lg, logits, over_t(gate_b[:]), ALU.add))
                chain(dve.tensor_reduce(red[:, 0, :], lg, AX.X, ALU.max))
                dve.tensor_tensor(lg, lg, over_e(red[:, 0, :]), ALU.subtract).then_inc(exp_in[f], 1)
                dve.wait_ge(exp_out[f], 1)
                chain(dve.tensor_reduce(red[:, 0, :], ex, AX.X, ALU.add))
                chain(dve.reciprocal(red[:, 1, :], red[:, 0, :]))
                chain(dve.tensor_tensor(ex, ex, over_e(red[:, 1, :]), ALU.mult))
                for k, hot in enumerate((hot1, hot2)):
                    chain(dve.tensor_reduce(top[:, k, :], ex, AX.X, ALU.max))
                    chain(dve.tensor_tensor(eq, ex, over_e(top[:, k, :]), ALU.is_equal))
                    chain(dve.tensor_tensor(eq, eq, over_t(rank[:]), ALU.mult))
                    chain(dve.tensor_reduce(red[:, 0, :], eq, AX.X, ALU.max))
                    chain(dve.tensor_tensor(hot, eq, over_e(red[:, 0, :]), ALU.is_equal))
                    if k == 0:
                        chain(dve.scalar_tensor_tensor(ex, hot, -2.0, ex, ALU.mult, ALU.add))
                dve.tensor_tensor(hots16[:], hot1, hot2, ALU.add).then_inc(hots_ready[f], 1)
                if f == 0:
                    chain(dve.tensor_tensor(red[:, 0, :], top[:, 0, :], top[:, 1, :], ALU.add))
                    chain(dve.tensor_scalar(red[:, 0, :], red[:, 0, :], 1e-8, None, ALU.add))
                    chain(dve.reciprocal(red[:, 1, :], red[:, 0, :]))
                    for k in range(2):
                        chain(dve.tensor_tensor(top[:, 2 + k, :], top[:, k, :], red[:, 1, :], ALU.mult))
                else:
                    chain(dve.tensor_copy(top[:, 2:4, :], top[:, 0:2, :]))
                dve.wait_ge(counts_psum[f], 1)
                pre = misc[:, 0:NT * E].rearrange("p (t e) -> p t e", e=E)
                chain(dve.tensor_copy(tot, misc[:, NT * E:2 * NT * E].rearrange("p (t e) -> p t e", e=E)))
                chain(dve.memset(eq, 1.0))
                for e in range(E):
                    last = dve.tensor_tensor_scan(incl[:, :, e], eq[:, :, e], tot[:, :, e], 0.0, ALU.mult, ALU.add)
                chain(last)
                need, base = per_e[:, 1, :], per_e[:, 2, :]
                chain(dve.tensor_scalar(per_e[:, 0, :], incl[:, NT - 1, :], TILE - 1.0, None, ALU.add))
                chain(dve.tensor_copy(int_e[:, 0, :], per_e[:, 0, :]))
                chain(dve.tensor_scalar(int_e[:, 1, :], int_e[:, 0, :], 8, None, ALU.logical_shift_right))
                chain(dve.tensor_copy(per_e[:, 3, :], int_e[:, 1, :]))
                chain(dve.tensor_scalar(need, per_e[:, 3, :], 1.0, None, ALU.max))
                chain(dve.tensor_tensor_scan(per_e[:, 0, :], eq[:, 0, :], need, 0.0, ALU.mult, ALU.add))
                chain(dve.memset(bounds[:, 0:1], 0))
                chain(dve.tensor_copy(bounds[:, 1:E + 1], per_e[:, 0, :]))
                chain(dve.tensor_tensor(base, per_e[:, 0, :], need, ALU.subtract))
                chain(dve.tensor_scalar(per_e[:, 3, :], base, float(TILE), None, ALU.mult))
                chain(dve.tensor_tensor(slot_f, incl, tot, ALU.subtract))
                chain(dve.tensor_tensor(slot_f, slot_f, pre, ALU.add))
                chain(dve.tensor_tensor(slot_f, slot_f, over_t(per_e[:, 3, :]), ALU.add))
                for k, hot in enumerate((hot1, hot2)):
                    chain(dve.tensor_tensor(eq, slot_f, hot, ALU.mult))
                    chain(dve.tensor_reduce(red[:, k, :], eq, AX.X, ALU.add))
                dve.tensor_copy(slots[:], red[:]).then_inc(slots_ready[f], 1)

            def peaks(f, e, i, j):
                loads, parts = ((3, 3), (2, 2))[f]
                dve.wait_ge(stage_loaded[f][j], 16 * loads * (i + 1))
                at = lambda v: v[:, bass.ds(e, 1), :].rearrange("p a m -> p (a m)")
                stage = (stage0, stage1)[f]
                last = dve.tensor_reduce(at(peak)[:, 0:parts], stage[:, j], AX.X, ALU.max, apply_absolute_value=True)
                if f == 1:
                    last = dve.tensor_reduce(at(peak)[:, 2:3], b1_t[:, bass.ds(e, 1), :].rearrange("p a c -> p (a c)"),
                                             AX.X, ALU.max, apply_absolute_value=True)
                last.then_inc(peak_ready[f], 1)
                dve.wait_ge(peak_spread[f], e + 1)
                dve.tensor_scalar(at(pw).bitcast(U32), at(peak_all).bitcast(U32), 0x7F800000, None, ALU.bitwise_and
                                  ).then_inc(pw_step[f], 1)
                dve.wait_ge(pw_step[f], 3 * e + 1)
                dve.tensor_scalar(at(pw), at(pw), 2.0 ** -40, None, ALU.max).then_inc(pw_step[f], 1)
                dve.wait_ge(pw_step[f], 3 * e + 2)
                dve.reciprocal(at(inv), at(pw)).then_inc(pw_step[f], 1)
                dve.wait_ge(pw_step[f], 3 * e + 3)
                dve.tensor_scalar(at(scl), at(inv), BIG, None, ALU.mult).then_inc(w_scale[f], 1)
                dve.wait_ge(w_scale[f], e + 1)

            def lows0(e):
                for q in range(6):
                    m, k = divmod(q, 2)
                    dve.wait_ge(w_hi[0], 6 * e + q + 1)
                    if m < 2:
                        to, hi = ((w1_s, w3_s)[m][:, bass.ds(e, 1), k, s_, :].rearrange("p a n -> p (a n)") for s_ in (1, 0))
                        src = zb[q][:]
                    else:
                        to, hi = (w2_s[:, bass.ds(e, 1), 2 * k:2 * k + 2, s_, :].rearrange("p a c n -> p (a c) n") for s_ in (1, 0))
                        src = turn[k][:].rearrange("p (c n) -> p c n", c=2)
                    last = dve.scalar_tensor_tensor(to, src, scl[:, bass.ds(e, 1), m:m + 1].rearrange("p a b -> p (a b)"),
                                                    hi, ALU.mult, ALU.subtract)
                last.then_inc(w_lo[0], 1)

            def lows1(e, j):
                for m, (w, c) in enumerate(((v1_s, KC), (v2_s, 8))):
                    dve.wait_ge(w_hi[1], 2 * e + m + 1)
                    to, hi = (w[:, bass.ds(e, 1), :, s_, :].rearrange("p a c n -> p (a c) n") for s_ in (1, 0))
                    last = dve.scalar_tensor_tensor(to, stage1[:, j, m].rearrange("p (c n) -> p c n", c=c),
                                                    scl[:, bass.ds(e, 1), m:m + 1].rearrange("p a b -> p (a b)"),
                                                    hi, ALU.mult, ALU.subtract)
                last.then_inc(w_lo[1], 1)

            def factors(f):
                p = [pw[:, :, m] for m in range(3)]
                if f == 0:
                    chain(dve.tensor_scalar(fac[:, 0], p[0], 2.0 ** -24, None, ALU.mult))
                    chain(dve.tensor_scalar(fac[:, 1], inv[:, :, 0], 2.0 ** -27, None, ALU.mult))
                    chain(dve.scalar_tensor_tensor(per_e[:, 0], p[0], 2.0 ** -11, p[1], ALU.mult, ALU.mult))
                    last = dve.tensor_tensor(fac[:, 2], per_e[:, 0], p[2], ALU.mult)
                else:
                    chain(dve.tensor_scalar(fac[:, 0], p[0], 2.0 ** -24, None, ALU.mult))
                    chain(dve.scalar_tensor_tensor(per_e[:, 0], p[2], 2.0 ** -8, p[0], ALU.mult, ALU.max))
                    chain(dve.reciprocal(per_e[:, 1], per_e[:, 0]))
                    chain(dve.tensor_scalar(fac[:, 1], per_e[:, 1], 2.0 ** 5, None, ALU.mult))
                    last = dve.scalar_tensor_tensor(fac[:, 2], per_e[:, 0], 2.0 ** -19, p[1], ALU.mult, ALU.mult)
                last.then_inc(fac_ready[f], 1)
                dve.wait_ge(fac_ready[f], 1)

            def experts(f):
                halves = FH[f] // (2 * P)
                edges = [dve.value_load(bounds[0:1, e:e + 1], min_val=0, max_val=TILES) for e in range(E + 1)]
                if f == 1:
                    dve.wait_ge(late_loaded, 16)
                for e in range(E):
                    with dve.Fori(edges[e], edges[e + 1]) as n:
                        for h in range(halves):
                            dve.wait_ge(silu_done[f], halves * n + h + 1)
                            to_hi, to_lo = (v[:, 2 * h:2 * h + 2].rearrange("p c n -> p (c n)") for v in (hid_hi, hid_lo))
                            if f == 0:
                                dve.scalar_tensor_tensor(hid[:, h], zb[2 * h + 1][:], fac[:, 1, e:e + 1], gate_act[:, h],
                                                         ALU.mult, ALU.mult).then_inc(hid_ready, 1)
                                dve.wait_ge(hi_ready[f], halves * n + h + 1)
                                dve.tensor_tensor(to_lo, hid[:, h], to_hi, ALU.subtract).then_inc(lo_ready[f], 1)
                            else:
                                dve.tensor_scalar(to_hi, gate_act[:, h], fac[:, 1, e:e + 1], None, ALU.mult
                                                  ).then_inc(hi_ready[f], 1)
                                dve.wait_ge(hi_ready[f], halves * n + h + 1)
                                dve.scalar_tensor_tensor(to_lo, gate_act[:, h], fac[:, 1, e:e + 1], to_hi, ALU.mult, ALU.subtract
                                                         ).then_inc(lo_ready[f], 1)
                        if f == 1:
                            dve.wait_ge(y_ready[f], n + 1)
                            dve.wait_ge(y_stored[f], 16 * n)
                            dve.scalar_tensor_tensor(y_rows, yb[:].rearrange("p (g c) -> p g c", g=2), fac[:, 2, e:e + 1],
                                                     b2_all[:, e].unsqueeze(1).to_broadcast([P, 2, C]), ALU.mult, ALU.add
                                                     ).then_inc(y_copied[f], 1)

            def combine(f, i, q, to):
                t = 4 * i + q
                y = (gath0, gath1)[f][q]
                row = tok[:, bass.ds(t, 1), :].rearrange("p a c -> p (a c)")
                w = lambda k: top[:, 2 + k, bass.ds(t, 1)]
                dve.wait_ge(y_gathered[q], 32 * (HB * f + i + 1))
                dve.scalar_tensor_tensor(row, y[:, 0], w(0), row, ALU.mult, ALU.add).then_inc(y_half[f], 1)
                dve.wait_ge(y_half[f], t + 1)
                return dve.scalar_tensor_tensor(row if to is None else to, y[:, 1], w(1), row, ALU.mult, ALU.add)

            route(0)
            with dve.Fori(0, E // 2) as i:
                for j in range(2):
                    peaks(0, 2 * i + j, i, j)
                    lows0(2 * i + j)
            dve.wait_ge(w_lo[0], E)
            factors(0)
            experts(0)
            with dve.Fori(0, E // 2) as i:
                for j in range(2):
                    peaks(1, 2 * i + j, i, j)
                    lows1(2 * i + j, j)
            dve.wait_ge(w_lo[1], E)
            factors(1)
            dve.memset(ones_row, 1.0).then_inc(ones_set, 1)
            with dve.Fori(0, NT // 4) as i:
                for q in range(4):
                    combine(0, i, q, None).then_inc(y_used[q], 1)
                for q in range(4):
                    dve.wait_ge(y_used[q], i + 1)
                    t = 4 * i + q
                    dve.bn_stats(st[:, bass.ds(t, 1), :].rearrange("p a b -> p (a b)"),
                                 tok[:, bass.ds(t, 1), :].rearrange("p a b -> p (a b)")).then_inc(stats, 1)
            dve.wait_ge(stats, NT * 3)
            deviations(2, C, 1e-6)
            with dve.Fori(0, HB) as i:
                for j in range(2):
                    norm(2, i, j)
                for j in range(2):
                    dve.wait_ge(conv_psum[j], i + 1)
                    t = tok[:, bass.ds(4 * i + 2 * j, UT), :].rearrange("p h c -> p (h c)")
                    dve.tensor_tensor(t, t, zb[j][:], ALU.add).then_inc(conv_added[j], 1)
                for j in range(2):
                    dve.wait_ge(conv_added[j], i + 1)
                    tile_stats(3, i, j)
            dve.wait_ge(stats, NT * 4)
            route(1)
            experts(1)
            with dve.Fori(0, NT // 4) as i:
                for j in range(2):
                    dve.wait_ge(fin_turned[j], i)
                    for h in range(UT):
                        last = combine(1, i, 2 * j + h, xn[:, j, h])
                        last.then_inc(y_used[2 * j + h], 1)


_INS = ["x", "L0_conv_conv_w", "L0_conv_conv_b", "L0_conv_gn_w", "L0_conv_gn_b", "L0_ffn_gate_w", "L0_ffn_w1",
        "L0_ffn_w2", "L0_ffn_w3", "L1_conv_weight", "L1_conv_bias", "L1_ffn_gate_w", "L1_ffn_gate_b", "L1_ffn_w1",
        "L1_ffn_b1", "L1_ffn_w2", "L1_ffn_b2"]


def kernel(**inputs):
    import numpy as _np
    import concourse.bacc as _bacc
    from concourse import mybir as _mybir
    from concourse.bass_utils import run_bass_kernel_spmd as _run

    nc = _bacc.Bacc("TRN2", target_bir_lowering=False, num_devices=1)
    shape = inputs["x"].shape
    arrays, args = {}, []
    for name in _INS:
        a = _np.ascontiguousarray(inputs[name])
        if name == "x":
            a = a.reshape(NB, C, L)
        arrays[f"in_{name}_dram"] = a
        args.append(nc.dram_tensor(f"in_{name}_dram", a.shape, _mybir.dt.from_np(a.dtype), kind="ExternalInput").ap())
    args.append(nc.dram_tensor("out_dram", (NB, C, L), _mybir.dt.float32, kind="ExternalOutput").ap())
    bass_metaformer(nc, *args)
    r = _run(nc, [arrays], core_ids=[0])
    return r.results[0]["out_dram"].reshape(shape)
```

```python
from contextlib import ExitStack

import concourse.bass as bass
from concourse import mybir

ALU = mybir.AluOpType
ACT = mybir.ActivationFunctionType
AX = mybir.AxisListType
F32 = mybir.dt.float32
F16 = mybir.dt.float16
I32 = mybir.dt.int32
U32 = mybir.dt.uint32

P = 128
NB, C, HW = 16, 256, 16
L = HW * HW
KC = C // P
HB = NB // 2
UT = L // P
NT = NB * UT
CG = 8
NG = P // CG
E = 8
FH = (512, 1024)
TILE = 256
TILES = (2 * NB * L + E * TILE) // TILE
XSCALE = 1024.0
BIG = 2.0 ** 14


def bass_metaformer(nc, x, conv_w, conv_b, gn_w, gn_b, gate0, w1, w2, w3, weight, bias,
                    gate1, gate1_b, v1, b1, v2, b2, out):
    ctx = ExitStack()
    with ctx:
        def sb(name, shape, dt=F32):
            return ctx.enter_context(nc.sbuf_tensor(name, shape, dt))

        def sem(name):
            return ctx.enter_context(nc.semaphore(name))

        def sem2(name):
            return [sem(f"{name}_{j}") for j in range(2)]

        sorted_x = nc.dram_tensor("sorted_x", ((TILES + 1) * TILE, 2 * C), F16, kind="Internal").ap()
        sorted_y = nc.dram_tensor("sorted_y", (TILES * TILE, C), F32, kind="Internal").ap()

        bank = [ctx.enter_context(nc.psum_tensor(f"bank{n}", [P, 512], F32)) for n in range(8)]
        turn = bank[0:2]
        zb = bank[2:6]
        yb = bank[6]
        misc = bank[7]

        tok = sb("tok", [P, NT, C])
        region = sb("region", [P, 8192])
        wreg = sb("wreg", [P, 32768])
        line = region[:, 0:2048].rearrange("p (r k b l) -> p r k b l", r=2, k=KC, b=NB)
        sig = region[:, 2048:4096].rearrange("p (r k b l) -> p r k b l", r=2, k=KC, b=NB)
        rows = region[:, :].bitcast(F16).rearrange("p (t c) -> p t c", t=NT)
        gate_act = region[:, 0:2048].rearrange("p (h n) -> p h n", h=4)
        hid_hi = region[:, 2048:3072].bitcast(F16).rearrange("p (c n) -> p c n", n=TILE)
        hid_lo = region[:, 3072:4096].bitcast(F16).rearrange("p (c n) -> p c n", n=TILE)
        hid = region[:, 5632:6656].rearrange("p (h n) -> p h n", h=2)
        b2_all = region[:, 5632:7680].rearrange("p (e c) -> p e c", e=E)
        x_rows = region[:, 4096:4608].bitcast(F16).rearrange("p (g c) -> p g c", g=2)
        x_cols = region[:, 4608:5120].bitcast(F16).rearrange("p (k s n) -> p k s n", k=KC, s=2)
        y_rows = region[:, 5120:5632].rearrange("p (g c) -> p g c", g=2)
        stage1 = region[:, :].rearrange("p (j m n) -> p j m n", j=2, m=2)
        g = wreg[:, 0:8192].rearrange("p (k n) -> p k n", k=KC)
        gated = wreg[:, 8192:24576].rearrange("p (r k n) -> p r k n", r=2, k=KC)
        w1_s = wreg[:, 0:8192].bitcast(F16).rearrange("p (e k s n) -> p e k s n", e=E, k=KC, s=2)
        w3_s = wreg[:, 8192:16384].bitcast(F16).rearrange("p (e k s n) -> p e k s n", e=E, k=KC, s=2)
        w2_s = wreg[:, 16384:24576].bitcast(F16).rearrange("p (e c s n) -> p e c s n", e=E, c=4, s=2)
        stage0 = wreg[:, 24576:30720].rearrange("p (j m n) -> p j m n", j=2, m=3)
        scan1 = wreg[:, 24576:32768].rearrange("p (j m n) -> p j m n", j=2, m=2)
        v1_s = wreg[:, 0:16384].bitcast(F16).rearrange("p (e k s n) -> p e k s n", e=E, k=KC, s=2)
        v2_s = wreg[:, 16384:32768].bitcast(F16).rearrange("p (e c s n) -> p e c s n", e=E, c=8, s=2)

        x_in = region[:, 4096:5120].rearrange("p (j k n) -> p j k n", j=2, k=KC)
        mix = region[:, 5120:6144].rearrange("p (j r k n) -> p j r k n", j=2, r=2, k=KC)
        mix_flat = region[:, 5120:6144]
        sig_mix = region[:, 6144:7168].rearrange("p (j k n) -> p j k n", j=2, k=KC)
        own = iter((region[:, a:b] for a, b in [(7168 + 64 * n, 7232 + 64 * n) for n in range(7)]))
        four = lambda v: v.rearrange("p (r k b) -> p r k b", r=2, k=KC)
        coef, a_gn, b_gn, soft, shift, ends = (four(next(own)) for _ in range(6))
        soft_in = next(own)
        soft_t = region[0:64, 7616:7872].rearrange("p (a n) -> p a n", a=2)
        soft_s = region[0:64, 7872:7904].rearrange("p (a n) -> p a n", a=2)
        in_group = region[:, 7904:8032]
        conv_bd = region[:, 8032:8160]
        xn = sb("xn", [P, 2, UT, C])
        xt = sb("xt", [P, 2, KC, L])
        ident = sb("ident", [P, P])
        ident16 = sb("ident16", [P, P], F16)
        ones16 = sb("ones16", [P, P], F16)
        before16 = sb("before16", [P, P], F16)
        small8 = sb("small8", [CG, CG + 3])
        repeat8 = mix_flat[0:CG, 0:P]
        small = sb("small", [P, CG + 3])
        st_lg = sb("st_lg", [P, NT * 10])
        st = st_lg[:, 0:NT * 6].rearrange("p (t s) -> p t s", s=6)
        tmp = st_lg[:, NT * 6:].rearrange("p (q t) -> p q t", q=4)
        logits = st_lg[:, 0:NT * E].rearrange("p (t e) -> p t e", e=E)
        st_gn = xt[:, 0].rearrange("p k n -> p (k n)")[:, 0:384].rearrange("p (n s) -> p n s", s=6)
        conv1_nat = xn[:, 0].rearrange("p a c -> p (a c)").rearrange("p (q i) -> p q i", q=KC)
        gate0_nat = xt[0:E, 1].rearrange("p k n -> p (k n)")[:, 0:C]
        b1_nat = xt[0:64, 1].rearrange("p k n -> p (k n)")[:, C:C + P]
        gath0 = [xn[:, 0], xn[:, 1], xt[:, 0], xt[:, 1]]
        gath1 = [wreg[:, 512 * n:512 * n + 512].rearrange("p (a c) -> p a c", a=2) for n in range(4)]
        quart = [v[:, j, h] for v in (xn, xt) for j in range(2) for h in range(2)]
        lg, ex, hot1, hot2, eq, slot_f, incl, tot = (q.rearrange("p (t e) -> p t e", e=E) for q in quart)
        hots16 = sb("hots16", [P, NT, E], F16)
        conv1_wt = sb("conv1_wt", [P, KC, C])
        bias_rows = region[:, 0:C]
        gate_w = sb("gate_w", [P, 2, KC, E])
        gate_b = sb("gate_b", [P, E])
        rank = sb("rank", [P, E])
        top = sb("top", [P, 4, NT])
        red = sb("red", [P, 2, NT])
        per_e = sb("per_e", [P, 4, E])
        int_e = sb("int_e", [P, 2, E], I32)
        bounds = sb("bounds", [P, E + 1], I32)
        slots = sb("slots", [P, 2, NT], U32)
        b1_t = sb("b1_t", [P, E, 8])
        peak = sb("peak", [P, E, 3])
        peak_all = sb("peak_all", [P, E, 3])
        pw = sb("pw", [P, E, 3])
        inv = sb("inv", [P, E, 3])
        scl = sb("scl", [P, E, 3])
        fac = sb("fac", [P, 3, E])
        mean, var, rstd = (sb(name, [P, NT]) for name in ("mean", "var", "rstd"))
        wide = xt[:, 1].rearrange("p k n -> p (k n)")
        tmp_gn = wide[:, 0:256].rearrange("p (q n) -> p q n", q=4)
        mean_gn, var_gn, rstd_gn = (wide[:, 256 + 64 * q:320 + 64 * q] for q in range(3))

        step = sem("vector_step")
        consts = sem("consts")
        params = sem("params")

        x_loaded, x_turned, x_copied = sem2("x_loaded"), sem2("x_turned"), sem2("x_copied")
        stats = sem("stats")
        var_ready = [sem(f"var_ready{s}") for s in range(5)]
        sd_ready = [sem(f"sd_ready{s}") for s in range(5)]
        xn_ready, xn_turned, xt_ready, xt_used = sem2("xn_ready"), sem2("xn_turned"), sem2("xt_ready"), sem2("xt_used")
        bd_ready, lines_ready, gates_psum, sig_ready = sem("bd_ready"), sem("lines_ready"), sem("gates_psum"), sem("sig_ready")
        gated_mid, gated_ready, gn_stats = sem("gated_mid"), sem("gated_ready"), sem("gn_stats")
        logit_ready, logit_turned, logit_sub, logit_exp = sem("logit_ready"), sem("logit_turned"), sem("logit_sub"), sem("logit_exp")
        soft_ready, soft_turned, shift_ready, shift_psum = sem("soft_ready"), sem("soft_turned"), sem("shift_ready"), sem("shift_psum")
        coef_ready = sem("coef_ready")
        mix_ready, mix_psum, mix_sig, mix_out = sem2("mix_ready"), sem2("mix_psum"), sem2("mix_sig"), sem2("mix_out")
        mix_turned, mix_added = sem2("mix_turned"), sem2("mix_added")
        fin_turned, fin_copied, fin_stored = sem2("fin_turned"), sem2("fin_copied"), sem2("fin_stored")

        def pairs(eng, body, first=0):
            body(first)
            with eng.Fori(first + 1, HB) as i:
                body(i)

        def free(eng, semaphore, count):
            if not isinstance(count, int) or count > 0:
                eng.wait_ge(semaphore, count)

        zeros = wreg[:, 30720:32768]
        ZX = (TILES + 1) * TILE * 2 * C // P
        ZY = TILES * TILE * C // P
        ZERO_DMAS = -(-ZX // 4096) + -(-ZY // 2048)
        zeroed, zero_stored = sem("zeroed"), sem("zero_stored")
        nat_loaded, nat_turned, nat_copied, bias_loaded = sem("nat_loaded"), sem("nat_turned"), sem("nat_copied"), sem("bias_loaded")
        small_psum, small_ready = sem("small_psum"), sem("small_ready")
        gates_loaded = sem("gates_loaded")
        two = lambda name: [sem(f"{name}{f}") for f in range(2)]
        rows_hi, rows_ready = sem2("rows_hi"), sem2("rows_ready")
        logits_kept, exp_in, exp_out = sem2("logits_kept"), two("exp_in"), two("exp_out")
        hots_ready, counts_psum, slots_ready, scattered = two("hots_ready"), two("counts_psum"), two("slots_ready"), two("scattered")
        y_used = [sem(f"y_used_{n}") for n in range(4)]
        y_gathered = [sem(f"y_gathered_{n}") for n in range(4)]
        y_half = two("y_half")
        peak_ready, peak_spread = sem("peak_ready"), two("peak_spread")
        scan_loaded, scanned = sem2("scan_loaded"), sem("scanned")
        stage_loaded = [sem2(f"stage_loaded{f}") for f in range(2)]
        w_scale, w_turned, w_hi, w_lo = two("w_scale"), sem("w_turned"), two("w_hi"), two("w_lo")
        pw_step = two("pw_step")
        fac_ready = two("fac_ready")
        xr_loaded, xr_turned, xc_ready = two("xr_loaded"), two("xr_turned"), two("xc_ready")
        z_ready, silu_done, hid_ready, hi_ready, lo_ready = two("z_ready"), two("silu_done"), sem("hid_ready"), two("hi_ready"), two("lo_ready")
        y_ready, y_copied, y_free = two("y_ready"), two("y_copied"), two("y_free")
        bias_added, conv_added = sem2("bias_added"), sem2("conv_added")

        block = ctx.enter_context(nc.Block())

        @block.sync
        def _(sp):
            def load_images(i):
                for j in range(2):
                    free(sp, x_turned[j], i)
                    sp.dma_start(x_in[:, j], x[bass.ds(2 * i + j, 1)].rearrange("a (k p) l -> p (a k) l", p=P)
                                 ).then_inc(x_loaded[j], 16)
                if isinstance(i, int):
                    sp.dma_start(conv1_nat, weight.rearrange("(q p) i -> p q i", p=P)).then_inc(nat_loaded, 16)
                    sp.dma_start(gate0_nat, gate0).then_inc(nat_loaded, 16)
                    sp.dma_start(b1_nat, b1.rearrange("e (c n) -> (e c) n", n=P)).then_inc(nat_loaded, 16)

            pairs(sp, load_images)
            sp.dma_start(small8[:, 0:CG], conv_w.rearrange("o i -> i o"), allow_slow_non_contiguous=True).then_inc(params, 16)
            for c, v in enumerate((conv_b, gn_w, gn_b)):
                sp.dma_start(small8[:, CG + c:CG + c + 1], v.rearrange("(c a) -> c a", a=1)).then_inc(params, 16)
            sp.dma_start(gate_w[:, 1], gate1.rearrange("(k p) e -> p k e", p=P)).then_inc(gates_loaded, 16)
            sp.wait_ge(zeroed, 1)
            zx = sorted_x.rearrange("(p a) c -> p (a c)", p=P)
            for a in range(0, ZX, 4096):
                n = min(4096, ZX - a)
                sp.dma_start(zx[:, a:a + n], zeros.bitcast(F16)[:, 0:n]).then_inc(zero_stored, 16)
            zy = sorted_y.rearrange("(p a) c -> p (a c)", p=P)
            for a in range(0, ZY, 2048):
                n = min(2048, ZY - a)
                sp.dma_start(zy[:, a:a + n], zeros[:, 0:n]).then_inc(zero_stored, 16)

            def load_stage0(e, j):
                for m, w in enumerate((w1, w3)):
                    sp.dma_start(stage0[:, j, m].rearrange("p (c d) -> p c d", c=4),
                                 w[bass.ds(e, 1)].rearrange("a (c p) d -> p (a c) d", p=P)).then_inc(stage_loaded[0][j], 16)
                sp.dma_start(stage0[:, j, 2].rearrange("p (c h) -> p c h", c=KC),
                             w2[bass.ds(e, 1)].rearrange("a (c p) h -> p (a c) h", p=P)).then_inc(stage_loaded[0][j], 16)

            def load_stage1(e, j):
                sp.dma_start(stage1[:, j, 0].rearrange("p (c h) -> p c h", c=KC),
                             v1[bass.ds(e, 1)].rearrange("a (c p) h -> p (a c) h", p=P)).then_inc(stage_loaded[1][j], 16)
                sp.dma_start(stage1[:, j, 1].rearrange("p (c d) -> p c d", c=8),
                             v2[bass.ds(e, 1)].rearrange("a (c p) d -> p (a c) d", p=P)).then_inc(stage_loaded[1][j], 16)

            def load_rows(tile):
                return sp.dma_start(x_rows, sorted_x[bass.ds(tile * TILE, TILE)].rearrange("(g p) c -> p g c", p=P))

            for f, load in enumerate((load_stage0, load_stage1)):
                if f == 1:
                    sp.wait_ge(y_free[0], 16 * total + 16)
                for j in range(2):
                    load(j, j)
                with sp.Fori(1, E // 2) as i:
                    for j in range(2):
                        sp.wait_ge(w_lo[f], 2 * i + j - 1)
                        load(2 * i + j, j)
                if f == 1:
                    sp.wait_ge(w_lo[1], E)
                    sp.dma_start(bias_rows, bias.rearrange("c a -> (c a)").partition_broadcast(P)).then_inc(bias_loaded, 16)
                sp.wait_ge(scattered[f], 16 * 2 * NT)
                total = sp.value_load(bounds[0:1, E:E + 1], min_val=E, max_val=TILES)
                if f == 0:
                    sp.dma_start(gate_b[:], gate1_b.partition_broadcast(P)).then_inc(y_free[0], 16)
                else:
                    sp.dma_start(b2_all, b2.partition_broadcast(P)).then_inc(y_free[1], 16)
                load_rows(0).then_inc(xr_loaded[f], 16)
                with sp.Fori(0, total) as n:
                    sp.wait_ge(xr_turned[f], n + 1)
                    load_rows(n + 1).then_inc(xr_loaded[f], 16)
                    sp.wait_ge(y_copied[f], n + 1)
                    sp.dma_start(sorted_y[bass.ds(n * TILE, TILE)].rearrange("(g p) c -> p g c", p=P), y_rows
                                 ).then_inc(y_free[f], 16)

        CONSTS = 12

        @block.gpsimd
        def _(pool):
            ones = zeros[:, 0:P]
            nc.gpsimd.memset(ones, 1.0).then_inc(consts, 1)
            nc.gpsimd.memset(ident[:], 0.0).then_inc(consts, 1)
            nc.gpsimd.memset(zeros[:, P:2 * P], 0.0).then_inc(consts, 1)
            nc.gpsimd.memset(ones16[:], 1.0).then_inc(consts, 1)
            nc.gpsimd.iota(int_e[:, 0, :], [[-1, E]], base=E, channel_multiplier=0).then_inc(consts, 1)
            pool.wait_ge(consts, 5)
            nc.gpsimd.affine_select(out=ident[:], in_=ident[:], compare_op=ALU.not_equal, fill=1.0, base=0,
                                    pattern=[[-1, P]], channel_multiplier=1).then_inc(consts, 1)
            nc.gpsimd.affine_select(out=before16[:], in_=ones16[:], compare_op=ALU.is_gt, fill=0.0, base=0,
                                    pattern=[[1, P]], channel_multiplier=-1).then_inc(consts, 1)
            grp = in_group.rearrange("p (g c) -> p g c", c=CG)
            nc.gpsimd.affine_select(out=grp, in_=ones.rearrange("p (g c) -> p g c", c=CG),
                                    compare_op=ALU.is_ge, fill=0.0, base=0,
                                    pattern=[[-CG, NG], [0, CG]], channel_multiplier=1).then_inc(consts, 1)
            nc.gpsimd.tensor_copy(rank[:], int_e[:, 0, :]).then_inc(consts, 1)
            pool.wait_ge(consts, 9)
            rep8 = repeat8.rearrange("p (g c) -> p g c", c=CG)
            nc.gpsimd.affine_select(out=rep8, in_=zeros[0:CG, P:2 * P].rearrange("p (g c) -> p g c", c=CG),
                                    compare_op=ALU.not_equal, fill=1.0, base=0, pattern=[[0, NG], [1, CG]],
                                    channel_multiplier=-1).then_inc(consts, 1)
            nc.gpsimd.tensor_copy(ident16[:], ident[:]).then_inc(consts, 1)
            nc.gpsimd.affine_select(out=grp, in_=grp, compare_op=ALU.is_ge, fill=0.0, base=CG - 1,
                                    pattern=[[CG, NG], [0, CG]], channel_multiplier=-1).then_inc(consts, 1)
            pool.wait_ge(consts, CONSTS)
            nc.gpsimd.memset(zeros, 0.0).then_inc(zeroed, 1)

            def scatter(f, t, k):
                nc.gpsimd.indirect_dma_start(sorted_x, bass.IndirectOffsetOnAxis(ap=slots[:, k, t:t + 1], axis=0),
                                             rows[:, t, :], None).then_inc(scattered[f], 16)

            def gather(f, t):
                free(pool, y_used[t % 4], HB * f + t // 4)
                to = (gath0, gath1)[f][t % 4]
                for k in range(2):
                    nc.gpsimd.indirect_dma_start(to[:, k, :], None, sorted_y,
                                                 bass.IndirectOffsetOnAxis(ap=slots[:, k, t:t + 1], axis=0)
                                                 ).then_inc(y_gathered[t % 4], 16)

            def scan_second_mixture():
                def load(e):
                    pool.dma_start(scan1[:, e % 2, 0].rearrange("p (c h) -> p c h", c=KC),
                                   v1[e].rearrange("(c p) h -> p c h", p=P)).then_inc(scan_loaded[e % 2], 16)
                    pool.dma_start(scan1[:, e % 2, 1].rearrange("p (c d) -> p c d", c=8),
                                   v2[e].rearrange("(c p) d -> p c d", p=P)).then_inc(scan_loaded[e % 2], 16)

                pool.wait_ge(w_lo[0], E)
                for e in range(2):
                    load(e)
                for e in range(E - 2):
                    pool.wait_ge(scanned, e + 1)
                    load(e + 2)
                pool.wait_ge(scanned, E)
                nc.gpsimd.partition_all_reduce(peak_all[:].rearrange("p e m -> p (e m)"), peak[:].rearrange("p e m -> p (e m)"),
                                               P, bass.bass_isa.ReduceOp.max).then_inc(peak_spread[1], 1)

            for f in range(2):
                pool.wait_ge(slots_ready[f], 1)
                for j in range(2):
                    pool.wait_ge(rows_ready[j], HB * (f + 1))
                if f == 0:
                    pool.wait_ge(zero_stored, 16 * ZERO_DMAS)
                for n in range(E):
                    if f == 0:
                        pool.wait_ge(peak_ready, n + 1)
                        nc.gpsimd.partition_all_reduce(peak_all[:, n], peak[:, n], P, bass.bass_isa.ReduceOp.max
                                                       ).then_inc(peak_spread[0], 1)
                    for t in range(4 * n, 4 * n + 4):
                        for k in range(2):
                            scatter(f, t, k)
                total = pool.value_load(bounds[0:1, E:E + 1], min_val=E, max_val=TILES)
                if f == 0:
                    scan_second_mixture()
                with pool.Fori(total - 1, total) as n:
                    pool.wait_ge(xc_ready[f], n + 2)
                    pool.wait_ge(y_free[f], 16 * (n + 2))
                for t in range(NT):
                    gather(f, t)
                if f == 0:
                    pool.wait_ge(bias_loaded, 16)
                    with pool.Fori(0, HB) as i:
                        for j in range(2):
                            pool.wait_ge(xn_ready[j], HB * 2 + i + 1)
                            t = tok[:, bass.ds(4 * i + 2 * j, UT), :]
                            nc.gpsimd.tensor_tensor(t, t, bias_rows.unsqueeze(1).to_broadcast([P, UT, C]), ALU.add
                                                    ).then_inc(bias_added[j], 1)


        @block.tensor
        def _(pe):
            def norm_turn(s, i, j):
                pe.wait_ge(xn_ready[j], HB * s + i + 1)
                free(pe, xt_ready[j], HB * s + i)
                to = turn[j][:].rearrange("p (k n) -> p k n", k=KC)
                for k in range(KC):
                    for h in range(UT):
                        last = pe.transpose(to[:, k, h * P:(h + 1) * P], xn[:, j, h, k * P:(k + 1) * P], ident[:])
                last.then_inc(xn_turned[j], 1)

            def turn_images(i):
                for j in range(2):
                    pe.wait_ge(x_loaded[j], 16 * (i + 1))
                    free(pe, x_copied[j], i)
                    to = turn[j][:].rearrange("p (h c) -> p h c", h=UT)
                    for h in range(UT):
                        for k in range(KC):
                            last = pe.transpose(to[:, h, k * P:(k + 1) * P], x_in[:, j, k, h * P:(h + 1) * P], ident[:])
                    last.then_inc(x_turned[j], 1)

            pe.wait_ge(consts, CONSTS)
            pairs(pe, turn_images)
            pe.wait_ge(nat_loaded, 16 * 3)
            for q in range(KC):
                for k in range(KC):
                    pe.transpose(zb[0][:, k * C + q * P:k * C + (q + 1) * P], conv1_nat[:, q, k * P:(k + 1) * P], ident[:])
            for k in range(KC):
                pe.transpose(zb[1][:, k * E:(k + 1) * E], gate0_nat[:, k * P:(k + 1) * P], ident[0:E, 0:E])
            pe.transpose(zb[1][:, 64:128], b1_nat, ident[0:64, 0:64]).then_inc(nat_turned, 1)
            pe.wait_ge(params, 16 * 4)
            pe.matmul(misc[:, 0:CG + 3], repeat8, small8[:], start=True, stop=True).then_inc(small_psum, 1)

            def turn_normed(i):
                for j in range(2):
                    norm_turn(0, i, j)

            pairs(pe, turn_normed)
            pe.wait_ge(bd_ready, 1)
            for r in range(2):
                for k in range(KC):
                    pe.wait_ge(lines_ready, 2 * (r * KC + k) + 2)
                    pe.matmul(zb[2 * r + k][:], conv_bd[:], line[:, r, k].rearrange("p b l -> p (b l)"),
                              start=True, stop=True).then_inc(gates_psum, 1)
            pe.wait_ge(logit_ready, 1)
            pe.transpose(misc[0:64, 0:P], soft_in[:], ident[:]).then_inc(logit_turned, 1)
            pe.wait_ge(soft_ready, 1)
            pe.transpose(misc[:, P:P + 64], soft_t[:, 0, :], ident[0:64, 0:64]).then_inc(soft_turned, 1)
            pe.wait_ge(shift_ready, 1)
            pe.matmul(misc[:, 256:256 + KC * NB], in_group[:], shift[:, 0].rearrange("p k b -> p (k b)"),
                      start=True, stop=True).then_inc(shift_psum, 1)
            def mix_units(i):
                for j in range(2):
                    pe.wait_ge(mix_ready[j], i + 1)
                    free(pe, mix_sig[j], i)
                    for k in range(KC):
                        for r in range(2):
                            last = pe.matmul(zb[j][:, k * L:(k + 1) * L], mix[:, j, r, k],
                                             gated[:, r, k, bass.ds((2 * i + j) * L, L)], start=(r == 0), stop=(r == 1))
                    last.then_inc(mix_psum[j], 1)
                for j in range(2):
                    pe.wait_ge(mix_out[j], i + 1)
                    free(pe, mix_added[j], i)
                    to = turn[j][:].rearrange("p (h c) -> p h c", h=UT)
                    for h in range(UT):
                        for k in range(KC):
                            last = pe.transpose(to[:, h, k * P:(k + 1) * P], sig_mix[:, j, k, h * P:(h + 1) * P], ident[:])
                    last.then_inc(mix_turned[j], 1)

            pairs(pe, mix_units)

            def router(f, i, j):
                pe.wait_ge(xt_ready[j], HB * (2 * f + 1) + i + 1)
                free(pe, logits_kept[j], HB * f + i)
                for h in range(UT):
                    for k in range(KC):
                        last = pe.matmul(zb[j][:, h * E:(h + 1) * E], xt[:, j, k, h * P:(h + 1) * P],
                                         gate_w[:, f, k], start=(k == 0), stop=(k == KC - 1))
                last.then_inc(xt_used[j], 1)

            def routing(f):
                def units(i):
                    for j in range(2):
                        norm_turn(2 * f + 1, i, j)
                    for j in range(2):
                        router(f, i, j)

                pairs(pe, units)
                pe.wait_ge(hots_ready[f], 1)
                flat_hots = hots16[:].rearrange("p t e -> p (t e)")
                pe.matmul(misc[:, 0:NT * E], before16[:], flat_hots, start=True, stop=True)
                pe.matmul(misc[:, NT * E:2 * NT * E], ones16[:], flat_hots, start=True, stop=True).then_inc(counts_psum[f], 1)

            def stage_turns(i, j):
                e = 2 * i + j
                pe.wait_ge(stage_loaded[0][j], 48 * (i + 1))
                free(pe, w_lo[0], e)
                for m in range(2):
                    for k in range(KC):
                        for c in range(4):
                            last = pe.transpose(zb[2 * m + k][:, c * P:(c + 1) * P],
                                                stage0[:, j, m, c * C + k * P:c * C + (k + 1) * P], ident[:])
                        last.then_inc(w_turned, 1)
                for c in range(4):
                    for k in range(KC):
                        last = pe.transpose(turn[c // 2][:, (c % 2) * C + k * P:(c % 2) * C + (k + 1) * P],
                                            stage0[:, j, 2, k * FH[0] + c * P:k * FH[0] + (c + 1) * P], ident[:])
                    if c % 2:
                        last.then_inc(w_turned, 1)

            x_turn16 = turn[0][:].bitcast(F16).rearrange("p (k s n) -> p k s n", k=KC, s=2)

            def turn_rows(f, tile):
                pe.wait_ge(xr_loaded[f], 16 * (tile + 1))
                for k in range(KC):
                    for s_ in range(2):
                        for r in range(2):
                            last = pe.transpose(x_turn16[:, k, s_, r * P:(r + 1) * P],
                                                x_rows[:, r, s_ * C + k * P:s_ * C + (k + 1) * P], ident16[:])
                last.then_inc(xr_turned[f], 1)

            PARTS = ((0, 0), (0, 1), (1, 0))

            def up(f, e, h):
                ws = ((w1_s, zb[2 * (h % 2)]), (w3_s, zb[2 * (h % 2) + 1])) if f == 0 else ((v1_s, zb[h]),)
                for w, z in ws:
                    for c in (2 * h, 2 * h + 1):
                        to = z[:, (c % 2) * TILE:(c % 2 + 1) * TILE]
                        for k in range(KC):
                            for ws_, xs_ in PARTS:
                                last = pe.matmul(to, w[:, e, k, ws_, c * P:(c + 1) * P], x_cols[:, k, xs_, :],
                                                 start=(k == 0 and ws_ + xs_ == 0), stop=(k == KC - 1 and ws_ == 1))
                    last.then_inc(z_ready[f], 1)

            def down(f, e, tile, h, halves):
                w = (w2_s, v2_s)[f]
                for c in (2 * h, 2 * h + 1):
                    if f == 0:
                        pe.wait_ge(lo_ready[0], 2 * halves * tile + c + 1)
                    elif c == 2 * h:
                        pe.wait_ge(lo_ready[1], halves * tile + h + 1)
                    for r in range(2):
                        for hs, ws_ in PARTS:
                            lhs = (hid_hi, hid_lo)[hs]
                            first = c == 0 and r == 0 and hs + ws_ == 0
                            end = c == 2 * halves - 1 and hs == 1
                            last = pe.matmul(yb[:, r * C:(r + 1) * C], lhs[:, c, r * P:(r + 1) * P], w[:, e, c, ws_, :],
                                             start=first, stop=end, skip_group_check=True)
                if h == halves - 1:
                    last.then_inc(y_ready[f], 1)

            def experts(f):
                halves = FH[f] // (2 * P)
                pe.wait_ge(w_lo[f], E)
                pe.wait_ge(fac_ready[f], 1)
                turn_rows(f, 0)
                edges = [pe.value_load(bounds[0:1, e:e + 1], min_val=0, max_val=TILES) for e in range(E + 1)]
                for e in range(E):
                    with pe.Fori(edges[e], edges[e + 1]) as n:
                        pe.wait_ge(xc_ready[f], n + 1)
                        for h in range(halves):
                            up(f, e, h)
                        for h in range(halves - 1):
                            down(f, e, n, h, halves)
                        turn_rows(f, n + 1)
                        down(f, e, n, halves - 1, halves)

            routing(0)
            for j in range(2):
                stage_turns(0, j)
            with pe.Fori(1, E // 2) as i:
                for j in range(2):
                    stage_turns(i, j)
            experts(0)
            def mix_channels(i, j):
                pe.wait_ge(xt_ready[j], HB * 2 + i + 1)
                free(pe, conv_added[j], i)
                for h in range(UT):
                    for k in range(KC):
                        last = pe.matmul(zb[j][:, h * C:(h + 1) * C], xt[:, j, k, h * P:(h + 1) * P], conv1_wt[:, k],
                                         start=(k == 0), stop=(k == KC - 1))
                last.then_inc(xt_used[j], 1)

            def turn_ahead(i):
                for j in range(2):
                    norm_turn(2, i + 1, j)
                    mix_channels(i, j)

            for j in range(2):
                norm_turn(2, 0, j)
            turn_ahead(0)
            with pe.Fori(1, HB - 1) as i:
                turn_ahead(i)
            for j in range(2):
                mix_channels(HB - 1, j)
            pe.wait_ge(gates_loaded, 16)
            routing(1)
            experts(1)
            def turn_result(i):
                for j in range(2):
                    for h in range(UT):
                        pe.wait_ge(y_used[2 * j + h], HB + i + 1)
                    free(pe, fin_copied[j], i)
                    to = turn[j][:].rearrange("p (k n) -> p k n", k=KC)
                    for k in range(KC):
                        for h in range(UT):
                            last = pe.transpose(to[:, k, h * P:(h + 1) * P], xn[:, j, h, k * P:(k + 1) * P], ident[:])
                    last.then_inc(fin_turned[j], 1)

            pairs(pe, turn_result)

        @block.scalar
        def _(act):
            def deviation(s):
                act.wait_ge(var_ready[s], 1)
                r, v = (rstd[:], var[:]) if s < 4 else (rstd_gn, var_gn)
                act.activation(r, v, ACT.Sqrt).then_inc(sd_ready[s], 1)

            def copy_images(i):
                for j in range(2):
                    act.wait_ge(x_turned[j], i + 1)
                    act.activation(tok[:, bass.ds(4 * i + 2 * j, UT), :].rearrange("p h c -> p (h c)"),
                                   turn[j][:], ACT.Copy).then_inc(x_copied[j], 1)

            pairs(act, copy_images)
            act.wait_ge(nat_turned, 1)
            act.activation(conv1_wt[:].rearrange("p k c -> p (k c)"), zb[0][:], ACT.Copy).then_inc(nat_copied, 1)
            act.activation(gate_w[:, 0].rearrange("p k e -> p (k e)"), zb[1][:, 0:KC * E], ACT.Copy).then_inc(nat_copied, 1)
            act.activation(b1_t[:].rearrange("p e c -> p (e c)"), zb[1][:, 64:128], ACT.Copy).then_inc(nat_copied, 1)
            act.wait_ge(small_psum, 1)
            act.activation(small[:], misc[:, 0:CG + 3], ACT.Copy).then_inc(small_ready, 1)
            deviation(0)
            with act.Fori(0, HB) as i:
                for j in range(2):
                    act.wait_ge(xn_turned[j], i + 1)
                    act.activation(g[:, :, bass.ds((2 * i + j) * L, L)], turn[j][:].rearrange("p (k n) -> p k n", k=KC),
                                   ACT.Copy).then_inc(xt_ready[j], 1)
            act.wait_ge(small_ready, 1)
            for r in range(2):
                for k in range(KC):
                    act.wait_ge(gates_psum, r * KC + k + 1)
                    act.activation(sig[:, r, k].rearrange("p b l -> p (b l)"), zb[2 * r + k][:], ACT.Sigmoid,
                                   bias=small[:, CG:CG + 1], scale=(1.0 / HW if r == 0 else 1.0)).then_inc(sig_ready, 1)
            deviation(4)
            act.wait_ge(logit_sub, 1)
            act.activation(soft_t[:, 1, :], soft_t[:, 0, :], ACT.Exp).then_inc(logit_exp, 1)
            def mix_gates(i):
                for j in range(2):
                    act.wait_ge(mix_psum[j], i + 1)
                    free(act, mix_turned[j], i)
                    for k in range(KC):
                        last = act.activation(sig_mix[:, j, k], zb[j][:, k * L:(k + 1) * L], ACT.Sigmoid,
                                              bias=shift[:, 1, k, bass.ds(2 * i + j, 1)])
                    last.then_inc(mix_sig[j], 1)

            pairs(act, mix_gates)

            def to_columns(s, i, j):
                act.wait_ge(xn_turned[j], HB * s + i + 1)
                free(act, xt_used[j], HB * (s - 1) + i)
                act.activation(xt[:, j].rearrange("p k n -> p (k n)"), turn[j][:], ACT.Copy).then_inc(xt_ready[j], 1)

            def route(f):
                deviation(2 * f + 1)
                def units(i):
                    for j in range(2):
                        act.wait_ge(xn_ready[j], HB * (2 * f + 1) + i + 1)
                        act.activation(rows[:, bass.ds(4 * i + 2 * j, UT), 0:C], xn[:, j], ACT.Copy, scale=XSCALE
                                       ).then_inc(rows_hi[j], 1)
                        to_columns(2 * f + 1, i, j)

                pairs(act, units)
                act.wait_ge(exp_in[f], 1)
                act.activation(ex, lg, ACT.Exp).then_inc(exp_out[f], 1)

            def columns16(f, tile):
                act.wait_ge(xr_turned[f], tile + 1)
                act.activation(x_cols.rearrange("p k s n -> p (k s n)"), turn[0][:].bitcast(F16), ACT.Copy
                               ).then_inc(xc_ready[f], 1)

            def experts(f):
                halves = FH[f] // (2 * P)
                columns16(f, 0)
                edges = [act.value_load(bounds[0:1, e:e + 1], min_val=0, max_val=TILES) for e in range(E + 1)]
                act.wait_ge(fac_ready[f], 1)
                for e in range(E):
                    with act.Fori(edges[e], edges[e + 1]) as n:
                        for h in range(halves):
                            if f == 0:
                                act.wait_ge(z_ready[0], 2 * halves * n + 2 * h + 1)
                                act.activation(gate_act[:, h], zb[2 * h][:], ACT.Silu, scale=fac[:, 0, e:e + 1]
                                               ).then_inc(silu_done[f], 1)
                                for c in (2 * h, 2 * h + 1):
                                    act.wait_ge(hid_ready, 2 * halves * n + c + 1)
                                    act.activation(hid_hi[:, c], hid[:, h, (c % 2) * TILE:(c % 2 + 1) * TILE], ACT.Copy
                                                   ).then_inc(hi_ready[f], 1)
                            else:
                                act.wait_ge(z_ready[1], halves * n + h + 1)
                                for c in range(2):
                                    last = act.activation(gate_act[:, h, c * TILE:(c + 1) * TILE], zb[h][:, c * TILE:(c + 1) * TILE],
                                                          ACT.Silu, bias=b1_t[:, e, 2 * h + c:2 * h + c + 1], scale=fac[:, 0, e:e + 1])
                                last.then_inc(silu_done[f], 1)
                        columns16(f, n + 1)
                        if f == 0:
                            act.wait_ge(y_ready[f], n + 1)
                            act.wait_ge(y_free[f], 16 * (n + 1))
                            act.activation(y_rows.rearrange("p g c -> p (g c)"), yb[:], ACT.Copy, scale=fac[:, 2, e:e + 1]
                                           ).then_inc(y_copied[f], 1)

            route(0)
            with act.Fori(0, E // 2) as i:
                for j in range(2):
                    e = 2 * i + j
                    act.wait_ge(w_scale[0], e + 1)
                    for q in range(6):
                        act.wait_ge(w_turned, 6 * e + q + 1)
                        m, k = divmod(q, 2)
                        to = ((w1_s, w3_s)[m][:, bass.ds(e, 1), k, 0, :].rearrange("p a n -> p (a n)") if m < 2 else
                              w2_s[:, bass.ds(e, 1), 2 * k:2 * k + 2, 0, :].rearrange("p a c n -> p (a c) n"))
                        src = zb[q][:] if m < 2 else turn[k][:].rearrange("p (c n) -> p c n", c=2)
                        act.activation(to, src, ACT.Copy, scale=scl[:, bass.ds(e, 1), m:m + 1].rearrange("p a b -> p (a b)")
                                       ).then_inc(w_hi[0], 1)
            experts(0)
            act.wait_ge(w_scale[1], 1)
            with act.Fori(0, E // 2) as i:
                for j in range(2):
                    e = 2 * i + j
                    act.wait_ge(stage_loaded[1][j], 32 * (i + 1))
                    for m, (w, c) in enumerate(((v1_s, KC), (v2_s, 8))):
                        act.activation(w[:, bass.ds(e, 1), :, 0, :].rearrange("p a c n -> p (a c) n"),
                                       stage1[:, j, m].rearrange("p (c n) -> p c n", c=c), ACT.Copy,
                                       scale=scl[:, bass.ds(e, 1), m:m + 1].rearrange("p a b -> p (a b)")).then_inc(w_hi[1], 1)
            deviation(2)
            with act.Fori(0, HB) as i:
                for j in range(2):
                    to_columns(2, i, j)
            route(1)
            experts(1)
            def store_result(i):
                for j in range(2):
                    act.wait_ge(fin_turned[j], i + 1)
                    free(act, fin_stored[j], 16 * i)
                    act.activation(xt[:, j].rearrange("p k n -> p (k n)"), turn[j][:], ACT.Copy).then_inc(fin_copied[j], 1)
                for j in range(2):
                    act.wait_ge(fin_copied[j], i + 1)
                    act.dma_start(out[bass.ds(2 * i + j, 1)].rearrange("a (k p) l -> p (a k) l", p=P), xt[:, j]
                                  ).then_inc(fin_stored[j], 16)

            pairs(act, store_result)
            for j in range(2):
                act.wait_ge(fin_stored[j], 16 * HB)

        @block.vector
        def _(dve):
            done = [0]

            def chain(ins):
                done[0] += 1
                ins.then_inc(step, 1)
                dve.wait_ge(step, done[0])

            def deviations(s, count, eps):
                a, b = (st[:] if s < 4 else st_gn), [(tmp if s < 4 else tmp_gn)[:, q, :] for q in range(4)]
                m, v, r = (mean[:], var[:], rstd[:]) if s < 4 else (mean_gn, var_gn, rstd_gn)
                chain(dve.tensor_tensor(b[0], a[:, :, 1], a[:, :, 4], ALU.add))
                chain(dve.tensor_tensor(b[1], a[:, :, 1], a[:, :, 4], ALU.subtract))
                chain(dve.tensor_tensor(b[2], a[:, :, 2], a[:, :, 5], ALU.add))
                chain(dve.tensor_scalar(m, b[0], 0.5, None, ALU.mult))
                chain(dve.scalar_tensor_tensor(b[3], b[1], 0.25, b[1], ALU.mult, ALU.mult))
                chain(dve.scalar_tensor_tensor(b[0], b[2], 1.0 / count, b[3], ALU.mult, ALU.add))
                dve.tensor_scalar(v, b[0], eps, None, ALU.add).then_inc(var_ready[s], 1)
                dve.wait_ge(sd_ready[s], 1)
                chain(dve.reciprocal(b[1], r))
                chain(dve.tensor_tensor(b[2], b[1], b[1], ALU.mult))
                chain(dve.tensor_tensor(b[3], b[2], v, ALU.mult))
                chain(dve.tensor_scalar(b[0], b[3], -0.5, 1.5, ALU.mult, ALU.add))
                chain(dve.tensor_tensor(r, b[1], b[0], ALU.mult))

            def tile_stats(s, i, j):
                for h in range(UT):
                    t = 4 * i + 2 * j + h
                    dve.bn_stats(st[:, bass.ds(t, 1), :].rearrange("p a b -> p (a b)"),
                                 tok[:, bass.ds(t, 1), :].rearrange("p a b -> p (a b)")).then_inc(stats, 1)

            def norm(s, i, j):
                if s % 2:
                    free(dve, rows_ready[j], HB * (s // 2) + i)
                free(dve, xn_turned[j], HB * s + i)
                for h in range(UT):
                    t = 4 * i + 2 * j + h
                    last = dve.tensor_scalar(xn[:, j, h], tok[:, bass.ds(t, 1), :].rearrange("p a b -> p (a b)"),
                                             mean[:, bass.ds(t, 1)], rstd[:, bass.ds(t, 1)], ALU.subtract, ALU.mult)
                last.then_inc(xn_ready[j], 1)

            with dve.Fori(0, HB) as i:
                for j in range(2):
                    dve.wait_ge(x_copied[j], i + 1)
                    tile_stats(0, i, j)
            dve.wait_ge(stats, NT * 1)
            deviations(0, C, 1e-6)

            def norm_units(i):
                for j in range(2):
                    norm(0, i, j)

            pairs(dve, norm_units)
            dve.wait_ge(small_ready, 1)
            dve.wait_ge(consts, CONSTS)
            dve.tensor_tensor(conv_bd[:].rearrange("p (g c) -> p g c", c=CG), in_group[:].rearrange("p (g c) -> p g c", c=CG),
                              small[:, 0:CG].unsqueeze(1).to_broadcast([P, NG, CG]), ALU.mult).then_inc(bd_ready, 1)
            for j in range(2):
                dve.wait_ge(xt_ready[j], HB)
            for r, op in enumerate((ALU.add, ALU.max)):
                for k in range(KC):
                    v = g[:, k, :].rearrange("p (b h w) -> p b h w", b=NB, h=HW)
                    dve.tensor_reduce(line[:, r, k, :, 0:HW], v, AX.X, op).then_inc(lines_ready, 1)
                    dve.tensor_reduce(line[:, r, k, :, HW:2 * HW], v.rearrange("p b h w -> p b w h"), AX.X, op).then_inc(lines_ready, 1)
            for r in range(2):
                for k in range(KC):
                    dve.wait_ge(sig_ready, r * KC + k + 1)
                    v = g[:, k, :].rearrange("p (b h w) -> p b h w", b=NB, h=HW)
                    o = gated[:, r, k, :].rearrange("p (b h w) -> p b h w", b=NB, h=HW)
                    rows_g = sig[:, r, k, :, 0:HW].unsqueeze(3).to_broadcast([P, NB, HW, HW])
                    cols_g = sig[:, r, k, :, HW:2 * HW].unsqueeze(2).to_broadcast([P, NB, HW, HW])
                    dve.tensor_tensor(o, v, rows_g, ALU.mult).then_inc(gated_mid, 1)
                    dve.wait_ge(gated_mid, r * KC + k + 1)
                    dve.tensor_tensor(o, o, cols_g, ALU.mult).then_inc(gated_ready, 1)
            dve.wait_ge(nat_copied, 3)
            for r in range(2):
                for k in range(KC):
                    dve.wait_ge(gated_ready, r * KC + k + 1)
                    with dve.Fori(0, NB) as b:
                        dve.bn_stats(st_gn[:, bass.ds((r * KC + k) * NB + b, 1), :].rearrange("p a b -> p (a b)"),
                                     gated[:, r, k, bass.ds(b * L, L)]).then_inc(gn_stats, 1)
            for k in range(KC):
                v = gated[:, 1, k, :].rearrange("p (b n) -> p b n", b=NB)
                dve.tensor_reduce(ends[:, 0, k], v, AX.X, ALU.max)
                chain(dve.tensor_reduce(ends[:, 1, k], v, AX.X, ALU.min))
            dve.wait_ge(gn_stats, 64)
            deviations(4, L, 1e-5)
            flat = lambda v: v.rearrange("p r k b -> p (r k b)")
            chain(dve.tensor_scalar(flat(a_gn[:]), rstd_gn, small[:, CG + 1:CG + 2], None, ALU.mult))
            chain(dve.tensor_tensor(tmp_gn[:, 0, :], mean_gn, flat(a_gn[:]), ALU.mult))
            chain(dve.tensor_scalar(flat(b_gn[:]), tmp_gn[:, 0, :], -1.0, small[:, CG + 2:CG + 3], ALU.mult, ALU.add))
            m0, a1 = tmp_gn[:, 0, 0:32], a_gn[:, 1].rearrange("p k b -> p (k b)")
            chain(dve.tensor_tensor(m0, mean_gn[:, 0:32], a_gn[:, 0].rearrange("p k b -> p (k b)"), ALU.mult))
            chain(dve.tensor_tensor(soft_in[:, 0:32], m0, b_gn[:, 0].rearrange("p k b -> p (k b)"), ALU.add))
            for q in range(2):
                chain(dve.tensor_tensor(tmp_gn[:, 1 + q, 0:32], ends[:, q].rearrange("p k b -> p (k b)"), a1, ALU.mult))
            chain(dve.tensor_tensor(tmp_gn[:, 3, 0:32], tmp_gn[:, 1, 0:32], tmp_gn[:, 2, 0:32], ALU.max))
            dve.tensor_tensor(soft_in[:, 32:64], tmp_gn[:, 3, 0:32], b_gn[:, 1].rearrange("p k b -> p (k b)"),
                              ALU.add).then_inc(logit_ready, 1)
            dve.wait_ge(logit_turned, 1)
            of_group = lambda v: v.rearrange("p (g c) -> p g c", c=CG)
            wide = lambda v: v.unsqueeze(2).to_broadcast([64, NG, CG])
            chain(dve.tensor_reduce(soft_s[:, 0, :], of_group(misc[0:64, 0:P]), AX.X, ALU.max))
            dve.tensor_tensor(of_group(soft_t[:, 0, :]), of_group(misc[0:64, 0:P]), wide(soft_s[:, 0, :]),
                              ALU.subtract).then_inc(logit_sub, 1)
            dve.wait_ge(logit_exp, 1)
            chain(dve.tensor_reduce(soft_s[:, 0, :], of_group(soft_t[:, 1, :]), AX.X, ALU.add))
            chain(dve.reciprocal(soft_s[:, 1, :], soft_s[:, 0, :]))
            dve.tensor_tensor(of_group(soft_t[:, 0, :]), of_group(soft_t[:, 1, :]), wide(soft_s[:, 1, :]),
                              ALU.mult).then_inc(soft_ready, 1)
            dve.wait_ge(soft_turned, 1)
            chain(dve.tensor_copy(flat(soft[:]), misc[:, P:P + 64]))
            for r in range(2):
                chain(dve.tensor_tensor(coef[:, r], soft[:, 1 - r], a_gn[:, r], ALU.mult))
                chain(dve.tensor_tensor(shift[:, r], soft[:, 1 - r], b_gn[:, r], ALU.mult))
            dve.tensor_tensor(shift[:, 0], shift[:, 0], shift[:, 1], ALU.add).then_inc(shift_ready, 1)
            dve.wait_ge(shift_psum, 1)
            chain(dve.tensor_copy(shift[:, 1].rearrange("p k b -> p (k b)"), misc[:, 256:256 + KC * NB]))

            def masks(i, j):
                free(dve, mix_psum[j], i)
                for r in range(2):
                    for k in range(KC):
                        last = dve.tensor_scalar(mix[:, j, r, k], in_group[:], coef[:, r, k, bass.ds(2 * i + j, 1)],
                                                 None, ALU.mult)
                last.then_inc(mix_ready[j], 1)

            masks(0, 0)
            masks(0, 1)

            def gate_units(i, more):
                for j in range(2):
                    dve.wait_ge(mix_sig[j], i + 1)
                    dve.tensor_tensor(sig_mix[:, j], sig_mix[:, j], g[:, :, bass.ds((2 * i + j) * L, L)],
                                      ALU.mult).then_inc(mix_out[j], 1)
                if more:
                    masks(i + 1, 0)
                    masks(i + 1, 1)
                for j in range(2):
                    dve.wait_ge(mix_turned[j], i + 1)
                    t = tok[:, bass.ds(4 * i + 2 * j, UT), :].rearrange("p h c -> p (h c)")
                    dve.tensor_tensor(t, t, turn[j][:], ALU.add).then_inc(mix_added[j], 1)
                for j in range(2):
                    dve.wait_ge(mix_added[j], i + 1)
                    tile_stats(1, i, j)

            with dve.Fori(0, HB - 1) as i:
                gate_units(i, True)
            gate_units(HB - 1, False)
            dve.wait_ge(stats, NT * 2)

            def route(f):
                s = 2 * f + 1
                deviations(s, C, 1e-5)

                def keep_logits(i):
                    for j in range(2):
                        dve.wait_ge(xt_used[j], HB * (s - 1) + i + 1)
                        dve.tensor_copy(logits[:, bass.ds(4 * i + 2 * j, UT), :],
                                        zb[j][:, 0:UT * E].rearrange("p (t e) -> p t e", e=E)).then_inc(logits_kept[j], 1)

                def units(i, before=None):
                    for j in range(2):
                        norm(s, i, j)
                    if before is not None:
                        keep_logits(before)
                    for j in range(2):
                        dve.wait_ge(rows_hi[j], HB * f + i + 1)
                        at = rows[:, bass.ds(4 * i + 2 * j, UT), :]
                        dve.scalar_tensor_tensor(at[:, :, C:2 * C], xn[:, j], XSCALE, at[:, :, 0:C], ALU.mult, ALU.subtract
                                                 ).then_inc(rows_ready[j], 1)

                units(0)
                with dve.Fori(0, HB - 1) as i:
                    units(i + 1, i)
                keep_logits(HB - 1)
                for j in range(2):
                    dve.wait_ge(logits_kept[j], HB * (f + 1))
                    dve.wait_ge(rows_ready[j], HB * (f + 1))
                over_e = lambda v: v.unsqueeze(2).to_broadcast([P, NT, E])
                over_t = lambda v: v.unsqueeze(1).to_broadcast([P, NT, E])
                if f == 0:
                    chain(dve.tensor_copy(lg, logits))
                else:
                    dve.wait_ge(y_free[0], 16)
                    chain(dve.tensor_tensor(lg, logits, over_t(gate_b[:]), ALU.add))
                chain(dve.tensor_reduce(red[:, 0, :], lg, AX.X, ALU.max))
                dve.tensor_tensor(lg, lg, over_e(red[:, 0, :]), ALU.subtract).then_inc(exp_in[f], 1)
                dve.wait_ge(exp_out[f], 1)
                chain(dve.tensor_reduce(red[:, 0, :], ex, AX.X, ALU.add))
                chain(dve.reciprocal(red[:, 1, :], red[:, 0, :]))
                chain(dve.tensor_tensor(ex, ex, over_e(red[:, 1, :]), ALU.mult))
                for k, hot in enumerate((hot1, hot2)):
                    chain(dve.tensor_reduce(top[:, k, :], ex, AX.X, ALU.max))
                    chain(dve.tensor_tensor(eq, ex, over_e(top[:, k, :]), ALU.is_equal))
                    chain(dve.tensor_tensor(eq, eq, over_t(rank[:]), ALU.mult))
                    chain(dve.tensor_reduce(red[:, 0, :], eq, AX.X, ALU.max))
                    chain(dve.tensor_tensor(hot, eq, over_e(red[:, 0, :]), ALU.is_equal))
                    if k == 0:
                        chain(dve.scalar_tensor_tensor(ex, hot, -2.0, ex, ALU.mult, ALU.add))
                dve.tensor_tensor(hots16[:], hot1, hot2, ALU.add).then_inc(hots_ready[f], 1)
                if f == 0:
                    chain(dve.tensor_tensor(red[:, 0, :], top[:, 0, :], top[:, 1, :], ALU.add))
                    chain(dve.tensor_scalar(red[:, 0, :], red[:, 0, :], 1e-8, None, ALU.add))
                    chain(dve.reciprocal(red[:, 1, :], red[:, 0, :]))
                    for k in range(2):
                        chain(dve.tensor_tensor(top[:, 2 + k, :], top[:, k, :], red[:, 1, :], ALU.mult))
                else:
                    chain(dve.tensor_copy(top[:, 2:4, :], top[:, 0:2, :]))
                dve.wait_ge(counts_psum[f], 1)
                pre = misc[:, 0:NT * E].rearrange("p (t e) -> p t e", e=E)
                chain(dve.tensor_copy(tot, misc[:, NT * E:2 * NT * E].rearrange("p (t e) -> p t e", e=E)))
                chain(dve.memset(eq, 1.0))
                for e in range(E):
                    last = dve.tensor_tensor_scan(incl[:, :, e], eq[:, :, e], tot[:, :, e], 0.0, ALU.mult, ALU.add)
                chain(last)
                need, base = per_e[:, 1, :], per_e[:, 2, :]
                chain(dve.tensor_scalar(per_e[:, 0, :], incl[:, NT - 1, :], TILE - 1.0, None, ALU.add))
                chain(dve.tensor_copy(int_e[:, 0, :], per_e[:, 0, :]))
                chain(dve.tensor_scalar(int_e[:, 1, :], int_e[:, 0, :], 8, None, ALU.logical_shift_right))
                chain(dve.tensor_copy(per_e[:, 3, :], int_e[:, 1, :]))
                chain(dve.tensor_scalar(need, per_e[:, 3, :], 1.0, None, ALU.max))
                chain(dve.tensor_tensor_scan(per_e[:, 0, :], eq[:, 0, :], need, 0.0, ALU.mult, ALU.add))
                chain(dve.memset(bounds[:, 0:1], 0))
                chain(dve.tensor_copy(bounds[:, 1:E + 1], per_e[:, 0, :]))
                chain(dve.tensor_tensor(base, per_e[:, 0, :], need, ALU.subtract))
                chain(dve.tensor_scalar(per_e[:, 3, :], base, float(TILE), None, ALU.mult))
                chain(dve.tensor_tensor(slot_f, incl, tot, ALU.subtract))
                chain(dve.tensor_tensor(slot_f, slot_f, pre, ALU.add))
                chain(dve.tensor_tensor(slot_f, slot_f, over_t(per_e[:, 3, :]), ALU.add))
                for k, hot in enumerate((hot1, hot2)):
                    chain(dve.tensor_tensor(eq, slot_f, hot, ALU.mult))
                    chain(dve.tensor_reduce(red[:, k, :], eq, AX.X, ALU.add))
                dve.tensor_copy(slots[:], red[:]).then_inc(slots_ready[f], 1)

            def peaks(e, i, j):
                dve.wait_ge(stage_loaded[0][j], 16 * 3 * (i + 1))
                at = peak[:, bass.ds(e, 1), :].rearrange("p a m -> p (a m)")
                dve.tensor_reduce(at, stage0[:, j], AX.X, ALU.max, apply_absolute_value=True).then_inc(peak_ready, 1)
                scales(0, e + 1, 3 * e, lambda v: v[:, bass.ds(e, 1), :].rearrange("p a m -> p (a m)"))

            def scales(f, spread, steps, at):
                dve.wait_ge(peak_spread[f], spread)
                dve.tensor_scalar(at(pw).bitcast(U32), at(peak_all).bitcast(U32), 0x7F800000, None, ALU.bitwise_and
                                  ).then_inc(pw_step[f], 1)
                dve.wait_ge(pw_step[f], steps + 1)
                dve.tensor_scalar(at(pw), at(pw), 2.0 ** -40, None, ALU.max).then_inc(pw_step[f], 1)
                dve.wait_ge(pw_step[f], steps + 2)
                dve.reciprocal(at(inv), at(pw)).then_inc(pw_step[f], 1)
                dve.wait_ge(pw_step[f], steps + 3)
                dve.tensor_scalar(at(scl), at(inv), BIG, None, ALU.mult).then_inc(w_scale[f], 1)
                dve.wait_ge(w_scale[f], spread)

            def scan1_peaks(e):
                dve.wait_ge(scan_loaded[e % 2], 32 * (e // 2 + 1))
                last = dve.tensor_reduce(peak[:, e, 0:2], scan1[:, e % 2], AX.X, ALU.max, apply_absolute_value=True)
                if e == E - 1:
                    last = dve.tensor_reduce(peak[:, :, 2], b1_t[:], AX.X, ALU.max, apply_absolute_value=True)
                last.then_inc(scanned, 1)

            def lows0(e):
                for q in range(6):
                    m, k = divmod(q, 2)
                    dve.wait_ge(w_hi[0], 6 * e + q + 1)
                    if m < 2:
                        to, hi = ((w1_s, w3_s)[m][:, bass.ds(e, 1), k, s_, :].rearrange("p a n -> p (a n)") for s_ in (1, 0))
                        src = zb[q][:]
                    else:
                        to, hi = (w2_s[:, bass.ds(e, 1), 2 * k:2 * k + 2, s_, :].rearrange("p a c n -> p (a c) n") for s_ in (1, 0))
                        src = turn[k][:].rearrange("p (c n) -> p c n", c=2)
                    last = dve.scalar_tensor_tensor(to, src, scl[:, bass.ds(e, 1), m:m + 1].rearrange("p a b -> p (a b)"),
                                                    hi, ALU.mult, ALU.subtract)
                last.then_inc(w_lo[0], 1)

            def lows1(e, j):
                for m, (w, c) in enumerate(((v1_s, KC), (v2_s, 8))):
                    dve.wait_ge(w_hi[1], 2 * e + m + 1)
                    to, hi = (w[:, bass.ds(e, 1), :, s_, :].rearrange("p a c n -> p (a c) n") for s_ in (1, 0))
                    last = dve.scalar_tensor_tensor(to, stage1[:, j, m].rearrange("p (c n) -> p c n", c=c),
                                                    scl[:, bass.ds(e, 1), m:m + 1].rearrange("p a b -> p (a b)"),
                                                    hi, ALU.mult, ALU.subtract)
                last.then_inc(w_lo[1], 1)

            def factors(f):
                p = [pw[:, :, m] for m in range(3)]
                if f == 0:
                    chain(dve.tensor_scalar(fac[:, 0], p[0], 2.0 ** -24, None, ALU.mult))
                    chain(dve.tensor_scalar(fac[:, 1], inv[:, :, 0], 2.0 ** -27, None, ALU.mult))
                    chain(dve.scalar_tensor_tensor(per_e[:, 0], p[0], 2.0 ** -11, p[1], ALU.mult, ALU.mult))
                    last = dve.tensor_tensor(fac[:, 2], per_e[:, 0], p[2], ALU.mult)
                else:
                    chain(dve.tensor_scalar(fac[:, 0], p[0], 2.0 ** -24, None, ALU.mult))
                    chain(dve.scalar_tensor_tensor(per_e[:, 0], p[2], 2.0 ** -8, p[0], ALU.mult, ALU.max))
                    chain(dve.reciprocal(per_e[:, 1], per_e[:, 0]))
                    chain(dve.tensor_scalar(fac[:, 1], per_e[:, 1], 2.0 ** 5, None, ALU.mult))
                    last = dve.scalar_tensor_tensor(fac[:, 2], per_e[:, 0], 2.0 ** -19, p[1], ALU.mult, ALU.mult)
                last.then_inc(fac_ready[f], 1)
                dve.wait_ge(fac_ready[f], 1)

            def experts(f):
                halves = FH[f] // (2 * P)
                edges = [dve.value_load(bounds[0:1, e:e + 1], min_val=0, max_val=TILES) for e in range(E + 1)]
                for e in range(E):
                    with dve.Fori(edges[e], edges[e + 1]) as n:
                        for h in range(halves):
                            dve.wait_ge(silu_done[f], halves * n + h + 1)
                            to_hi, to_lo = (v[:, 2 * h:2 * h + 2].rearrange("p c n -> p (c n)") for v in (hid_hi, hid_lo))
                            if f == 0:
                                dve.wait_ge(z_ready[0], 2 * halves * n + 2 * h + 2)
                                half = lambda v, c: v[:, (c % 2) * TILE:(c % 2 + 1) * TILE]
                                for c in (2 * h, 2 * h + 1):
                                    dve.scalar_tensor_tensor(half(hid[:, h], c), half(zb[2 * h + 1], c), fac[:, 1, e:e + 1],
                                                             half(gate_act[:, h], c), ALU.mult, ALU.mult).then_inc(hid_ready, 1)
                                for c in (2 * h, 2 * h + 1):
                                    dve.wait_ge(hi_ready[f], 2 * halves * n + c + 1)
                                    dve.tensor_tensor(hid_lo[:, c], half(hid[:, h], c), hid_hi[:, c], ALU.subtract
                                                      ).then_inc(lo_ready[f], 1)
                            else:
                                dve.tensor_scalar(to_hi, gate_act[:, h], fac[:, 1, e:e + 1], None, ALU.mult
                                                  ).then_inc(hi_ready[f], 1)
                                dve.wait_ge(hi_ready[f], halves * n + h + 1)
                                dve.scalar_tensor_tensor(to_lo, gate_act[:, h], fac[:, 1, e:e + 1], to_hi, ALU.mult, ALU.subtract
                                                         ).then_inc(lo_ready[f], 1)
                        if f == 1:
                            dve.wait_ge(y_ready[f], n + 1)
                            dve.wait_ge(y_free[f], 16 * (n + 1))
                            dve.scalar_tensor_tensor(y_rows, yb[:].rearrange("p (g c) -> p g c", g=2), fac[:, 2, e:e + 1],
                                                     b2_all[:, e].unsqueeze(1).to_broadcast([P, 2, C]), ALU.mult, ALU.add
                                                     ).then_inc(y_copied[f], 1)
                    if f == 0:
                        scan1_peaks(e)

            def combine(f, i, q, to):
                t = 4 * i + q
                y = (gath0, gath1)[f][q]
                row = tok[:, bass.ds(t, 1), :].rearrange("p a c -> p (a c)")
                w = lambda k: top[:, 2 + k, bass.ds(t, 1)]
                dve.wait_ge(y_gathered[q], 32 * (HB * f + i + 1))
                dve.scalar_tensor_tensor(row, y[:, 0], w(0), row, ALU.mult, ALU.add).then_inc(y_half[f], 1)
                dve.wait_ge(y_half[f], t + 1)
                return dve.scalar_tensor_tensor(row if to is None else to, y[:, 1], w(1), row, ALU.mult, ALU.add)

            route(0)
            with dve.Fori(0, E // 2) as i:
                for j in range(2):
                    peaks(2 * i + j, i, j)
                    lows0(2 * i + j)
            dve.wait_ge(w_lo[0], E)
            factors(0)
            experts(0)
            scales(1, 1, 0, lambda v: v.rearrange("p e m -> p (e m)"))
            with dve.Fori(0, E // 2) as i:
                for j in range(2):
                    e = 2 * i + j
                    for q in range(4):
                        combine(0, e, q, None).then_inc(y_used[q], 1)
                    dve.wait_ge(stage_loaded[1][j], 32 * (i + 1))
                    lows1(e, j)
                    for q in range(4):
                        dve.wait_ge(y_used[q], e + 1)
                        t = 4 * e + q
                        dve.bn_stats(st[:, bass.ds(t, 1), :].rearrange("p a b -> p (a b)"),
                                     tok[:, bass.ds(t, 1), :].rearrange("p a b -> p (a b)")).then_inc(stats, 1)
            dve.wait_ge(w_lo[1], E)
            factors(1)
            dve.wait_ge(stats, NT * 3)
            deviations(2, C, 1e-6)
            def add_mixed(i):
                for j in range(2):
                    dve.wait_ge(xt_used[j], HB + i + 1)
                    dve.wait_ge(bias_added[j], i + 1)
                    t = tok[:, bass.ds(4 * i + 2 * j, UT), :].rearrange("p h c -> p (h c)")
                    dve.tensor_tensor(t, t, zb[j][:], ALU.add).then_inc(conv_added[j], 1)
                for j in range(2):
                    dve.wait_ge(conv_added[j], i + 1)
                    tile_stats(3, i, j)

            for j in range(2):
                norm(2, 0, j)
            with dve.Fori(0, HB - 1) as i:
                for j in range(2):
                    norm(2, i + 1, j)
                add_mixed(i)
            add_mixed(HB - 1)
            dve.wait_ge(stats, NT * 4)
            route(1)
            experts(1)
            def final_units(i):
                for j in range(2):
                    free(dve, fin_turned[j], i)
                    for h in range(UT):
                        last = combine(1, i, 2 * j + h, xn[:, j, h])
                        last.then_inc(y_used[2 * j + h], 1)

            pairs(dve, final_units)


_INS = ["x", "L0_conv_conv_w", "L0_conv_conv_b", "L0_conv_gn_w", "L0_conv_gn_b", "L0_ffn_gate_w", "L0_ffn_w1",
        "L0_ffn_w2", "L0_ffn_w3", "L1_conv_weight", "L1_conv_bias", "L1_ffn_gate_w", "L1_ffn_gate_b", "L1_ffn_w1",
        "L1_ffn_b1", "L1_ffn_w2", "L1_ffn_b2"]


def kernel(**inputs):
    import numpy as _np
    import concourse.bacc as _bacc
    from concourse import mybir as _mybir
    from concourse.bass_utils import run_bass_kernel_spmd as _run

    nc = _bacc.Bacc("TRN2", target_bir_lowering=False, num_devices=1)
    shape = inputs["x"].shape
    arrays, args = {}, []
    for name in _INS:
        a = _np.ascontiguousarray(inputs[name])
        if name == "x":
            a = a.reshape(NB, C, L)
        arrays[f"in_{name}_dram"] = a
        args.append(nc.dram_tensor(f"in_{name}_dram", a.shape, _mybir.dt.from_np(a.dtype), kind="ExternalInput").ap())
    args.append(nc.dram_tensor("out_dram", (NB, C, L), _mybir.dt.float32, kind="ExternalOutput").ap())
    bass_metaformer(nc, *args)
    r = _run(nc, [arrays], core_ids=[0])
    return r.results[0]["out_dram"].reshape(shape)
```

```python
from contextlib import ExitStack

import concourse.bass as bass
from concourse import mybir

ALU = mybir.AluOpType
ACT = mybir.ActivationFunctionType
AX = mybir.AxisListType
F32 = mybir.dt.float32
F16 = mybir.dt.float16
I32 = mybir.dt.int32
U32 = mybir.dt.uint32

P = 128
NB, C, HW = 16, 256, 16
L = HW * HW
KC = C // P
HB = NB // 2
UT = L // P
NT = NB * UT
CG = 8
NG = P // CG
E = 8
FH = (512, 1024)
TILE = 256
TILES = (2 * NB * L + E * TILE) // TILE
GROUPS = TILES * TILE // P
XSCALE = 1024.0
BIG = 2.0 ** 14


def bass_metaformer(nc, x, conv_w, conv_b, gn_w, gn_b, gate0, w1, w2, w3, weight, bias,
                    gate1, gate1_b, v1, b1, v2, b2, out):
    ctx = ExitStack()
    with ctx:
        def sb(name, shape, dt=F32):
            return ctx.enter_context(nc.sbuf_tensor(name, shape, dt))

        def sem(name):
            return ctx.enter_context(nc.semaphore(name))

        def sem2(name):
            return [sem(f"{name}_{j}") for j in range(2)]

        rows_x = [nc.dram_tensor(f"rows_x{f}", (NT * P, 2 * C), F16, kind="Internal").ap() for f in range(2)]
        rows_y = [nc.dram_tensor(f"rows_y{f}", ((2 * NT + 2) * P, C), F32, kind="Internal").ap() for f in range(2)]

        bank = [ctx.enter_context(nc.psum_tensor(f"bank{n}", [P, 512], F32)) for n in range(8)]
        turn = bank[0:2]
        zb = bank[2:6]
        yb = bank[6]
        misc = bank[7]

        tok = sb("tok", [P, NT, C])
        region = sb("region", [P, 8192])
        wreg = sb("wreg", [P, 32768])
        line = region[:, 0:2048].rearrange("p (r k b l) -> p r k b l", r=2, k=KC, b=NB)
        sig = region[:, 2048:4096].rearrange("p (r k b l) -> p r k b l", r=2, k=KC, b=NB)
        rows = region[:, :].bitcast(F16).rearrange("p (t c) -> p t c", t=NT)
        gate_act = region[:, 0:2048].rearrange("p (h n) -> p h n", h=4)
        hid_hi = region[:, 2048:3072].bitcast(F16).rearrange("p (c n) -> p c n", n=TILE)
        hid_lo = region[:, 3072:4096].bitcast(F16).rearrange("p (c n) -> p c n", n=TILE)
        hid = region[:, 5632:6656].rearrange("p (h n) -> p h n", h=2)
        b2_all = region[:, 5632:7680].rearrange("p (e c) -> p e c", e=E)
        x_rows = region[:, 4096:4608].bitcast(F16).rearrange("p (g c) -> p g c", g=2)
        x_cols = region[:, 4608:5120].bitcast(F16).rearrange("p (k s n) -> p k s n", k=KC, s=2)
        y_rows = region[:, 5120:5632].rearrange("p (g c) -> p g c", g=2)
        stage1 = region[:, :].rearrange("p (j m n) -> p j m n", j=2, m=2)
        g = wreg[:, 0:8192].rearrange("p (k n) -> p k n", k=KC)
        gated = wreg[:, 8192:24576].rearrange("p (r k n) -> p r k n", r=2, k=KC)
        x_in = wreg[:, 16384:24576].rearrange("p (b k n) -> p b k n", b=NB, k=KC)
        w1_s = wreg[:, 0:8192].bitcast(F16).rearrange("p (e k s n) -> p e k s n", e=E, k=KC, s=2)
        w3_s = wreg[:, 8192:16384].bitcast(F16).rearrange("p (e k s n) -> p e k s n", e=E, k=KC, s=2)
        w2_s = wreg[:, 16384:24576].bitcast(F16).rearrange("p (e c s n) -> p e c s n", e=E, c=4, s=2)
        stage0 = wreg[:, 24576:30720].rearrange("p (j m n) -> p j m n", j=2, m=3)
        scan1 = wreg[:, 24576:32768].rearrange("p (j m n) -> p j m n", j=2, m=2)
        v1_s = wreg[:, 0:16384].bitcast(F16).rearrange("p (e k s n) -> p e k s n", e=E, k=KC, s=2)
        v2_s = wreg[:, 16384:32768].bitcast(F16).rearrange("p (e c s n) -> p e c s n", e=E, c=8, s=2)

        mix = region[:, 5120:6144].rearrange("p (j r k n) -> p j r k n", j=2, r=2, k=KC)
        sig_mix = region[:, 6144:7168].rearrange("p (j k n) -> p j k n", j=2, k=KC)
        own = iter((region[:, a:b] for a, b in [(7168 + 64 * n, 7232 + 64 * n) for n in range(7)]))
        four = lambda v: v.rearrange("p (r k b) -> p r k b", r=2, k=KC)
        coef, a_gn, b_gn, soft, shift = (four(next(own)) for _ in range(5))
        ends = next(own)[:, 0:KC * NB].rearrange("p (k b) -> p k b", k=KC)
        soft_in = next(own)
        soft_t = region[0:64, 7616:7872].rearrange("p (a n) -> p a n", a=2)
        soft_s = region[0:64, 7872:7904].rearrange("p (a n) -> p a n", a=2)
        in_group = region[:, 7904:8032]
        conv_bd = region[:, 8032:8160]
        xn = sb("xn", [P, 2, UT, C])
        xt = sb("xt", [P, 2, KC, L])
        ident = sb("ident", [P, P])
        ident16 = sb("ident16", [P, P], F16)
        ones16 = sb("ones16", [P, 2], F16)
        small8 = region[0:CG, 8176:8176 + CG + 3]
        repeat8 = region[0:CG, 5120:5120 + P]
        small = region[:, 8160:8160 + CG + 5]
        st_lg = sb("st_lg", [P, NT * 10])
        st = st_lg[:, 0:NT * 6].rearrange("p (t s) -> p t s", s=6)
        tmp = st_lg[:, NT * 6:].rearrange("p (q t) -> p q t", q=4)
        logits = st_lg[:, 0:NT * E].rearrange("p (t e) -> p t e", e=E)
        st_gn = xt[:, 0].rearrange("p k n -> p (k n)")[:, 0:384].rearrange("p (n s) -> p n s", s=6)
        conv1_nat = xn[:, 0].rearrange("p a c -> p (a c)").rearrange("p (q i) -> p q i", q=KC)
        gate0_nat = xt[0:E, 1].rearrange("p k n -> p (k n)")[:, 0:C]
        b1_nat = xt[0:64, 1].rearrange("p k n -> p (k n)")[:, C:C + P]
        gath0 = [[xn[:, 0], xn[:, 1], xt[:, 0], xt[:, 1]],
                 [wreg[:, 14336 + 512 * n:14848 + 512 * n].rearrange("p (a c) -> p a c", a=2) for n in range(4)]]
        gath1 = [wreg[:, 512 * n:512 * n + 512].rearrange("p (a c) -> p a c", a=2) for n in range(4)]
        quart = [v[:, j, h] for v in (xn, xt) for j in range(2) for h in range(2)]
        ex, hot1, hot2, eq, slot_f, incl, tot = (q.rearrange("p (t e) -> p t e", e=E) for q in quart[1:])
        hots16 = quart[0][:, 0:NT * E // 2].bitcast(F16).rearrange("p (t e) -> p t e", e=E)
        xn_all, xt_all = (v.rearrange("p j a c -> p (j a c)") for v in (xn[:], xt[:]))
        hot_lane = xn_all[:, 0:8 * P // 2].bitcast(F16).rearrange("p (b n) -> p b n", n=P)
        by_choice = lambda v: v.rearrange("p (k t) -> p k t", k=2)
        slot_i, lane_i, group_i = (by_choice(xn_all[:, 512 + 64 * q:576 + 64 * q].bitcast(U32)) for q in range(3))
        lane_f, group_f = (by_choice(xn_all[:, 512 + 64 * q:576 + 64 * q]) for q in range(2))
        id_f = by_choice(xt_all[:, 960:1024])
        hot_group = xt_all[:, 0:8 * GROUPS].bitcast(F16).rearrange("p (b v n) -> p b v n", v=2, n=GROUPS)
        hot_one = xt_all[:, 8 * GROUPS:12 * GROUPS].bitcast(F16).rearrange("p (b n) -> p b n", n=GROUPS)
        pad_f, sum_f, to_f = (xn_all[:, 704 + GROUPS * q:704 + GROUPS * (q + 1)] for q in range(3))
        conv1_wt = sb("conv1_wt", [P, KC, C])
        gate_w = sb("gate_w", [P, 2, KC, E])
        gate_b = sb("gate_b", [P, E])
        rank = sb("rank", [P, E])
        top = sb("top", [P, 4, NT])
        red = sb("red", [P, 2, NT])
        per_e = sb("per_e", [P, 4, E])
        int_e = sb("int_e", [P, 2, E], I32)
        bounds = sb("bounds", [P, E + 1], I32)
        routed = sb("routed", [P, C])
        moves = routed[:, 0:2 * GROUPS + 4].bitcast(U32).rearrange("p (g m) -> p g m", m=2)
        before16 = routed[:, 2 * GROUPS + 4:2 * GROUPS + 4 + P // 2].bitcast(F16)
        bias_rows = routed
        fetch_now, put_now = sb("fetch_now", [P, 2], U32), sb("put_now", [P, 2], U32)
        first_rows = sb("first_rows", [P, 2], U32)
        count16 = sb("count16", [P, P], F16)
        lane = sb("lane", [P, 3])
        b1_t = sb("b1_t", [P, E, 8])
        peak = sb("peak", [P, E, 3])
        peak_all = sb("peak_all", [P, E, 3])
        pw = sb("pw", [P, E, 3])
        inv = sb("inv", [P, E, 3])
        scl = sb("scl", [P, E, 3])
        fac = sb("fac", [P, 3, E])
        mean, var, rstd = (sb(name, [P, NT]) for name in ("mean", "var", "rstd"))
        wide = xt[:, 1].rearrange("p k n -> p (k n)")
        tmp_gn = wide[:, 0:256].rearrange("p (q n) -> p q n", q=4)
        mean_gn, var_gn, rstd_gn = (wide[:, 256 + 64 * q:320 + 64 * q] for q in range(3))

        step = sem("vector_step")
        consts = sem("consts")
        params = sem("params")

        x_loaded = [sem(f"x_loaded_{q}") for q in range(4)]
        x_turned, x_copied = sem2("x_turned"), sem2("x_copied")
        stats = sem("stats")
        var_ready = [sem(f"var_ready{s}") for s in range(5)]
        sd_ready = [sem(f"sd_ready{s}") for s in range(5)]
        xn_ready, xn_turned, xt_ready, xt_used = sem2("xn_ready"), sem2("xn_turned"), sem2("xt_ready"), sem2("xt_used")
        bd_ready, lines_ready, gates_psum, sig_ready = sem("bd_ready"), sem("lines_ready"), sem("gates_psum"), sem("sig_ready")
        signed, pool_mid, gated_by_pool = sem("signed"), sem("pool_mid"), sem("gated_by_pool")
        gated_mid, gn_stats = sem("gated_mid"), sem("gn_stats")
        logit_ready, logit_turned, logit_sub, logit_exp = sem("logit_ready"), sem("logit_turned"), sem("logit_sub"), sem("logit_exp")
        soft_ready, soft_turned, shift_ready, shift_psum = sem("soft_ready"), sem("soft_turned"), sem("shift_ready"), sem("shift_psum")
        mix_ready, mix_psum, mix_sig, mix_out = sem2("mix_ready"), sem2("mix_psum"), sem2("mix_sig"), sem2("mix_out")
        mix_turned, mix_added = sem2("mix_turned"), sem2("mix_added")
        fin_turned, fin_copied, fin_stored = sem2("fin_turned"), sem2("fin_copied"), sem2("fin_stored")

        def pairs(eng, body, first=0):
            body(first)
            with eng.Fori(first + 1, HB) as i:
                body(i)

        def stage1_of(e):
            return scan1[:, 1 - e] if e < 2 else stage1[:, e % 2]

        def image_rows(v):
            return v.rearrange("p (b h w) -> p b h w", b=NB, h=HW)

        def gate_by_rows(eng, r, k):
            gates = sig[:, r, k, :, 0:HW].unsqueeze(3).to_broadcast([P, NB, HW, HW])
            return eng.tensor_tensor(image_rows(gated[:, r, k, :]), image_rows(g[:, k, :]), gates, ALU.mult)

        def gate_by_columns(eng, r, k):
            gates = sig[:, r, k, :, HW:2 * HW].unsqueeze(2).to_broadcast([P, NB, HW, HW])
            o = image_rows(gated[:, r, k, :])
            return eng.tensor_tensor(o, o, gates, ALU.mult)

        def free(eng, semaphore, count):
            if not isinstance(count, int) or count > 0:
                eng.wait_ge(semaphore, count)

        scratch = wreg[:, 32256:32768]
        nat_loaded, nat_turned, nat_copied, bias_loaded = sem("nat_loaded"), sem("nat_turned"), sem("nat_copied"), sem("bias_loaded")
        small_psum, small_ready = sem("small_psum"), sem("small_ready")
        gates_loaded = sem("gates_loaded")
        two = lambda name: [sem(f"{name}{f}") for f in range(2)]
        rows_hi, rows_ready = sem2("rows_hi"), sem2("rows_ready")
        logits_kept, exp_in, exp_out = sem2("logits_kept"), two("exp_in"), two("exp_out")
        hots_ready, counts_psum, moves_ready, rows_stored = two("hots_ready"), two("counts_psum"), two("moves_ready"), two("rows_stored")
        listed, list_taken = sem("listed"), sem("list_taken")
        fetches_copied, puts_copied = two("fetches_copied"), two("puts_copied")
        ids_listed = sem("ids_listed")
        y_used = [sem(f"y_used_{n}") for n in range(4)]
        y_gathered = [[sem(f"y_gathered_{n}") for n in range(4)], x_loaded]
        y_half = two("y_half")
        peak_ready, peak_spread = sem("peak_ready"), two("peak_spread")
        scan0_loaded = sem2("scan0_loaded")
        scan_loaded, scanned = sem2("scan_loaded"), sem("scanned")
        stage_loaded = [sem2(f"stage_loaded{f}") for f in range(2)]
        w_scale, w_turned, w_hi, w_lo = two("w_scale"), sem("w_turned"), two("w_hi"), two("w_lo")
        before_again = sem("before_again")
        v1_scaled, v1_lo, fac_ready = sem("v1_scaled"), sem("v1_lo"), two("fac_ready")
        xr_loaded, xr_turned, xc_ready = two("xr_loaded"), two("xr_turned"), two("xc_ready")
        z_ready, silu_done, hid_ready, hi_ready, lo_ready = two("z_ready"), two("silu_done"), sem("hid_ready"), two("hi_ready"), two("lo_ready")
        y_ready, y_copied, y_free = two("y_ready"), two("y_copied"), two("y_free")
        bias_added, conv_added = sem2("bias_added"), sem2("conv_added")

        block = ctx.enter_context(nc.Block())

        @block.sync
        def _(sp):
            for q in range(4):
                sp.dma_start(x_in[:, 4 * q:4 * q + 4].rearrange("p b k n -> p (b k) n"),
                             x[4 * q:4 * q + 4].rearrange("b (k p) l -> p (b k) l", p=P)).then_inc(x_loaded[q], 16)
            sp.dma_start(conv1_nat, weight.rearrange("(q p) i -> p q i", p=P)).then_inc(nat_loaded, 16)
            sp.dma_start(gate0_nat, gate0).then_inc(nat_loaded, 16)
            sp.dma_start(b1_nat, b1.rearrange("e (c n) -> (e c) n", n=P)).then_inc(nat_loaded, 16)
            sp.dma_start(small8[:, 0:CG], conv_w.rearrange("o i -> i o"), allow_slow_non_contiguous=True).then_inc(params, 16)
            for c, v in enumerate((conv_b, gn_w, gn_b)):
                sp.dma_start(small8[:, CG + c:CG + c + 1], v.rearrange("(c a) -> c a", a=1)).then_inc(params, 16)
            sp.dma_start(gate_w[:, 1], gate1.rearrange("(k p) e -> p k e", p=P)).then_inc(gates_loaded, 16)
            def load_stage0(e, j, loaded):
                for m, w in enumerate((w1, w3)):
                    sp.dma_start(stage0[:, j, m].rearrange("p (c d) -> p c d", c=4),
                                 w[bass.ds(e, 1)].rearrange("a (c p) d -> p (a c) d", p=P)).then_inc(loaded[j], 16)
                sp.dma_start(stage0[:, j, 2].rearrange("p (c h) -> p c h", c=KC),
                             w2[bass.ds(e, 1)].rearrange("a (c p) h -> p (a c) h", p=P)).then_inc(loaded[j], 16)

            def load_stage1(e, j):
                sp.dma_start(stage1[:, j, 0].rearrange("p (c h) -> p c h", c=KC),
                             v1[bass.ds(e, 1)].rearrange("a (c p) h -> p (a c) h", p=P)).then_inc(stage_loaded[1][j], 16)
                sp.dma_start(stage1[:, j, 1].rearrange("p (c d) -> p c d", c=8),
                             v2[bass.ds(e, 1)].rearrange("a (c p) d -> p (a c) d", p=P)).then_inc(stage_loaded[1][j], 16)

            def load_scan(n):
                e = E - 1 - n
                sp.dma_start(scan1[:, n % 2, 0].rearrange("p (c h) -> p c h", c=KC),
                             v1[e].rearrange("(c p) h -> p c h", p=P)).then_inc(scan_loaded[n % 2], 16)
                sp.dma_start(scan1[:, n % 2, 1].rearrange("p (c d) -> p c d", c=8),
                             v2[e].rearrange("(c p) d -> p c d", p=P)).then_inc(scan_loaded[n % 2], 16)

            def store_rows(f, i):
                for j in range(2):
                    sp.wait_ge(rows_ready[j], HB * f + i + 1)
                sp.dma_start(rows_x[f][bass.ds(i * 4 * P, 4 * P)].rearrange("(t p) c -> p t c", p=P),
                             rows[:, bass.ds(4 * i, 4), :]).then_inc(rows_stored[f], 16)

            def load_outputs(f, i, side=0):
                by_token = rows_y[f][0:2 * NT * P].rearrange("(k t p) c -> p k t c", k=2, p=P)
                for q in range(4):
                    free(sp, y_used[q], HB * f + i - (1 - f))
                    sp.dma_start((gath0[side], gath1)[f][q],
                                 by_token[:, :, bass.ds(4 * i + q, 1), :].rearrange("p k t c -> p (k t) c")
                                 ).then_inc(y_gathered[side][q], 16)

            for j in range(2):
                load_stage0(j, j, scan0_loaded)
            with sp.Fori(0, HB // 2 - 1) as h:
                for j in range(2):
                    store_rows(0, 2 * h + j)
                    sp.wait_ge(peak_ready, 2 * h + j + 1)
                    load_stage0(2 * h + j + 2, j, scan0_loaded)
            for j in range(2):
                store_rows(0, HB - 2 + j)
                sp.wait_ge(peak_ready, E - 1 + j)
                load_stage0(j, j, stage_loaded[0])
            with sp.Fori(1, E // 2) as i:
                for j in range(2):
                    sp.wait_ge(w_turned, 6 * (2 * i + j - 1))
                    load_stage0(2 * i + j, j, stage_loaded[0])
            sp.wait_ge(w_lo[0], 6 * E)
            for e in range(2):
                load_scan(e)
            for e in range(E - 2):
                sp.wait_ge(scanned, e + 1)
                load_scan(e + 2)
            total = sp.value_load(bounds[0:1, E:E + 1], min_val=E, max_val=TILES)
            sp.wait_ge(y_free[0], 32 * total + 16)
            sp.dma_start(bias_rows[:], bias.rearrange("c a -> (c a)").partition_broadcast(P)).then_inc(bias_loaded, 16)

            def reload_stage1(e):
                for by in (w_lo[1], v1_lo):
                    sp.wait_ge(by, e - 1)
                load_stage1(e, e % 2)

            for side in range(2):
                load_outputs(0, side, side)
            for h in range(1, 3):
                for side in range(2):
                    load_outputs(0, 2 * h + side, side)
                load_stage1(h + 1, (h + 1) % 2)
            load_outputs(0, HB - 2)
            load_outputs(0, HB - 1, side=1)
            reload_stage1(4)
            for e in range(5, E):
                reload_stage1(e)
            with sp.Fori(0, HB) as i:
                store_rows(1, i)
            sp.wait_ge(moves_ready[1], 1)
            total = sp.value_load(bounds[0:1, E:E + 1], min_val=E, max_val=TILES)
            sp.wait_ge(y_free[1], 32 * total + 16)
            pairs(sp, lambda i: load_outputs(1, i))

        CONSTS = 17

        @block.gpsimd
        def _(pool):
            ones, wide_i = scratch[:, 0:P], scratch[:, 2 * P:3 * P].bitcast(I32)
            nc.gpsimd.memset(ones, 1.0).then_inc(consts, 1)
            nc.gpsimd.memset(ident[:], 0.0).then_inc(consts, 1)
            nc.gpsimd.memset(scratch[:, P:2 * P], 0.0).then_inc(consts, 1)
            nc.gpsimd.memset(ones16[:], 1.0).then_inc(consts, 1)
            nc.gpsimd.iota(int_e[:, 0, :], [[-1, E]], base=E, channel_multiplier=0).then_inc(consts, 1)
            nc.gpsimd.iota(wide_i, [[1, P]], base=0, channel_multiplier=0).then_inc(consts, 1)
            nc.gpsimd.iota(int_e[:, 1, 0:1], [[0, 1]], base=0, channel_multiplier=1).then_inc(consts, 1)
            nc.gpsimd.iota(int_e[:, 1, 1:3], [[P, 2]], base=(2 * NT + 1) * P, channel_multiplier=1).then_inc(consts, 1)
            pool.wait_ge(consts, 8)
            nc.gpsimd.tensor_copy(count16[:], wide_i).then_inc(consts, 1)
            nc.gpsimd.tensor_copy(lane[:], int_e[:, 1, 0:3]).then_inc(consts, 1)
            nc.gpsimd.affine_select(out=ident[:], in_=ident[:], compare_op=ALU.not_equal, fill=1.0, base=0,
                                    pattern=[[-1, P]], channel_multiplier=1).then_inc(consts, 1)
            nc.gpsimd.affine_select(out=before16, in_=ones16[:, 0:1].to_broadcast([P, P]), compare_op=ALU.is_gt, fill=0.0, base=0,
                                    pattern=[[1, P]], channel_multiplier=-1).then_inc(consts, 1)
            grp = in_group.rearrange("p (g c) -> p g c", c=CG)
            nc.gpsimd.affine_select(out=grp, in_=ones.rearrange("p (g c) -> p g c", c=CG),
                                    compare_op=ALU.is_ge, fill=0.0, base=0,
                                    pattern=[[-CG, NG], [0, CG]], channel_multiplier=1).then_inc(consts, 1)
            nc.gpsimd.tensor_copy(rank[:], int_e[:, 0, :]).then_inc(consts, 1)
            pool.wait_ge(consts, 14)
            rep8 = repeat8.rearrange("p (g c) -> p g c", c=CG)
            nc.gpsimd.affine_select(out=rep8, in_=scratch[0:CG, P:2 * P].rearrange("p (g c) -> p g c", c=CG),
                                    compare_op=ALU.not_equal, fill=1.0, base=0, pattern=[[0, NG], [1, CG]],
                                    channel_multiplier=-1).then_inc(consts, 1)
            nc.gpsimd.tensor_copy(ident16[:], ident[:]).then_inc(consts, 1)
            nc.gpsimd.affine_select(out=grp, in_=grp, compare_op=ALU.is_ge, fill=0.0, base=CG - 1,
                                    pattern=[[CG, NG], [0, CG]], channel_multiplier=-1).then_inc(consts, 1)
            pool.wait_ge(consts, CONSTS)
            for j in range(2):
                pool.wait_ge(xt_ready[j], HB)
            for n, (r, k) in enumerate(((0, 0), (0, 1), (1, 1))):
                if r == 0:
                    pool.wait_ge(sig_ready, k + 1)
                else:
                    pool.wait_ge(signed, 1)
                gate_by_rows(nc.gpsimd, r, k).then_inc(pool_mid, 1)
                pool.wait_ge(pool_mid, n + 1)
                gate_by_columns(nc.gpsimd, r, k).then_inc(gated_by_pool, 1)

            def fetch(f, row_lists):
                for g_ in range(2):
                    nc.gpsimd.indirect_dma_start(x_rows[:, g_, :], None, rows_x[f],
                                                 bass.IndirectOffsetOnAxis(ap=row_lists[g_], axis=0)
                                                 ).then_inc(xr_loaded[f], 16)

            def after(n, waits):
                with pool.Fori(n, n + 1) as m:
                    waits(m)

            def spread_peaks(f):
                nc.gpsimd.partition_all_reduce(peak_all[:].rearrange("p e m -> p (e m)"), peak[:].rearrange("p e m -> p (e m)"),
                                               P, bass.bass_isa.ReduceOp.max).then_inc(peak_spread[f], 1)

            def feed_experts(f):
                if f == 0:
                    pool.wait_ge(peak_ready, E)
                    spread_peaks(0)
                pool.wait_ge(moves_ready[f], 1)
                pool.wait_ge(rows_stored[f], 16 * HB)
                total = pool.value_load(bounds[0:1, E:E + 1], min_val=E, max_val=TILES)
                fetch(f, [first_rows[:, g_:g_ + 1] for g_ in range(2)])
                to, bias_of = ((gate_b[:], gate1_b), (b2_all, b2))[f]
                pool.dma_start(to, bias_of.partition_broadcast(P)).then_inc(y_free[f], 16)

                def put(n):
                    pool.wait_ge(y_free[f], 32 * n + 16)
                    nc.gpsimd.tensor_copy(put_now[:], moves[:, bass.ds(2 * n, 2), 1]).then_inc(puts_copied[f], 1)

                    def may_put(m):
                        pool.wait_ge(puts_copied[f], m + 1)
                        pool.wait_ge(y_copied[f], m + 1)

                    after(n, may_put)
                    for g_ in range(2):
                        nc.gpsimd.indirect_dma_start(rows_y[f], bass.IndirectOffsetOnAxis(ap=put_now[:, g_:g_ + 1], axis=0),
                                                     y_rows[:, g_, :], None).then_inc(y_free[f], 16)

                def fetch_next(n):
                    pool.wait_ge(xr_turned[f], n + 1)
                    nc.gpsimd.tensor_copy(fetch_now[:], moves[:, bass.ds(2 * n, 2), 0]).then_inc(fetches_copied[f], 1)
                    after(n, lambda m: pool.wait_ge(fetches_copied[f], m + 1))
                    fetch(f, [fetch_now[:, g_:g_ + 1] for g_ in range(2)])

                fetch_next(0)
                with pool.Fori(0, total) as n:
                    fetch_next(n + 1)
                    put(n)

                def all_done(m):
                    pool.wait_ge(xc_ready[f], m + 2)
                    pool.wait_ge(xr_loaded[f], 32 * m + 96)
                    pool.wait_ge(y_free[f], 32 * m + 48)

                after(total - 1, all_done)
                if f == 0:
                    pool.wait_ge(scanned, E)
                    spread_peaks(1)


            def split_v1(e):
                pool.wait_ge(v1_scaled, e + 1)
                nc.gpsimd.tensor_tensor(v1_s[:, e, :, 1, :], stage1_of(e)[:, 0].rearrange("p (c n) -> p c n", c=KC),
                                        v1_s[:, e, :, 0, :], ALU.subtract).then_inc(v1_lo, 1)

            def add_bias(i):
                for j in range(2):
                    pool.wait_ge(xn_ready[j], HB * 2 + i + 1)
                    t = tok[:, bass.ds(4 * i + 2 * j, UT), :]
                    nc.gpsimd.tensor_tensor(t, t, bias_rows[:].unsqueeze(1).to_broadcast([P, UT, C]), ALU.add
                                            ).then_inc(bias_added[j], 1)

            for f in range(2):
                feed_experts(f)
                if f == 0:
                    for e in range(E // 2):
                        split_v1(e)
                    pool.wait_ge(bias_loaded, 16)
                    for e in range(E // 2, E):
                        with pool.Fori(2 * e - E, 2 * e - E + 2) as i:
                            add_bias(i)
                        split_v1(e)
                    for j in range(2):
                        pool.wait_ge(bias_added[j], HB)
                    nc.gpsimd.affine_select(out=before16, in_=ones16[:, 0:1].to_broadcast([P, P]), compare_op=ALU.is_gt,
                                            fill=0.0, base=0, pattern=[[1, P]], channel_multiplier=-1).then_inc(before_again, 1)

        @block.tensor
        def _(pe):
            def norm_turn(s, i, j):
                pe.wait_ge(xn_ready[j], HB * s + i + 1)
                free(pe, xt_ready[j], HB * s + i)
                to = turn[j][:].rearrange("p (k n) -> p k n", k=KC)
                for k in range(KC):
                    for h in range(UT):
                        last = pe.transpose(to[:, k, h * P:(h + 1) * P], xn[:, j, h, k * P:(k + 1) * P], ident[:])
                last.then_inc(xn_turned[j], 1)

            def turn_images(i):
                for j in range(2):
                    pe.wait_ge(x_loaded[i // 2], 16)
                    free(pe, x_copied[j], i)
                    to = turn[j][:].rearrange("p (h c) -> p h c", h=UT)
                    for h in range(UT):
                        for k in range(KC):
                            last = pe.transpose(to[:, h, k * P:(k + 1) * P], x_in[:, 2 * i + j, k, h * P:(h + 1) * P], ident[:])
                    last.then_inc(x_turned[j], 1)

            pe.wait_ge(consts, CONSTS)
            for i in range(HB):
                turn_images(i)
            pe.wait_ge(nat_loaded, 16 * 3)
            for q in range(KC):
                for k in range(KC):
                    pe.transpose(zb[0][:, k * C + q * P:k * C + (q + 1) * P], conv1_nat[:, q, k * P:(k + 1) * P], ident[:])
            for k in range(KC):
                pe.transpose(zb[1][:, k * E:(k + 1) * E], gate0_nat[:, k * P:(k + 1) * P], ident[0:E, 0:E])
            pe.transpose(zb[1][:, 64:128], b1_nat, ident[0:64, 0:64]).then_inc(nat_turned, 1)
            pe.wait_ge(params, 16 * 4)
            pe.matmul(misc[:, 0:CG + 3], repeat8, small8[:], start=True, stop=True).then_inc(small_psum, 1)

            def turn_normed(i):
                for j in range(2):
                    norm_turn(0, i, j)

            pairs(pe, turn_normed)
            pe.wait_ge(bd_ready, 1)
            for r in range(2):
                for k in range(KC):
                    pe.wait_ge(lines_ready, 2 * (r * KC + k) + 2)
                    pe.matmul(zb[2 * r + k][:], conv_bd[:], line[:, r, k].rearrange("p b l -> p (b l)"),
                              start=True, stop=True).then_inc(gates_psum, 1)
            pe.wait_ge(logit_ready, 1)
            pe.transpose(misc[0:64, 0:P], soft_in[:], ident[:]).then_inc(logit_turned, 1)
            pe.wait_ge(soft_ready, 1)
            pe.transpose(misc[:, P:P + 64], soft_t[:, 0, :], ident[0:64, 0:64]).then_inc(soft_turned, 1)
            pe.wait_ge(shift_ready, 1)
            pe.matmul(misc[:, 256:256 + KC * NB], in_group[:], shift[:, 0].rearrange("p k b -> p (k b)"),
                      start=True, stop=True).then_inc(shift_psum, 1)
            def mix_sums(i, j):
                pe.wait_ge(mix_ready[j], i + 1)
                free(pe, mix_sig[j], i)
                for k in range(KC):
                    for r in range(2):
                        u = 2 * i + j
                        last = pe.matmul(zb[j][:, k * L:(k + 1) * L], mix[:, j, r, k], gated[:, r, k, u * L:(u + 1) * L],
                                         start=(r == 0), stop=(r == 1))
                last.then_inc(mix_psum[j], 1)

            def turn_gated(i, j):
                pe.wait_ge(mix_out[j], i + 1)
                free(pe, mix_added[j], i)
                to = turn[j][:].rearrange("p (h c) -> p h c", h=UT)
                for h in range(UT):
                    for k in range(KC):
                        last = pe.transpose(to[:, h, k * P:(k + 1) * P], sig_mix[:, j, k, h * P:(h + 1) * P], ident[:])
                last.then_inc(mix_turned[j], 1)

            for j in range(2):
                mix_sums(0, j)
            for i in range(HB):
                for j in range(2):
                    turn_gated(i, j)
                    if i + 1 < HB:
                        mix_sums(i + 1, j)

            def router(f, i, j):
                pe.wait_ge(xt_ready[j], HB * (2 * f + 1) + i + 1)
                free(pe, logits_kept[j], HB * f + i)
                for h in range(UT):
                    for k in range(KC):
                        last = pe.matmul(zb[j][:, h * E:(h + 1) * E], xt[:, j, k, h * P:(h + 1) * P],
                                         gate_w[:, f, k], start=(k == 0), stop=(k == KC - 1))
                last.then_inc(xt_used[j], 1)

            def routing(f):
                def units(i):
                    for j in range(2):
                        norm_turn(2 * f + 1, i, j)
                    for j in range(2):
                        router(f, i, j)

                pairs(pe, units)
                pe.wait_ge(hots_ready[f], 1)
                flat_hots = hots16[:].rearrange("p t e -> p (t e)")
                if f == 1:
                    pe.wait_ge(before_again, 1)
                pe.matmul(misc[:, 0:NT * E], before16, flat_hots, start=True, stop=True)
                pe.matmul(misc[:, NT * E:2 * NT * E], ones16[:, 0:1].to_broadcast([P, P]), flat_hots, start=True, stop=True).then_inc(counts_psum[f], 1)

                def lists(i, start=False, stop=False):
                    for b in range(8):
                        pe.wait_ge(ids_listed, 8 * HB * f + 8 * i + b + 1)
                        pe.matmul(yb[:, 0:2 * GROUPS], hot_lane[:, b], hot_group[:, b].rearrange("p v n -> p (v n)"),
                                  start=start and b == 0, stop=stop and b == 7).then_inc(list_taken, 1)

                lists(0, start=True)
                with pe.Fori(1, HB - 1) as i:
                    lists(i)
                lists(HB - 1, stop=True)

            def stage_turns(i, j):
                e = 2 * i + j
                pe.wait_ge(stage_loaded[0][j], 48 * (i + 1))
                bank_free = lambda q: free(pe, w_lo[0], 6 * e + q - 5)
                for m in range(2):
                    for k in range(KC):
                        bank_free(2 * m + k)
                        for c in range(4):
                            last = pe.transpose(zb[2 * m + k][:, c * P:(c + 1) * P],
                                                stage0[:, j, m, c * C + k * P:c * C + (k + 1) * P], ident[:])
                        last.then_inc(w_turned, 1)
                for c in range(4):
                    if c % 2 == 0:
                        bank_free(4 + c // 2)
                    for k in range(KC):
                        last = pe.transpose(turn[c // 2][:, (c % 2) * C + k * P:(c % 2) * C + (k + 1) * P],
                                            stage0[:, j, 2, k * FH[0] + c * P:k * FH[0] + (c + 1) * P], ident[:])
                    if c % 2:
                        last.then_inc(w_turned, 1)

            x_turn16 = turn[0][:].bitcast(F16).rearrange("p (k s n) -> p k s n", k=KC, s=2)

            def turn_rows(f, tile):
                pe.wait_ge(xr_loaded[f], 32 * (tile + 1))
                for k in range(KC):
                    for s_ in range(2):
                        for r in range(2):
                            last = pe.transpose(x_turn16[:, k, s_, r * P:(r + 1) * P],
                                                x_rows[:, r, s_ * C + k * P:s_ * C + (k + 1) * P], ident16[:])
                last.then_inc(xr_turned[f], 1)

            PARTS = ((0, 0), (0, 1), (1, 0))

            def up(f, e, h):
                ws = ((w1_s, zb[2 * (h % 2)]), (w3_s, zb[2 * (h % 2) + 1])) if f == 0 else ((v1_s, zb[h]),)
                for w, z in ws:
                    for c in (2 * h, 2 * h + 1):
                        to = z[:, (c % 2) * TILE:(c % 2 + 1) * TILE]
                        for k in range(KC):
                            for ws_, xs_ in PARTS:
                                last = pe.matmul(to, w[:, e, k, ws_, c * P:(c + 1) * P], x_cols[:, k, xs_, :],
                                                 start=(k == 0 and ws_ + xs_ == 0), stop=(k == KC - 1 and ws_ == 1))
                    last.then_inc(z_ready[f], 1)

            def down(f, e, tile, h, halves):
                w = (w2_s, v2_s)[f]
                for c in (2 * h, 2 * h + 1):
                    if f == 0:
                        pe.wait_ge(lo_ready[0], 2 * halves * tile + c + 1)
                    elif c == 2 * h:
                        pe.wait_ge(lo_ready[1], halves * tile + h + 1)
                    for r in range(2):
                        for hs, ws_ in PARTS:
                            lhs = (hid_hi, hid_lo)[hs]
                            first = c == 0 and r == 0 and hs + ws_ == 0
                            end = c == 2 * halves - 1 and hs == 1
                            last = pe.matmul(yb[:, r * C:(r + 1) * C], lhs[:, c, r * P:(r + 1) * P], w[:, e, c, ws_, :],
                                             start=first, stop=end, skip_group_check=True)
                if h == halves - 1:
                    last.then_inc(y_ready[f], 1)

            def experts(f):
                halves = FH[f] // (2 * P)
                pe.wait_ge(w_lo[f], (6, 1)[f] * E)
                if f == 1:
                    pe.wait_ge(v1_lo, E)
                pe.wait_ge(fac_ready[f], 1)
                turn_rows(f, 0)
                edges = [pe.value_load(bounds[0:1, e:e + 1], min_val=0, max_val=TILES) for e in range(E + 1)]
                for e in range(E):
                    with pe.Fori(edges[e], edges[e + 1]) as n:
                        pe.wait_ge(xc_ready[f], n + 1)
                        for h in range(halves):
                            up(f, e, h)
                        for h in range(halves - 1):
                            down(f, e, n, h, halves)
                        turn_rows(f, n + 1)
                        down(f, e, n, halves - 1, halves)
                if f == 1:
                    pe.wait_ge(xc_ready[1], edges[E] + 1)

            routing(0)
            for j in range(2):
                stage_turns(0, j)
            with pe.Fori(1, E // 2) as i:
                for j in range(2):
                    stage_turns(i, j)
            experts(0)
            def mix_channels(i, j):
                pe.wait_ge(xt_ready[j], HB * 2 + i + 1)
                free(pe, conv_added[j], i)
                for h in range(UT):
                    for k in range(KC):
                        last = pe.matmul(zb[j][:, h * C:(h + 1) * C], xt[:, j, k, h * P:(h + 1) * P], conv1_wt[:, k],
                                         start=(k == 0), stop=(k == KC - 1))
                last.then_inc(xt_used[j], 1)

            def turn_ahead(i):
                for j in range(2):
                    mix_channels(i, j)
                    norm_turn(2, i + 1, j)

            for j in range(2):
                norm_turn(2, 0, j)
            turn_ahead(0)
            with pe.Fori(1, HB - 1) as i:
                turn_ahead(i)
            for j in range(2):
                mix_channels(HB - 1, j)
            pe.wait_ge(gates_loaded, 16)
            routing(1)
            experts(1)
            def turn_result(i):
                for j in range(2):
                    for h in range(UT):
                        pe.wait_ge(y_used[2 * j + h], HB + i + 1)
                    free(pe, fin_copied[j], i)
                    to = turn[j][:].rearrange("p (k n) -> p k n", k=KC)
                    for k in range(KC):
                        for h in range(UT):
                            last = pe.transpose(to[:, k, h * P:(h + 1) * P], xn[:, j, h, k * P:(k + 1) * P], ident[:])
                    last.then_inc(fin_turned[j], 1)

            pairs(pe, turn_result)

        @block.scalar
        def _(act):
            def deviation(s):
                act.wait_ge(var_ready[s], 1)
                r, v = (rstd[:], var[:]) if s < 4 else (rstd_gn, var_gn)
                act.activation(r, v, ACT.Sqrt).then_inc(sd_ready[s], 1)

            def copy_images(i):
                for j in range(2):
                    act.wait_ge(x_turned[j], i + 1)
                    act.activation(tok[:, bass.ds(4 * i + 2 * j, UT), :].rearrange("p h c -> p (h c)"),
                                   turn[j][:], ACT.Copy).then_inc(x_copied[j], 1)

            pairs(act, copy_images)
            act.wait_ge(nat_turned, 1)
            act.activation(conv1_wt[:].rearrange("p k c -> p (k c)"), zb[0][:], ACT.Copy).then_inc(nat_copied, 1)
            act.activation(gate_w[:, 0].rearrange("p k e -> p (k e)"), zb[1][:, 0:KC * E], ACT.Copy).then_inc(nat_copied, 1)
            act.activation(b1_t[:].rearrange("p e c -> p (e c)"), zb[1][:, 64:128], ACT.Copy).then_inc(nat_copied, 1)
            act.wait_ge(small_psum, 1)
            act.activation(small[:, 0:CG + 3], misc[:, 0:CG + 3], ACT.Copy).then_inc(small_ready, 1)
            deviation(0)
            with act.Fori(0, HB) as i:
                for j in range(2):
                    act.wait_ge(xn_turned[j], i + 1)
                    act.activation(g[:, :, bass.ds((2 * i + j) * L, L)], turn[j][:].rearrange("p (k n) -> p k n", k=KC),
                                   ACT.Copy).then_inc(xt_ready[j], 1)
            act.wait_ge(small_ready, 1)
            for r in range(2):
                for k in range(KC):
                    act.wait_ge(gates_psum, r * KC + k + 1)
                    act.activation(sig[:, r, k].rearrange("p b l -> p (b l)"), zb[2 * r + k][:], ACT.Sigmoid,
                                   bias=small[:, CG:CG + 1], scale=(1.0 / HW if r == 0 else 1.0)).then_inc(sig_ready, 1)
            deviation(4)
            act.wait_ge(logit_sub, 1)
            act.activation(soft_t[:, 1, :], soft_t[:, 0, :], ACT.Exp).then_inc(logit_exp, 1)
            def mix_gates(i):
                for j in range(2):
                    act.wait_ge(mix_psum[j], i + 1)
                    free(act, mix_turned[j], i)
                    for k in range(KC):
                        last = act.activation(sig_mix[:, j, k], zb[j][:, k * L:(k + 1) * L], ACT.Sigmoid,
                                              bias=shift[:, 1, k, bass.ds(2 * i + j, 1)])
                    last.then_inc(mix_sig[j], 1)

            pairs(act, mix_gates)

            def to_columns(s, i, j):
                act.wait_ge(xn_turned[j], HB * s + i + 1)
                free(act, xt_used[j], HB * (s - 1) + i)
                act.activation(xt[:, j].rearrange("p k n -> p (k n)"), turn[j][:], ACT.Copy).then_inc(xt_ready[j], 1)

            def route(f):
                deviation(2 * f + 1)
                def units(i):
                    for j in range(2):
                        act.wait_ge(xn_ready[j], HB * (2 * f + 1) + i + 1)
                        act.activation(rows[:, bass.ds(4 * i + 2 * j, UT), 0:C], xn[:, j], ACT.Copy, scale=XSCALE
                                       ).then_inc(rows_hi[j], 1)
                        to_columns(2 * f + 1, i, j)

                pairs(act, units)
                act.wait_ge(exp_in[f], 1)
                act.activation(ex, logits, ACT.Exp).then_inc(exp_out[f], 1)
                with act.Fori(0, HB) as i:
                    for b in range(8):
                        act.wait_ge(listed, 8 * HB * f + 8 * i + b + 1)
                        if b % 2 == 0:
                            act.activation(hot_group[:, b, 0], hot_one[:, b], ACT.Copy, scale=lane[:, 0:1])
                        act.activation(hot_group[:, b, 1], hot_one[:, b], ACT.Copy,
                                       scale=id_f[:, b % 2, bass.ds(4 * i + b // 2, 1)]).then_inc(ids_listed, 1)

            def columns16(f, tile):
                act.wait_ge(xr_turned[f], tile + 1)
                act.activation(x_cols.rearrange("p k s n -> p (k s n)"), turn[0][:].bitcast(F16), ACT.Copy
                               ).then_inc(xc_ready[f], 1)

            def experts(f):
                halves = FH[f] // (2 * P)
                columns16(f, 0)
                edges = [act.value_load(bounds[0:1, e:e + 1], min_val=0, max_val=TILES) for e in range(E + 1)]
                act.wait_ge(fac_ready[f], 1)
                for e in range(E):
                    with act.Fori(edges[e], edges[e + 1]) as n:
                        for h in range(halves):
                            if f == 0:
                                act.wait_ge(z_ready[0], 2 * halves * n + 2 * h + 1)
                                act.activation(gate_act[:, h], zb[2 * h][:], ACT.Silu, scale=fac[:, 0, e:e + 1]
                                               ).then_inc(silu_done[f], 1)
                                for c in (2 * h, 2 * h + 1):
                                    act.wait_ge(hid_ready, 2 * halves * n + c + 1)
                                    act.activation(hid_hi[:, c], hid[:, h, (c % 2) * TILE:(c % 2 + 1) * TILE], ACT.Copy
                                                   ).then_inc(hi_ready[f], 1)
                            else:
                                act.wait_ge(z_ready[1], halves * n + h + 1)
                                for c in range(2):
                                    last = act.activation(gate_act[:, h, c * TILE:(c + 1) * TILE], zb[h][:, c * TILE:(c + 1) * TILE],
                                                          ACT.Silu, bias=b1_t[:, e, 2 * h + c:2 * h + c + 1], scale=fac[:, 0, e:e + 1])
                                last.then_inc(silu_done[f], 1)
                        columns16(f, n + 1)
                        if f == 0:
                            act.wait_ge(y_ready[f], n + 1)
                            act.wait_ge(y_free[f], 32 * n + 16)
                            act.activation(y_rows.rearrange("p g c -> p (g c)"), yb[:], ACT.Copy, scale=fac[:, 2, e:e + 1]
                                           ).then_inc(y_copied[f], 1)

            route(0)
            act.wait_ge(w_scale[0], 1)
            with act.Fori(0, E // 2) as i:
                for j in range(2):
                    e = 2 * i + j
                    for q in range(6):
                        act.wait_ge(w_turned, 6 * e + q + 1)
                        m, k = divmod(q, 2)
                        to = ((w1_s, w3_s)[m][:, bass.ds(e, 1), k, 0, :].rearrange("p a n -> p (a n)") if m < 2 else
                              w2_s[:, bass.ds(e, 1), 2 * k:2 * k + 2, 0, :].rearrange("p a c n -> p (a c) n"))
                        src = zb[q][:] if m < 2 else turn[k][:].rearrange("p (c n) -> p c n", c=2)
                        act.activation(to, src, ACT.Copy, scale=scl[:, bass.ds(e, 1), m:m + 1].rearrange("p a b -> p (a b)")
                                       ).then_inc(w_hi[0], 1)
            experts(0)
            act.wait_ge(w_scale[1], 1)

            def high1(e, m):
                if m == 0 and e >= 2:
                    act.wait_ge(stage_loaded[1][e % 2], 32 * (e // 2))
                w, c = ((v1_s, KC), (v2_s, 8))[m]
                act.activation(w[:, e, :, 0, :], stage1_of(e)[:, m].rearrange("p (c n) -> p c n", c=c), ACT.Copy,
                               scale=scl[:, e, m:m + 1]).then_inc(w_hi[1], 1)

            def scale_v1(e):
                stage = stage1_of(e)[:, 0]
                act.activation(stage, stage, ACT.Copy, scale=scl[:, e, 0:1]).then_inc(v1_scaled, 1)

            for e in range(E // 2):
                high1(e, 0)
                high1(e, 1)
                scale_v1(e)
            deviation(2)
            for i in range(HB):
                e = E // 2 + i // 2
                for j in range(2):
                    to_columns(2, i, j)
                    if i % 2 == 0:
                        high1(e, j)
                    elif j == 0:
                        scale_v1(e)
            for by in (w_lo[1], v1_lo):
                act.wait_ge(by, E)
            route(1)
            experts(1)
            def store_result(i):
                for j in range(2):
                    act.wait_ge(fin_turned[j], i + 1)
                    free(act, fin_stored[j], 16 * i)
                    act.activation(xt[:, j].rearrange("p k n -> p (k n)"), turn[j][:], ACT.Copy).then_inc(fin_copied[j], 1)
                for j in range(2):
                    act.wait_ge(fin_copied[j], i + 1)
                    act.dma_start(out[bass.ds(2 * i + j, 1)].rearrange("a (k p) l -> p (a k) l", p=P), xt[:, j]
                                  ).then_inc(fin_stored[j], 16)

            pairs(act, store_result)
            for j in range(2):
                act.wait_ge(fin_stored[j], 16 * HB)

        @block.vector
        def _(dve):
            done = [0]

            def chain(ins):
                done[0] += 1
                ins.then_inc(step, 1)
                dve.wait_ge(step, done[0])

            def deviations(s, count, eps):
                a, b = (st[:] if s < 4 else st_gn), [(tmp if s < 4 else tmp_gn)[:, q, :] for q in range(4)]
                m, v, r = (mean[:], var[:], rstd[:]) if s < 4 else (mean_gn, var_gn, rstd_gn)
                chain(dve.tensor_tensor(b[0], a[:, :, 1], a[:, :, 4], ALU.add))
                chain(dve.tensor_tensor(b[1], a[:, :, 1], a[:, :, 4], ALU.subtract))
                chain(dve.tensor_tensor(b[2], a[:, :, 2], a[:, :, 5], ALU.add))
                chain(dve.tensor_scalar(m, b[0], 0.5, None, ALU.mult))
                chain(dve.scalar_tensor_tensor(b[3], b[1], 0.25, b[1], ALU.mult, ALU.mult))
                chain(dve.scalar_tensor_tensor(b[0], b[2], 1.0 / count, b[3], ALU.mult, ALU.add))
                dve.tensor_scalar(v, b[0], eps, None, ALU.add).then_inc(var_ready[s], 1)
                dve.wait_ge(sd_ready[s], 1)
                chain(dve.reciprocal(b[1], r))
                chain(dve.tensor_tensor(b[2], b[1], b[1], ALU.mult))
                chain(dve.tensor_tensor(b[3], b[2], v, ALU.mult))
                chain(dve.tensor_scalar(b[0], b[3], -0.5, 1.5, ALU.mult, ALU.add))
                chain(dve.tensor_tensor(r, b[1], b[0], ALU.mult))

            def tile_stats(s, i, j):
                for h in range(UT):
                    t = 4 * i + 2 * j + h
                    dve.bn_stats(st[:, bass.ds(t, 1), :].rearrange("p a b -> p (a b)"),
                                 tok[:, bass.ds(t, 1), :].rearrange("p a b -> p (a b)")).then_inc(stats, 1)

            def norm(s, i, j):
                if s % 2:
                    free(dve, rows_ready[j], HB * (s // 2) + i)
                free(dve, xn_turned[j], HB * s + i)
                for h in range(UT):
                    t = 4 * i + 2 * j + h
                    last = dve.tensor_scalar(xn[:, j, h], tok[:, bass.ds(t, 1), :].rearrange("p a b -> p (a b)"),
                                             mean[:, bass.ds(t, 1)], rstd[:, bass.ds(t, 1)], ALU.subtract, ALU.mult)
                last.then_inc(xn_ready[j], 1)

            with dve.Fori(0, HB) as i:
                for j in range(2):
                    dve.wait_ge(x_copied[j], i + 1)
                    tile_stats(0, i, j)
            dve.wait_ge(stats, NT * 1)
            deviations(0, C, 1e-6)

            def norm_units(i):
                for j in range(2):
                    norm(0, i, j)

            pairs(dve, norm_units)
            dve.wait_ge(small_ready, 1)
            dve.wait_ge(consts, CONSTS)
            dve.tensor_tensor(conv_bd[:].rearrange("p (g c) -> p g c", c=CG), in_group[:].rearrange("p (g c) -> p g c", c=CG),
                              small[:, 0:CG].unsqueeze(1).to_broadcast([P, NG, CG]), ALU.mult).then_inc(bd_ready, 1)
            for j in range(2):
                dve.wait_ge(xt_ready[j], HB)
            for r, op in enumerate((ALU.add, ALU.max)):
                for k in range(KC):
                    v = g[:, k, :].rearrange("p (b h w) -> p b h w", b=NB, h=HW)
                    dve.tensor_reduce(line[:, r, k, :, 0:HW], v, AX.X, op).then_inc(lines_ready, 1)
                    dve.tensor_reduce(line[:, r, k, :, HW:2 * HW], v.rearrange("p b h w -> p b w h"), AX.X, op).then_inc(lines_ready, 1)
            gn_w_, sign, size = (small[:, CG + n:CG + n + 1] for n in (1, 3, 4))
            chain(dve.tensor_scalar(sign, gn_w_, 0.0, None, ALU.is_ge))
            chain(dve.tensor_scalar(sign, sign, 2.0, -1.0, ALU.mult, ALU.add))
            chain(dve.tensor_tensor(size, sign, gn_w_, ALU.mult))
            dve.wait_ge(nat_copied, 3)

            def channel_stats(r, k):
                for b in range(NB):
                    dve.bn_stats(st_gn[:, (r * KC + k) * NB + b, :], gated[:, r, k, b * L:(b + 1) * L]).then_inc(gn_stats, 1)

            def maxima(k):
                return dve.tensor_reduce(ends[:, k], gated[:, 1, k, :].rearrange("p (b n) -> p b n", b=NB), AX.X, ALU.max)

            dve.wait_ge(gated_by_pool, 1)
            channel_stats(0, 0)
            dve.wait_ge(sig_ready, KC * 2)
            for k in range(KC):
                last = dve.tensor_scalar(sig[:, 1, k, :, 0:HW], sig[:, 1, k, :, 0:HW], sign, None, ALU.mult)
            last.then_inc(signed, 1)
            dve.wait_ge(signed, 1)
            gate_by_rows(dve, 1, 0).then_inc(gated_mid, 1)
            dve.wait_ge(gated_mid, 1)
            gate_by_columns(dve, 1, 0).then_inc(gated_mid, 1)
            dve.wait_ge(gated_by_pool, 2)
            channel_stats(0, 1)
            dve.wait_ge(gated_mid, 2)
            channel_stats(1, 0)
            maxima(0)
            dve.wait_ge(gated_by_pool, 3)
            channel_stats(1, 1)
            chain(maxima(1))
            dve.wait_ge(gn_stats, 64)
            deviations(4, L, 1e-5)
            flat = lambda v: v.rearrange("p r k b -> p (r k b)")
            for r, w in enumerate((gn_w_, size)):
                chain(dve.tensor_scalar(flat(a_gn[:])[:, 32 * r:32 * r + 32], rstd_gn[:, 32 * r:32 * r + 32], w, None, ALU.mult))
            chain(dve.tensor_tensor(tmp_gn[:, 0, :], mean_gn, flat(a_gn[:]), ALU.mult))
            chain(dve.tensor_scalar(flat(b_gn[:]), tmp_gn[:, 0, :], -1.0, small[:, CG + 2:CG + 3], ALU.mult, ALU.add))
            m0, a1 = tmp_gn[:, 0, 0:32], a_gn[:, 1].rearrange("p k b -> p (k b)")
            chain(dve.tensor_tensor(m0, mean_gn[:, 0:32], a_gn[:, 0].rearrange("p k b -> p (k b)"), ALU.mult))
            chain(dve.tensor_tensor(soft_in[:, 0:32], m0, b_gn[:, 0].rearrange("p k b -> p (k b)"), ALU.add))
            chain(dve.tensor_tensor(tmp_gn[:, 1, 0:32], ends.rearrange("p k b -> p (k b)"), a1, ALU.mult))
            dve.tensor_tensor(soft_in[:, 32:64], tmp_gn[:, 1, 0:32], b_gn[:, 1].rearrange("p k b -> p (k b)"),
                              ALU.add).then_inc(logit_ready, 1)
            dve.wait_ge(logit_turned, 1)
            of_group = lambda v: v.rearrange("p (g c) -> p g c", c=CG)
            wide = lambda v: v.unsqueeze(2).to_broadcast([64, NG, CG])
            chain(dve.tensor_reduce(soft_s[:, 0, :], of_group(misc[0:64, 0:P]), AX.X, ALU.max))
            dve.tensor_tensor(of_group(soft_t[:, 0, :]), of_group(misc[0:64, 0:P]), wide(soft_s[:, 0, :]),
                              ALU.subtract).then_inc(logit_sub, 1)
            dve.wait_ge(logit_exp, 1)
            chain(dve.tensor_reduce(soft_s[:, 0, :], of_group(soft_t[:, 1, :]), AX.X, ALU.add))
            chain(dve.reciprocal(soft_s[:, 1, :], soft_s[:, 0, :]))
            dve.tensor_tensor(of_group(soft_t[:, 0, :]), of_group(soft_t[:, 1, :]), wide(soft_s[:, 1, :]),
                              ALU.mult).then_inc(soft_ready, 1)
            dve.wait_ge(soft_turned, 1)
            chain(dve.tensor_copy(flat(soft[:]), misc[:, P:P + 64]))
            for r in range(2):
                chain(dve.tensor_tensor(coef[:, r], soft[:, 1 - r], a_gn[:, r], ALU.mult))
                chain(dve.tensor_tensor(shift[:, r], soft[:, 1 - r], b_gn[:, r], ALU.mult))
            dve.tensor_tensor(shift[:, 0], shift[:, 0], shift[:, 1], ALU.add).then_inc(shift_ready, 1)
            dve.wait_ge(shift_psum, 1)
            chain(dve.tensor_copy(shift[:, 1].rearrange("p k b -> p (k b)"), misc[:, 256:256 + KC * NB]))

            def masks(i, j):
                free(dve, mix_psum[j], i)
                for r in range(2):
                    for k in range(KC):
                        last = dve.tensor_scalar(mix[:, j, r, k], in_group[:], coef[:, r, k, bass.ds(2 * i + j, 1)],
                                                 None, ALU.mult)
                last.then_inc(mix_ready[j], 1)

            masks(0, 0)
            masks(0, 1)

            def gate_units(i, more):
                for j in range(2):
                    dve.wait_ge(mix_sig[j], i + 1)
                    dve.tensor_tensor(sig_mix[:, j], sig_mix[:, j], g[:, :, bass.ds((2 * i + j) * L, L)],
                                      ALU.mult).then_inc(mix_out[j], 1)
                    if more:
                        masks(i + 1, j)
                for j in range(2):
                    dve.wait_ge(mix_turned[j], i + 1)
                    t = tok[:, bass.ds(4 * i + 2 * j, UT), :].rearrange("p h c -> p (h c)")
                    dve.tensor_tensor(t, t, turn[j][:], ALU.add).then_inc(mix_added[j], 1)
                for j in range(2):
                    dve.wait_ge(mix_added[j], i + 1)
                    tile_stats(1, i, j)

            with dve.Fori(0, HB - 1) as i:
                gate_units(i, True)
            gate_units(HB - 1, False)
            dve.wait_ge(stats, NT * 2)

            def scan0_peaks(e, j):
                dve.wait_ge(scan0_loaded[j], 24 * (e - j) + 48)
                dve.tensor_reduce(peak[:, bass.ds(e, 1), :].rearrange("p a m -> p (a m)"), stage0[:, j], AX.X, ALU.max,
                                  apply_absolute_value=True).then_inc(peak_ready, 1)

            def route(f):
                s = 2 * f + 1
                deviations(s, C, 1e-5)

                def keep_logits(i):
                    for j in range(2):
                        dve.wait_ge(xt_used[j], HB * (s - 1) + i + 1)
                        dve.tensor_copy(logits[:, bass.ds(4 * i + 2 * j, UT), :],
                                        zb[j][:, 0:UT * E].rearrange("p (t e) -> p t e", e=E)).then_inc(logits_kept[j], 1)

                def units(i, i_odd, before=None):
                    for j in range(2):
                        norm(s, i, j)
                    if f == 0:
                        scan0_peaks(i, i_odd)
                    if before is not None:
                        keep_logits(before)
                    for j in range(2):
                        dve.wait_ge(rows_hi[j], HB * f + i + 1)
                        at = rows[:, bass.ds(4 * i + 2 * j, UT), :]
                        dve.scalar_tensor_tensor(at[:, :, C:2 * C], xn[:, j], XSCALE, at[:, :, 0:C], ALU.mult, ALU.subtract
                                                 ).then_inc(rows_ready[j], 1)

                units(0, 0)
                units(1, 1, before=0)
                with dve.Fori(1, HB // 2) as h:
                    for j in range(2):
                        units(2 * h + j, j, before=2 * h + j - 1)
                keep_logits(HB - 1)
                for j in range(2):
                    dve.wait_ge(logits_kept[j], HB * (f + 1))
                    dve.wait_ge(rows_ready[j], HB * (f + 1))
                over_e = lambda v: v.unsqueeze(2).to_broadcast([P, NT, E])
                over_t = lambda v: v.unsqueeze(1).to_broadcast([P, NT, E])
                lg = logits
                if f == 1:
                    dve.wait_ge(y_free[0], 16)
                    chain(dve.tensor_tensor(lg, logits, over_t(gate_b[:]), ALU.add))
                chain(dve.tensor_reduce(red[:, 0, :], lg, AX.X, ALU.max))
                dve.tensor_tensor(lg, lg, over_e(red[:, 0, :]), ALU.subtract).then_inc(exp_in[f], 1)
                dve.wait_ge(exp_out[f], 1)
                chain(dve.tensor_reduce(red[:, 0, :], ex, AX.X, ALU.add))
                chain(dve.reciprocal(red[:, 1, :], red[:, 0, :]))
                chain(dve.tensor_tensor(ex, ex, over_e(red[:, 1, :]), ALU.mult))
                for k, hot in enumerate((hot1, hot2)):
                    chain(dve.tensor_reduce(top[:, k, :], ex, AX.X, ALU.max))
                    chain(dve.tensor_tensor(eq, ex, over_e(top[:, k, :]), ALU.is_equal))
                    chain(dve.tensor_tensor(eq, eq, over_t(rank[:]), ALU.mult))
                    chain(dve.tensor_reduce(red[:, 0, :], eq, AX.X, ALU.max))
                    chain(dve.tensor_tensor(hot, eq, over_e(red[:, 0, :]), ALU.is_equal))
                    if k == 0:
                        chain(dve.scalar_tensor_tensor(ex, hot, -2.0, ex, ALU.mult, ALU.add))
                dve.tensor_tensor(hots16[:], hot1, hot2, ALU.add).then_inc(hots_ready[f], 1)
                if f == 0:
                    chain(dve.tensor_tensor(red[:, 0, :], top[:, 0, :], top[:, 1, :], ALU.add))
                    chain(dve.tensor_scalar(red[:, 0, :], red[:, 0, :], 1e-8, None, ALU.add))
                    chain(dve.reciprocal(red[:, 1, :], red[:, 0, :]))
                    for k in range(2):
                        chain(dve.tensor_tensor(top[:, 2 + k, :], top[:, k, :], red[:, 1, :], ALU.mult))
                else:
                    chain(dve.tensor_copy(top[:, 2:4, :], top[:, 0:2, :]))
                dve.wait_ge(counts_psum[f], 1)
                pre = misc[:, 0:NT * E].rearrange("p (t e) -> p t e", e=E)
                chain(dve.tensor_copy(tot, misc[:, NT * E:2 * NT * E].rearrange("p (t e) -> p t e", e=E)))
                chain(dve.memset(eq, 1.0))
                for e in range(E):
                    last = dve.tensor_tensor_scan(incl[:, :, e], eq[:, :, e], tot[:, :, e], 0.0, ALU.mult, ALU.add)
                chain(last)
                need, base = per_e[:, 1, :], per_e[:, 2, :]
                chain(dve.tensor_scalar(per_e[:, 0, :], incl[:, NT - 1, :], TILE - 1.0, None, ALU.add))
                chain(dve.tensor_copy(int_e[:, 0, :], per_e[:, 0, :]))
                chain(dve.tensor_scalar(int_e[:, 1, :], int_e[:, 0, :], 8, None, ALU.logical_shift_right))
                chain(dve.tensor_copy(per_e[:, 3, :], int_e[:, 1, :]))
                chain(dve.tensor_scalar(need, per_e[:, 3, :], 1.0, None, ALU.max))
                chain(dve.tensor_tensor_scan(per_e[:, 0, :], eq[:, 0, :], need, 0.0, ALU.mult, ALU.add))
                chain(dve.memset(bounds[:, 0:1], 0))
                chain(dve.tensor_copy(bounds[:, 1:E + 1], per_e[:, 0, :]))
                chain(dve.tensor_tensor(base, per_e[:, 0, :], need, ALU.subtract))
                chain(dve.tensor_scalar(per_e[:, 3, :], base, float(TILE), None, ALU.mult))
                chain(dve.tensor_tensor(slot_f, incl, tot, ALU.subtract))
                chain(dve.tensor_tensor(slot_f, slot_f, pre, ALU.add))
                chain(dve.tensor_tensor(slot_f, slot_f, over_t(per_e[:, 3, :]), ALU.add))
                for k, hot in enumerate((hot1, hot2)):
                    chain(dve.tensor_tensor(eq, slot_f, hot, ALU.mult))
                    chain(dve.tensor_reduce(red[:, k, :], eq, AX.X, ALU.add))
                chain(dve.tensor_copy(slot_i, red[:]))
                chain(dve.tensor_scalar(lane_i, slot_i, P - 1, None, ALU.bitwise_and))
                chain(dve.tensor_scalar(group_i, slot_i, 7, None, ALU.logical_shift_right))
                chain(dve.tensor_copy(lane_f, lane_i))
                chain(dve.tensor_copy(group_f, group_i))
                flat = lambda v: v.rearrange("p k t -> p (k t)")
                chain(dve.memset(flat(red), 1.0))
                chain(dve.tensor_tensor_scan(flat(id_f), flat(red), flat(red), 0.0, ALU.mult, ALU.add))

                def lists(i):
                    for b in range(8):
                        q, k = divmod(b, 2)
                        at = lambda v: v[:, k, bass.ds(4 * i + q, 1)]
                        if f or not isinstance(i, int):
                            dve.wait_ge(list_taken, 8 * HB * f + 8 * i + b - 7)
                        dve.tensor_scalar(hot_lane[:, b], count16[:], at(lane_f), None, ALU.is_equal)
                        if b % 2:
                            dve.tensor_scalar(hot_group[:, b, 0], count16[:, 0:GROUPS], at(group_f), lane[:, 0:1],
                                              ALU.is_equal, ALU.mult)
                        dve.tensor_scalar(hot_one[:, b], count16[:, 0:GROUPS], at(group_f), None, ALU.is_equal).then_inc(listed, 1)

                pairs(dve, lists)
                dve.wait_ge(list_taken, 8 * HB * (f + 1))
                lane_sum, id_sum = yb[:, 0:GROUPS], yb[:, GROUPS:2 * GROUPS]
                by_half = lambda v, h: v.rearrange("p (n h) -> p n h", h=2)[:, :, h]
                for h in range(2):
                    chain(dve.tensor_scalar(by_half(pad_f, h), by_half(id_sum, h), 0.0, lane[:, 1 + h:2 + h],
                                            ALU.is_equal, ALU.mult))
                chain(dve.scalar_tensor_tensor(sum_f, id_sum, float(P), pad_f, ALU.mult, ALU.add))
                chain(dve.tensor_tensor(pad_f, sum_f, lane_sum, ALU.add))
                chain(dve.tensor_scalar(to_f, pad_f, -float(P), None, ALU.add))
                chain(dve.tensor_copy(moves[:, 0:GROUPS, 1], to_f))
                chain(dve.tensor_scalar(moves[:, 0:GROUPS - 2, 0], moves[:, 2:GROUPS, 1], NT * P - 1, None, ALU.bitwise_and))
                chain(dve.memset(moves[:, GROUPS - 2:GROUPS + 2, 0], 0))
                dve.tensor_scalar(first_rows[:], moves[:, 0:2, 1], NT * P - 1, None, ALU.bitwise_and).then_inc(moves_ready[f], 1)

            def scales(f):
                at = lambda v: v.rearrange("p e m -> p (e m)")
                dve.wait_ge(peak_spread[f], 1)
                chain(dve.tensor_scalar(at(pw).bitcast(U32), at(peak_all).bitcast(U32), 0x7F800000, None, ALU.bitwise_and))
                chain(dve.tensor_scalar(at(pw), at(pw), 2.0 ** -40, None, ALU.max))
                chain(dve.reciprocal(at(inv), at(pw)))
                dve.tensor_scalar(at(scl), at(inv), BIG, None, ALU.mult).then_inc(w_scale[f], 1)
                dve.wait_ge(w_scale[f], 1)

            def scan1_peaks(e):
                dve.wait_ge(scan_loaded[e % 2], 32 * (e // 2 + 1))
                last = dve.tensor_reduce(peak[:, E - 1 - e, 0:2], scan1[:, e % 2], AX.X, ALU.max, apply_absolute_value=True)
                if e == E - 1:
                    last = dve.tensor_reduce(peak[:, :, 2], b1_t[:], AX.X, ALU.max, apply_absolute_value=True)
                last.then_inc(scanned, 1)

            def lows0(e):
                for q in range(6):
                    m, k = divmod(q, 2)
                    dve.wait_ge(w_hi[0], 6 * e + q + 1)
                    if m < 2:
                        to, hi = ((w1_s, w3_s)[m][:, bass.ds(e, 1), k, s_, :].rearrange("p a n -> p (a n)") for s_ in (1, 0))
                        src = zb[q][:]
                    else:
                        to, hi = (w2_s[:, bass.ds(e, 1), 2 * k:2 * k + 2, s_, :].rearrange("p a c n -> p (a c) n") for s_ in (1, 0))
                        src = turn[k][:].rearrange("p (c n) -> p c n", c=2)
                    dve.scalar_tensor_tensor(to, src, scl[:, bass.ds(e, 1), m:m + 1].rearrange("p a b -> p (a b)"),
                                             hi, ALU.mult, ALU.subtract).then_inc(w_lo[0], 1)

            def low1(e):
                dve.wait_ge(w_hi[1], 2 * e + 2)
                to, hi = (v2_s[:, e, :, s_, :] for s_ in (1, 0))
                dve.scalar_tensor_tensor(to, stage1_of(e)[:, 1].rearrange("p (c n) -> p c n", c=8), scl[:, e, 1:2],
                                         hi, ALU.mult, ALU.subtract).then_inc(w_lo[1], 1)

            def factors(f):
                p = [pw[:, :, m] for m in range(3)]
                if f == 0:
                    chain(dve.tensor_scalar(fac[:, 0], p[0], 2.0 ** -24, None, ALU.mult))
                    chain(dve.tensor_scalar(fac[:, 1], inv[:, :, 0], 2.0 ** -27, None, ALU.mult))
                    chain(dve.scalar_tensor_tensor(per_e[:, 0], p[0], 2.0 ** -11, p[1], ALU.mult, ALU.mult))
                    last = dve.tensor_tensor(fac[:, 2], per_e[:, 0], p[2], ALU.mult)
                else:
                    chain(dve.tensor_scalar(fac[:, 0], p[0], 2.0 ** -24, None, ALU.mult))
                    chain(dve.scalar_tensor_tensor(per_e[:, 0], p[2], 2.0 ** -8, p[0], ALU.mult, ALU.max))
                    chain(dve.reciprocal(per_e[:, 1], per_e[:, 0]))
                    chain(dve.tensor_scalar(fac[:, 1], per_e[:, 1], 2.0 ** 5, None, ALU.mult))
                    last = dve.scalar_tensor_tensor(fac[:, 2], per_e[:, 0], 2.0 ** -19, p[1], ALU.mult, ALU.mult)
                last.then_inc(fac_ready[f], 1)
                dve.wait_ge(fac_ready[f], 1)

            def experts(f):
                halves = FH[f] // (2 * P)
                edges = [dve.value_load(bounds[0:1, e:e + 1], min_val=0, max_val=TILES) for e in range(E + 1)]
                for e in range(E):
                    with dve.Fori(edges[e], edges[e + 1]) as n:
                        for h in range(halves):
                            dve.wait_ge(silu_done[f], halves * n + h + 1)
                            to_hi, to_lo = (v[:, 2 * h:2 * h + 2].rearrange("p c n -> p (c n)") for v in (hid_hi, hid_lo))
                            if f == 0:
                                dve.wait_ge(z_ready[0], 2 * halves * n + 2 * h + 2)
                                half = lambda v, c: v[:, (c % 2) * TILE:(c % 2 + 1) * TILE]
                                for c in (2 * h, 2 * h + 1):
                                    dve.scalar_tensor_tensor(half(hid[:, h], c), half(zb[2 * h + 1], c), fac[:, 1, e:e + 1],
                                                             half(gate_act[:, h], c), ALU.mult, ALU.mult).then_inc(hid_ready, 1)
                                for c in (2 * h, 2 * h + 1):
                                    dve.wait_ge(hi_ready[f], 2 * halves * n + c + 1)
                                    dve.tensor_tensor(hid_lo[:, c], half(hid[:, h], c), hid_hi[:, c], ALU.subtract
                                                      ).then_inc(lo_ready[f], 1)
                            else:
                                dve.tensor_scalar(to_hi, gate_act[:, h], fac[:, 1, e:e + 1], None, ALU.mult
                                                  ).then_inc(hi_ready[f], 1)
                                dve.wait_ge(hi_ready[f], halves * n + h + 1)
                                dve.scalar_tensor_tensor(to_lo, gate_act[:, h], fac[:, 1, e:e + 1], to_hi, ALU.mult, ALU.subtract
                                                         ).then_inc(lo_ready[f], 1)
                        if f == 1:
                            dve.wait_ge(y_ready[f], n + 1)
                            dve.wait_ge(y_free[f], 32 * n + 16)
                            dve.scalar_tensor_tensor(y_rows, yb[:].rearrange("p (g c) -> p g c", g=2), fac[:, 2, e:e + 1],
                                                     b2_all[:, e].unsqueeze(1).to_broadcast([P, 2, C]), ALU.mult, ALU.add
                                                     ).then_inc(y_copied[f], 1)
                    if f == 0:
                        scan1_peaks(e)

            def combine(f, i, j, to, side=0):
                row = lambda t: tok[:, bass.ds(t, 1), :].rearrange("p a c -> p (a c)")
                y = lambda q: (gath0[side], gath1)[f][q]
                w = lambda t, k: top[:, 2 + k, bass.ds(t, 1)]
                for q in (2 * j, 2 * j + 1):
                    t = 4 * i + q
                    dve.wait_ge(y_gathered[side][q], 8 * (i - side) + 16 + 16 * side if f == 0 else 8 * HB + 16 * (i + 1))
                    dve.scalar_tensor_tensor(row(t), y(q)[:, 0], w(t, 0), row(t), ALU.mult, ALU.add).then_inc(y_half[f], 1)
                for h in range(UT):
                    q = 2 * j + h
                    t = 4 * i + q
                    dve.wait_ge(y_half[f], t + 1)
                    dve.scalar_tensor_tensor(row(t) if to is None else to[:, h], y(q)[:, 1], w(t, 1), row(t),
                                             ALU.mult, ALU.add).then_inc(y_used[q], 1)

            route(0)
            scales(0)
            with dve.Fori(0, E // 2) as i:
                for j in range(2):
                    lows0(2 * i + j)
            dve.wait_ge(w_lo[0], 6 * E)
            factors(0)
            experts(0)
            scales(1)
            def combine_tiles(i, side):
                for j in range(2):
                    combine(0, i, j, None, side)
                for q in range(4):
                    dve.wait_ge(y_used[q], i + 1)
                    t = 4 * i + q
                    dve.bn_stats(st[:, bass.ds(t, 1), :].rearrange("p a b -> p (a b)"),
                                 tok[:, bass.ds(t, 1), :].rearrange("p a b -> p (a b)")).then_inc(stats, 1)

            for e in range(E // 2):
                for side in range(2):
                    combine_tiles(2 * e + side, side)
                low1(e)
            factors(1)
            dve.wait_ge(stats, NT * 3)
            deviations(2, C, 1e-6)
            def add_mixed(i):
                for j in range(2):
                    dve.wait_ge(xt_used[j], HB + i + 1)
                    dve.wait_ge(bias_added[j], i + 1)
                    t = tok[:, bass.ds(4 * i + 2 * j, UT), :].rearrange("p h c -> p (h c)")
                    dve.tensor_tensor(t, t, zb[j][:], ALU.add).then_inc(conv_added[j], 1)
                for j in range(2):
                    dve.wait_ge(conv_added[j], i + 1)
                    tile_stats(3, i, j)

            for j in range(2):
                norm(2, 0, j)
            for e in range(E // 2, E):
                with dve.Fori(2 * e - E, min(2 * e - E + 2, HB - 1)) as i:
                    for j in range(2):
                        norm(2, i + 1, j)
                    add_mixed(i)
                low1(e)
            add_mixed(HB - 1)
            dve.wait_ge(v1_lo, E)
            dve.wait_ge(stats, NT * 4)
            route(1)
            experts(1)
            def final_units(i):
                for j in range(2):
                    free(dve, fin_turned[j], i)
                    combine(1, i, j, xn[:, j])

            pairs(dve, final_units)


_INS = ["x", "L0_conv_conv_w", "L0_conv_conv_b", "L0_conv_gn_w", "L0_conv_gn_b", "L0_ffn_gate_w", "L0_ffn_w1",
        "L0_ffn_w2", "L0_ffn_w3", "L1_conv_weight", "L1_conv_bias", "L1_ffn_gate_w", "L1_ffn_gate_b", "L1_ffn_w1",
        "L1_ffn_b1", "L1_ffn_w2", "L1_ffn_b2"]


def kernel(**inputs):
    import numpy as _np
    import concourse.bacc as _bacc
    from concourse import mybir as _mybir
    from concourse.bass_utils import run_bass_kernel_spmd as _run

    nc = _bacc.Bacc("TRN2", target_bir_lowering=False, num_devices=1)
    shape = inputs["x"].shape
    arrays, args = {}, []
    for name in _INS:
        a = _np.ascontiguousarray(inputs[name])
        if name == "x":
            a = a.reshape(NB, C, L)
        arrays[f"in_{name}_dram"] = a
        args.append(nc.dram_tensor(f"in_{name}_dram", a.shape, _mybir.dt.from_np(a.dtype), kind="ExternalInput").ap())
    args.append(nc.dram_tensor("out_dram", (NB, C, L), _mybir.dt.float32, kind="ExternalOutput").ap())
    bass_metaformer(nc, *args)
    r = _run(nc, [arrays], core_ids=[0])
    return r.results[0]["out_dram"].reshape(shape)
```
